# Optimizing a Trainium2 kernel written in Bass

```python
import numpy as np
import jax
import jax.numpy as jnp

def _softmax(x, axis=-1):
    return jax.nn.softmax(x, axis=axis)

def _gelu(x):
    return jax.nn.gelu(x, approximate=True)

def _silu(x):
    return jax.nn.silu(x)

def _sigmoid(x):
    return jax.nn.sigmoid(x)

def _layernorm(x, axis=-1, eps=1e-05):
    m = jnp.mean(x, axis=axis, keepdims=True)
    v = jnp.var(x, axis=axis, keepdims=True)
    return (x - m) / jnp.sqrt(v + eps)

def _scatter_add(tgt, idx, src, axis=0):
    return tgt.at[idx].add(src)

def _segment_sum(src, seg, n):
    return jax.ops.segment_sum(src, seg, n)
kernel_name = 'mk_audio_tower_d2_tok_audfeat512_r4_6c00e6'

def setup_inputs(seed: int=0):
    np.random.seed(seed)
    _w = jnp.asarray

    def _rec_inputs():
        import jax
        import jax.numpy as jnp
        _rk = jax.random.key(seed)
        x = -7.10856e-05 + 0.999911 * jax.random.normal(jax.random.fold_in(_rk, 1), (8, 750, 128), jnp.float32)
        return x
    x = _rec_inputs()

    def _L0_tok_setup():
        import jax, jax.numpy as jnp
        import numpy as np
        EPS = 1e-05

        def conv1d(x, w, b, stride=1, padding=0):
            out = jax.lax.conv_general_dilated(x, w, window_strides=(stride,), padding=[(padding, padding)], dimension_numbers=('NCH', 'OIH', 'NCH'))
            return out + b[None, :, None]

        def layer_norm(x, g, b):
            mu = jnp.mean(x, axis=-1, keepdims=True)
            var = jnp.mean(jnp.square(x - mu), axis=-1, keepdims=True)
            return (x - mu) * jax.lax.rsqrt(var + EPS) * g + b
        key = jax.random.key(seed)
        ks = jax.random.split(key, 16)
        B, T, H = (64, 512, 128)
        Bn = H // 2
        s = 0.02
        return {'x': jax.random.normal(ks[0], (B, T, H), dtype=jnp.float32), 'w_compress': jax.random.normal(ks[1], (Bn, H, 1), dtype=jnp.float32) * s, 'b_compress': jnp.zeros((Bn,), dtype=jnp.float32), 'w_main': jax.random.normal(ks[2], (Bn, Bn, 3), dtype=jnp.float32) * s, 'b_main': jnp.zeros((Bn,), dtype=jnp.float32), 'w_expand': jax.random.normal(ks[3], (H, Bn, 1), dtype=jnp.float32) * s, 'b_expand': jnp.zeros((H,), dtype=jnp.float32), 'g_conv_norm': jnp.ones((H,), dtype=jnp.float32), 'b_conv_norm': jnp.zeros((H,), dtype=jnp.float32), 'w_ff1': jax.random.normal(ks[4], (Bn, H), dtype=jnp.float32) * s, 'b_ff1': jnp.zeros((Bn,), dtype=jnp.float32), 'w_ff2': jax.random.normal(ks[5], (H, Bn), dtype=jnp.float32) * s, 'b_ff2': jnp.zeros((H,), dtype=jnp.float32), 'g_ff_norm': jnp.ones((H,), dtype=jnp.float32), 'b_ff_norm': jnp.zeros((H,), dtype=jnp.float32)}
    _L0_tok_all = _L0_tok_setup()
    _L0_tok_in = {k: v for k, v in _L0_tok_all.items() if k in ('w_compress', 'b_compress', 'w_main', 'b_main', 'w_expand', 'b_expand', 'g_conv_norm', 'b_conv_norm', 'w_ff1', 'b_ff1', 'w_ff2', 'b_ff2', 'g_ff_norm', 'b_ff_norm')}
    del _L0_tok_all

    def _L0_attn_setup():
        import math
        import jax, jax.numpy as jnp
        import numpy as np
        INPUT_DIM = 128
        HIDDEN_DIM = 128
        BATCH = 8
        SEQ_LEN = 1024

        def _xavier(key, shape):
            fan_out, fan_in = shape
            limit = math.sqrt(6.0 / (fan_in + fan_out))
            return jax.random.uniform(key, shape, jnp.float32, -limit, limit)
        key = jax.random.key(seed)
        kx, kA, kB, kC, kD, kWg = jax.random.split(key, 6)
        return {'x': jax.random.normal(kx, (BATCH, SEQ_LEN, INPUT_DIM), jnp.float32), 'A': jax.random.uniform(kA, (HIDDEN_DIM,), jnp.float32, 0.8, 0.95), 'B': _xavier(kB, (HIDDEN_DIM, INPUT_DIM)), 'C': _xavier(kC, (HIDDEN_DIM, HIDDEN_DIM)), 'D': _xavier(kD, (HIDDEN_DIM, INPUT_DIM)), 'Wg': _xavier(kWg, (HIDDEN_DIM, INPUT_DIM)), 'bias_h': jnp.zeros((HIDDEN_DIM,), jnp.float32), 'bias_y': jnp.zeros((HIDDEN_DIM,), jnp.float32)}
    _L0_attn_all = _L0_attn_setup()
    _L0_attn_in = {k: v for k, v in _L0_attn_all.items() if k in ('A', 'B', 'C', 'D', 'Wg', 'bias_h', 'bias_y')}
    del _L0_attn_all

    def _L0_ffn_setup():
        import jax, jax.numpy as jnp
        import numpy as np
        DIM = 128
        HID = 256
        E = 8
        K = 2
        B, S = (4, 512)
        key = jax.random.key(seed)
        ks = jax.random.split(key, 10)
        sd = DIM ** (-0.5)
        sh = HID ** (-0.5)
        return {'x': jax.random.normal(ks[0], (B, S, DIM), dtype=jnp.float32), 'gate_w': jax.random.normal(ks[1], (E, DIM), dtype=jnp.float32) * sd, 'biases': jnp.zeros((E,), dtype=jnp.float32), 'w1': jax.random.normal(ks[2], (E, DIM, HID), dtype=jnp.float32) * sd, 'w3': jax.random.normal(ks[3], (E, DIM, HID), dtype=jnp.float32) * sd, 'w2': jax.random.normal(ks[4], (E, HID, DIM), dtype=jnp.float32) * sh, 'sw1': jax.random.normal(ks[5], (DIM, HID), dtype=jnp.float32) * sd, 'sw3': jax.random.normal(ks[6], (DIM, HID), dtype=jnp.float32) * sd, 'sw2': jax.random.normal(ks[7], (HID, DIM), dtype=jnp.float32) * sh}
    _L0_ffn_all = _L0_ffn_setup()
    _L0_ffn_in = {k: v for k, v in _L0_ffn_all.items() if k in ('gate_w', 'biases', 'w1', 'w3', 'w2', 'sw1', 'sw3', 'sw2')}
    del _L0_ffn_all

    def _L1_attn_setup():
        import jax, jax.numpy as jnp
        import numpy as np
        B, L, E, H = (1, 512, 128, 8)
        D = E // H
        key = jax.random.key(seed)
        k0, k1, k2 = jax.random.split(key, 3)
        x = jax.random.normal(k0, (B, L, E), jnp.float32)
        W_qkv = jax.random.normal(k1, (E, 3 * E), jnp.float32) / np.sqrt(E).astype(np.float32)
        b_qkv = jnp.zeros((3 * E,), jnp.float32)
        W_out = jax.random.normal(k2, (E, E), jnp.float32) / np.sqrt(E).astype(np.float32)
        b_out = jnp.zeros((E,), jnp.float32)
        return {'x': x, 'W_qkv': W_qkv, 'b_qkv': b_qkv, 'W_out': W_out, 'b_out': b_out}
    _L1_attn_all = _L1_attn_setup()
    _L1_attn_in = {k: v for k, v in _L1_attn_all.items() if k in ('W_qkv', 'b_qkv', 'W_out', 'b_out')}
    del _L1_attn_all

    def _L1_ffn_setup():
        import jax, jax.numpy as jnp
        import numpy as np
        D_IN, D_HID, E, K = (128, 512, 10, 2)
        KS = (9, 1)

        def conv1d_same(x, w, b):
            y = jax.lax.conv_general_dilated(x, w, window_strides=(1,), padding='SAME', dimension_numbers=('NCH', 'OIH', 'NCH'))
            return y + b[None, :, None]
        key = jax.random.key(seed)
        ks = jax.random.split(key, 16)
        s = 0.02
        B, T = (2, 512)
        return {'x': jax.random.normal(ks[0], (B, T, D_IN), jnp.float32), 'rc_w1': jax.random.normal(ks[1], (D_IN, D_IN, 3), jnp.float32) * s, 'rc_b1': jnp.zeros((D_IN,), jnp.float32), 'rc_w2': jax.random.normal(ks[2], (E, D_IN, 3), jnp.float32) * s, 'rc_b2': jnp.zeros((E,), jnp.float32), 'sh_w1': jax.random.normal(ks[3], (D_HID, D_IN, KS[0]), jnp.float32) * s, 'sh_b1': jnp.zeros((D_HID,), jnp.float32), 'sh_w2': jax.random.normal(ks[4], (D_IN, D_HID, KS[1]), jnp.float32) * s, 'sh_b2': jnp.zeros((D_IN,), jnp.float32), 'e_w1': jax.random.normal(ks[5], (E, D_IN, D_HID), jnp.float32) * s, 'e_b1': jnp.zeros((E, D_HID), jnp.float32), 'e_w2': jax.random.normal(ks[6], (E, D_HID, D_IN), jnp.float32) * s, 'e_b2': jnp.zeros((E, D_IN), jnp.float32), 'ln_g': jnp.ones((D_IN,), jnp.float32), 'ln_b': jnp.zeros((D_IN,), jnp.float32)}
    _L1_ffn_all = _L1_ffn_setup()
    _L1_ffn_in = {k: v for k, v in _L1_ffn_all.items() if k in ('rc_w1', 'rc_b1', 'rc_w2', 'rc_b2', 'sh_w1', 'sh_b1', 'sh_w2', 'sh_b2', 'e_w1', 'e_b1', 'e_w2', 'e_b2', 'ln_g', 'ln_b')}
    del _L1_ffn_all
    return {'x': x, 'L0_tok_w_compress': _L0_tok_in['w_compress'], 'L0_tok_b_compress': _L0_tok_in['b_compress'], 'L0_tok_w_main': _L0_tok_in['w_main'], 'L0_tok_b_main': _L0_tok_in['b_main'], 'L0_tok_w_expand': _L0_tok_in['w_expand'], 'L0_tok_b_expand': _L0_tok_in['b_expand'], 'L0_tok_g_conv_norm': _L0_tok_in['g_conv_norm'], 'L0_tok_b_conv_norm': _L0_tok_in['b_conv_norm'], 'L0_tok_w_ff1': _L0_tok_in['w_ff1'], 'L0_tok_b_ff1': _L0_tok_in['b_ff1'], 'L0_tok_w_ff2': _L0_tok_in['w_ff2'], 'L0_tok_b_ff2': _L0_tok_in['b_ff2'], 'L0_tok_g_ff_norm': _L0_tok_in['g_ff_norm'], 'L0_tok_b_ff_norm': _L0_tok_in['b_ff_norm'], 'L0_attn_A': _L0_attn_in['A'], 'L0_attn_B': _L0_attn_in['B'], 'L0_attn_C': _L0_attn_in['C'], 'L0_attn_D': _L0_attn_in['D'], 'L0_attn_Wg': _L0_attn_in['Wg'], 'L0_attn_bias_h': _L0_attn_in['bias_h'], 'L0_attn_bias_y': _L0_attn_in['bias_y'], 'L0_ffn_gate_w': _L0_ffn_in['gate_w'], 'L0_ffn_biases': _L0_ffn_in['biases'], 'L0_ffn_w1': _L0_ffn_in['w1'], 'L0_ffn_w3': _L0_ffn_in['w3'], 'L0_ffn_w2': _L0_ffn_in['w2'], 'L0_ffn_sw1': _L0_ffn_in['sw1'], 'L0_ffn_sw3': _L0_ffn_in['sw3'], 'L0_ffn_sw2': _L0_ffn_in['sw2'], 'L1_attn_W_qkv': _L1_attn_in['W_qkv'], 'L1_attn_b_qkv': _L1_attn_in['b_qkv'], 'L1_attn_W_out': _L1_attn_in['W_out'], 'L1_attn_b_out': _L1_attn_in['b_out'], 'L1_ffn_rc_w1': _L1_ffn_in['rc_w1'], 'L1_ffn_rc_b1': _L1_ffn_in['rc_b1'], 'L1_ffn_rc_w2': _L1_ffn_in['rc_w2'], 'L1_ffn_rc_b2': _L1_ffn_in['rc_b2'], 'L1_ffn_sh_w1': _L1_ffn_in['sh_w1'], 'L1_ffn_sh_b1': _L1_ffn_in['sh_b1'], 'L1_ffn_sh_w2': _L1_ffn_in['sh_w2'], 'L1_ffn_sh_b2': _L1_ffn_in['sh_b2'], 'L1_ffn_e_w1': _L1_ffn_in['e_w1'], 'L1_ffn_e_b1': _L1_ffn_in['e_b1'], 'L1_ffn_e_w2': _L1_ffn_in['e_w2'], 'L1_ffn_e_b2': _L1_ffn_in['e_b2'], 'L1_ffn_ln_g': _L1_ffn_in['ln_g'], 'L1_ffn_ln_b': _L1_ffn_in['ln_b']}

def reference(x, L0_tok_w_compress, L0_tok_b_compress, L0_tok_w_main, L0_tok_b_main, L0_tok_w_expand, L0_tok_b_expand, L0_tok_g_conv_norm, L0_tok_b_conv_norm, L0_tok_w_ff1, L0_tok_b_ff1, L0_tok_w_ff2, L0_tok_b_ff2, L0_tok_g_ff_norm, L0_tok_b_ff_norm, L0_attn_A, L0_attn_B, L0_attn_C, L0_attn_D, L0_attn_Wg, L0_attn_bias_h, L0_attn_bias_y, L0_ffn_gate_w, L0_ffn_biases, L0_ffn_w1, L0_ffn_w3, L0_ffn_w2, L0_ffn_sw1, L0_ffn_sw3, L0_ffn_sw2, L1_attn_W_qkv, L1_attn_b_qkv, L1_attn_W_out, L1_attn_b_out, L1_ffn_rc_w1, L1_ffn_rc_b1, L1_ffn_rc_w2, L1_ffn_rc_b2, L1_ffn_sh_w1, L1_ffn_sh_b1, L1_ffn_sh_w2, L1_ffn_sh_b2, L1_ffn_e_w1, L1_ffn_e_b1, L1_ffn_e_w2, L1_ffn_e_b2, L1_ffn_ln_g, L1_ffn_ln_b):
    import jax
    import jax.numpy as jnp

    def _L0_tok_ref(x, w_compress, b_compress, w_main, b_main, w_expand, b_expand, g_conv_norm, b_conv_norm, w_ff1, b_ff1, w_ff2, b_ff2, g_ff_norm, b_ff_norm):
        import jax, jax.numpy as jnp
        import numpy as np
        EPS = 1e-05

        def conv1d(x, w, b, stride=1, padding=0):
            out = jax.lax.conv_general_dilated(x, w, window_strides=(stride,), padding=[(padding, padding)], dimension_numbers=('NCH', 'OIH', 'NCH'))
            return out + b[None, :, None]

        def layer_norm(x, g, b):
            mu = jnp.mean(x, axis=-1, keepdims=True)
            var = jnp.mean(jnp.square(x - mu), axis=-1, keepdims=True)
            return (x - mu) * jax.lax.rsqrt(var + EPS) * g + b
        xt = jnp.transpose(x, (0, 2, 1))
        identity = xt
        h = jax.nn.silu(conv1d(xt, w_compress, b_compress))
        h = jax.nn.silu(conv1d(h, w_main, b_main, stride=1, padding=1))
        h = conv1d(h, w_expand, b_expand)
        h = jnp.transpose(h, (0, 2, 1))
        identity = jnp.transpose(identity, (0, 2, 1))
        y = layer_norm(h + identity, g_conv_norm, b_conv_norm)
        ff = jnp.einsum('bth,oh->bto', y, w_ff1) + b_ff1
        ff = jax.nn.gelu(ff, approximate=False)
        ff = jnp.einsum('bto,ho->bth', ff, w_ff2) + b_ff2
        y = layer_norm(ff + y, g_ff_norm, b_ff_norm)
        yt = jnp.transpose(y, (0, 2, 1))
        pooled = jax.lax.reduce_window(yt, -jnp.inf, jax.lax.max, (1, 1, 3), (1, 1, 1), 'VALID')
        return jnp.transpose(pooled, (0, 2, 1))

    def _L0_attn_ref(x, A, B, C, D, Wg, bias_h, bias_y):
        import math
        import jax, jax.numpy as jnp
        import numpy as np
        INPUT_DIM = 128
        HIDDEN_DIM = 128
        BATCH = 8
        SEQ_LEN = 1024

        def _xavier(key, shape):
            fan_out, fan_in = shape
            limit = math.sqrt(6.0 / (fan_in + fan_out))
            return jax.random.uniform(key, shape, jnp.float32, -limit, limit)
        hidden_dim = A.shape[0]
        g = jnp.clip(jax.nn.sigmoid(jnp.einsum('bti,hi->bth', x, Wg)), 0.05, 0.95)
        xB = jnp.einsum('bti,hi->bth', x, B)
        a_coef = 1.0 - g * (1.0 - A)
        b_coef = g * (xB + bias_h)

        def step(h, ab):
            a_t, b_t = ab
            h = a_t * h + b_t
            return (h, h)
        h0 = jnp.zeros((x.shape[0], hidden_dim), x.dtype)
        _, hs = jax.lax.scan(step, h0, (jnp.swapaxes(a_coef, 0, 1), jnp.swapaxes(b_coef, 0, 1)))
        hs = jnp.swapaxes(hs, 0, 1)
        scale = 1.0 / math.sqrt(hidden_dim)
        y = (jnp.einsum('bth,oh->bto', hs, C) + jnp.einsum('bti,hi->bth', x, D) + bias_y) * scale
        return y

    def _L0_ffn_ref(x, gate_w, biases, w1, w3, w2, sw1, sw3, sw2):
        import jax, jax.numpy as jnp
        import numpy as np
        DIM = 128
        HID = 256
        E = 8
        K = 2
        B, S = (4, 512)
        Bb, Ss, D = x.shape
        xt = x.reshape(Bb * Ss, D)
        shared = jax.nn.silu(xt @ sw1) * (xt @ sw3) @ sw2
        scores = xt @ gate_w.T
        _, idx = jax.lax.top_k(scores + biases, K)
        topv, _ = jax.lax.top_k(scores, K)
        p = jax.nn.sigmoid(topv)
        p = p / jnp.sum(p, axis=-1, keepdims=True)
        h = jax.nn.silu(jnp.einsum('td,edh->eth', xt, w1)) * jnp.einsum('td,edh->eth', xt, w3)
        y = jnp.einsum('eth,ehd->etd', h, w2)
        onehot = jax.nn.one_hot(idx, E, dtype=xt.dtype)
        comb = jnp.einsum('tk,tke->te', p, onehot)
        out = jnp.einsum('te,etd->td', comb, y) + shared
        return out.reshape(Bb, Ss, D)

    def _L1_attn_ref(x, W_qkv, b_qkv, W_out, b_out):
        import jax, jax.numpy as jnp
        import numpy as np
        B, L, E, H = (1, 512, 128, 8)
        D = E // H
        num_heads = H
        eps = 1e-06
        b, l, e = x.shape
        d = e // num_heads
        qkv = x @ W_qkv + b_qkv
        q, k, v = jnp.split(qkv, 3, axis=-1)
        q = q.reshape(b, l, num_heads, d).transpose(0, 2, 1, 3)
        k = k.reshape(b, l, num_heads, d).transpose(0, 2, 1, 3)
        v = v.reshape(b, l, num_heads, d).transpose(0, 2, 1, 3)
        pos = jnp.arange(l, dtype=jnp.float32).reshape(1, 1, l, 1)
        cos_w = jnp.cos(jnp.pi / 2 * pos / l)
        sin_w = jnp.sin(jnp.pi / 2 * pos / l)
        q_prime = jax.nn.relu(q)
        k_prime = jax.nn.relu(k)

        def branch(w):
            qw = q_prime * w
            kw = k_prime * w
            kv = jnp.einsum('bhld,bhle->bhlde', kw, v)
            kv_cum = jnp.cumsum(kv, axis=2)
            ctx = jnp.einsum('bhld,bhlde->bhle', qw, kv_cum)
            nrm = jnp.einsum('bhld,bhld->bhl', qw, jnp.cumsum(kw, axis=2))
            return (ctx, nrm)
        ctx_cos, nrm_cos = branch(cos_w)
        ctx_sin, nrm_sin = branch(sin_w)
        out = (ctx_cos + ctx_sin) / ((nrm_cos + nrm_sin)[..., None] + eps)
        out = out.transpose(0, 2, 1, 3).reshape(b, l, e)
        return out @ W_out + b_out

    def _L1_ffn_ref(x, rc_w1, rc_b1, rc_w2, rc_b2, sh_w1, sh_b1, sh_w2, sh_b2, e_w1, e_b1, e_w2, e_b2, ln_g, ln_b):
        import jax, jax.numpy as jnp
        import numpy as np
        D_IN, D_HID, E, K = (128, 512, 10, 2)
        KS = (9, 1)

        def conv1d_same(x, w, b):
            y = jax.lax.conv_general_dilated(x, w, window_strides=(1,), padding='SAME', dimension_numbers=('NCH', 'OIH', 'NCH'))
            return y + b[None, :, None]
        B, T, d = x.shape
        residual = x
        xt = jnp.transpose(x, (0, 2, 1))
        rc = conv1d_same(xt, rc_w1, rc_b1)
        rc = jax.nn.gelu(rc, approximate=False)
        rc = conv1d_same(rc, rc_w2, rc_b2)
        logits = jnp.transpose(rc, (0, 2, 1)).reshape(-1, E)
        vals, idx = jax.lax.top_k(logits, K)
        gv = jax.nn.softmax(vals, axis=-1)
        N = logits.shape[0]
        gates = jnp.zeros((N, E), x.dtype).at[jnp.arange(N)[:, None], idx].set(gv)
        x2 = x.reshape(-1, d)
        h = jnp.einsum('nd,edh->enh', x2, e_w1) + e_b1[:, None, :]
        h = jax.nn.elu(h)
        eo = jnp.einsum('enh,ehd->end', h, e_w2) + e_b2[:, None, :]
        y = jnp.einsum('end,ne->nd', eo, gates).reshape(B, T, d)
        sh = conv1d_same(xt, sh_w1, sh_b1)
        sh = jax.nn.silu(sh)
        sh = conv1d_same(sh, sh_w2, sh_b2)
        sh = jnp.transpose(sh, (0, 2, 1))
        z = residual + y + sh
        mu = jnp.mean(z, axis=-1, keepdims=True)
        var = jnp.mean(jnp.square(z - mu), axis=-1, keepdims=True)
        return (z - mu) * jax.lax.rsqrt(var + 1e-05) * ln_g + ln_b
    h = _L0_tok_ref(x, L0_tok_w_compress, L0_tok_b_compress, L0_tok_w_main, L0_tok_b_main, L0_tok_w_expand, L0_tok_b_expand, L0_tok_g_conv_norm, L0_tok_b_conv_norm, L0_tok_w_ff1, L0_tok_b_ff1, L0_tok_w_ff2, L0_tok_b_ff2, L0_tok_g_ff_norm, L0_tok_b_ff_norm)
    h = h + _L0_attn_ref(_layernorm(h, axis=-1), L0_attn_A, L0_attn_B, L0_attn_C, L0_attn_D, L0_attn_Wg, L0_attn_bias_h, L0_attn_bias_y)
    h = h + _L0_ffn_ref(_layernorm(h, axis=-1), L0_ffn_gate_w, L0_ffn_biases, L0_ffn_w1, L0_ffn_w3, L0_ffn_w2, L0_ffn_sw1, L0_ffn_sw3, L0_ffn_sw2)
    h = h + _L1_attn_ref(_layernorm(h, axis=-1), L1_attn_W_qkv, L1_attn_b_qkv, L1_attn_W_out, L1_attn_b_out)
    h = h + _L1_ffn_ref(_layernorm(h, axis=-1), L1_ffn_rc_w1, L1_ffn_rc_b1, L1_ffn_rc_w2, L1_ffn_rc_b2, L1_ffn_sh_w1, L1_ffn_sh_b1, L1_ffn_sh_w2, L1_ffn_sh_b2, L1_ffn_e_w1, L1_ffn_e_b1, L1_ffn_e_w2, L1_ffn_e_b2, L1_ffn_ln_g, L1_ffn_ln_b)
    return h

_drawn_inputs = setup_inputs


def setup_inputs(seed=0):
    import zlib

    import numpy as np

    out = dict(_drawn_inputs(seed))
    spreads = {'L0_tok_b_compress': (0.0, 0.483),
     'L0_tok_b_main': (0.0, 0.1),
     'L0_tok_b_expand': (0.0, 0.1),
     'L0_tok_g_conv_norm': (1.0, 0.2),
     'L0_tok_b_conv_norm': (0.0, 0.1),
     'L0_tok_b_ff1': (0.0, 0.1),
     'L0_tok_b_ff2': (0.0, 0.1),
     'L0_tok_g_ff_norm': (1.0, 0.2),
     'L0_tok_b_ff_norm': (0.0, 0.1),
     'L0_attn_bias_h': (0.0, 0.1),
     'L0_attn_bias_y': (0.0, 0.1),
     'L0_ffn_biases': (0.0, 0.1),
     'L1_attn_b_qkv': (0.0, 0.1),
     'L1_attn_b_out': (0.0, 0.1),
     'L1_ffn_rc_b1': (0.0, 0.546),
     'L1_ffn_rc_b2': (0.0, 0.1),
     'L1_ffn_sh_b1': (0.0, 0.77),
     'L1_ffn_sh_b2': (0.0, 0.1),
     'L1_ffn_e_b1': (0.0, 0.635),
     'L1_ffn_e_b2': (0.0, 0.284),
     'L1_ffn_ln_g': (1.0, 0.2),
     'L1_ffn_ln_b': (0.0, 0.1)}
    factors = {'L0_tok_w_compress': 3.2, 'L0_tok_w_main': 3.274}
    for name, (base, spread) in spreads.items():
        noise = np.random.default_rng([zlib.crc32(name.encode()), seed]).standard_normal(out[name].shape)
        drawn = base * np.exp(spread * noise) if base else spread * noise
        out[name] = jnp.asarray(drawn.astype(out[name].dtype))
    for name, factor in factors.items():
        out[name] = (out[name] * factor).astype(out[name].dtype)
    return out
```

```python
from contextlib import ExitStack

import numpy as np
import concourse.bass as bass
from concourse import mybir

F32 = mybir.dt.float32
U32 = mybir.dt.uint32
BF16 = mybir.dt.bfloat16
I32 = mybir.dt.int32
ALU = mybir.AluOpType
ACT = mybir.ActivationFunctionType
AX = mybir.AxisListType

P = 128
B, T = 8, 750
L = T - 2
HALF_T = T // 2
TOK_ROWS = T // 6
TILES = 6
WIDTH = [min(P, L - P * j) for j in range(TILES)]
SPAN = [(0, 384), (384, L)]
NTILE = B * TILES
PAIRS = 2 * B * L
EXPERT_TILES = 104
E0, HID0 = 8, 256
E1, HID1 = 10, 512
assert (PAIRS + (E1 - 1 + 1) * (P - 1)) // P <= EXPERT_TILES
PAD = 4
NCOL = L + 2 * PAD
HEADS, DH = 8, 16
LANES = 2
ITERS = B // LANES
STRIDE0 = 2 * HID0 + (HID0 // P) * P
STRIDE1 = HID1 + (HID1 // P) * P
SLOTS = 4
EITERS = EXPERT_TILES // SLOTS
KTAPS = 9
EPS = 1e-5

PACK = {}
PACK_COLS = 0


def _place(name, rows, cols):
    global PACK_COLS
    PACK[name] = (PACK_COLS, rows, cols)
    PACK_COLS += cols


for _n, _r, _c in [
    ("compress", P, P), ("main01", P, 64), ("main2", 64, 64), ("expand", 65, P), ("ff1", P, 64), ("ff2", 65, P),
    ("b_compress", P, 1), ("b_main", 64, 1), ("b_ff1", 64, 1), ("g_conv", P, 1), ("b_conv", P, 1),
    ("g_ff", P, 1), ("b_ff", P, 1), ("A", P, 1), ("bias_h", P, 1),
    ("Wg", P, P), ("Bm", P, P), ("C", P, P), ("D", P, P), ("gate", P, E0), ("gate_bias", P, E0), ("bias_y", 1, P),
    ("q0", P, P), ("q1", P, P), ("k0", P, P), ("k1", P, P), ("b_qk", P, 4), ("v", P, P), ("b_v", 1, P),
    ("out", P, P), ("b_out", 1, P),
    ("rc1", P, 3 * P), ("b_rc1", P, 1), ("rc2", P, 3 * E1), ("b_rc2", 1, E1), ("b_sh1", P, 4), ("b_sh2", 1, P),
    ("ln_g", P, P), ("ln_b", P, P),
    ("ident", P, P), ("ones", P, P), ("earlier", P, P), ("causal", P, 2 * P), ("cos_sin", P, L), ("block", P, 136),
    ("valid", P, NTILE), ("descend", P, E1), ("tile_rows", P, 47), ("tile_id", P, EXPERT_TILES), ("minus_half", P, TILES),
]:
    _place(_n, _r, _c)

AHEAD = {"xT": 3, "load": 2, "up": 2, "silu": 2, "exp": 2, "u": 2, "uT": 1, "down": 0, "y": 0}


def turns(eng, stages, begin=None, end=None):
    def run(i, u, first=False, last=False):
        for name, f in stages:
            t = u + AHEAD[name]
            if first and t < 0 or last and t >= SLOTS:
                continue
            f(t % SLOTS, i + t // SLOTS, t)

    for u in range(-3, 0):
        run(0, u, first=True)
    with eng.Fori(0, EITERS - 1) as i:
        if begin:
            begin()
        for u in range(SLOTS):
            run(i, u)
        if end:
            end()
    if begin:
        begin()
    for u in range(SLOTS):
        run(EITERS - 1, u, last=True)




class Steps:

    CREDIT = 32

    def __init__(self, phases):
        self.phases, self.base, self.next = phases, {}, {}
        at = {}
        for phase, (iters, count, names) in phases.items():
            assert len(names) <= self.CREDIT
            for lane in range(count):
                self.base[phase, lane] = at.get(lane, self.CREDIT)
                at[lane] = self.base[phase, lane] + iters * len(names)

    def step(self, phase, step, lane):
        names = self.phases[phase][2]
        n = self.next.get((phase, lane), 0)
        assert names[n] == step, (phase, lane, step, names[n])
        self.next[phase, lane] = (n + 1) % len(names)
        return 1

    def at(self, phase, step, lane, i):
        names = self.phases[phase][2]
        return i * len(names) + (self.base[phase, lane] + names.index(step) + 1)

    def end(self, phase):
        if phase not in self.phases:
            return []
        iters, count, names = self.phases[phase]
        return [(lane, self.base[phase, lane] + iters * len(names)) for lane in range(count)]


def audio_tower(nc, d, out):
    with ExitStack() as ctx:
        def sb(name, shape, dt=F32):
            return ctx.enter_context(nc.sbuf_tensor(name, shape, dt))

        def sem(name):
            return ctx.enter_context(nc.semaphore(name))

        rows_in = [nc.dram_tensor(f"rows_in{m}", (EXPERT_TILES * P, P), F32, kind="Internal").ap() for m in range(2)]
        rows_out = [nc.dram_tensor(f"rows_out{m}", (EXPERT_TILES * P, P), F32, kind="Internal").ap() for m in range(2)]

        pack = sb("pack", [P, PACK_COLS])
        H = sb("H", [P, NTILE, P])
        N = sb("N", [P, NTILE, P])
        NT = sb("NT", [P, B, NCOL])
        S = sb("S", [P, NTILE, E1])
        gates = sb("gates", [P, 2, NTILE])
        slot_u = sb("slot_u", [P, 2, NTILE], U32)
        tile_expert = sb("tile_expert", [P, EXPERT_TILES], I32)
        zeros = sb("zeros", [P, P])
        a_minus_1 = sb("a_minus_1", [P, 1])

        def w(name, cols=None):
            at, rows, n = PACK[name]
            lo, hi = cols or (0, n)
            return pack[0:rows, at + lo:at + hi]

        ident = w("ident")

        W_COLS = 7040
        wreg = sb("wreg", [P, W_COLS])
        ew_0 = wreg[:, 0:E0 * STRIDE0]
        sw13 = wreg[:, 6144:6144 + 512]
        sw2 = wreg[:, 6656:6656 + 256]
        conv1 = wreg[:, 0:KTAPS * 512]
        conv2 = wreg[:, 4608:4608 + 512]

        LANE_COLS = 7776
        work = sb("work", [P, LANES * LANE_COLS])
        ew_1 = work[:, 0:E1 * STRIDE1]
        eb = sb("eb", [3, E1 * STRIDE1], BF16)
        eb_v = eb[:].rearrange("q (x c) -> q x c", x=E1)
        ones3 = sb("ones3", [3, P], BF16)
        EB = E1 * HID1 // P
        eb1_f = sb("eb1_f", [P, EB])
        eb1_part = sb("eb1_part", [P, 3, EB], BF16)
        eb1_dram = nc.dram_tensor("eb1_parts", (3, E1 * HID1), BF16, kind="Internal").ap()
        eb1_split = sem("eb1_split")
        eb1_stored = sem("eb1_stored")
        eb2_dram = nc.dram_tensor("eb2_parts", (3, E1 * P), BF16, kind="Internal").ap()
        eb2_split = sem("eb2_split")
        eb2_stored = sem("eb2_stored")
        eb2_in = sem("eb2_in")
        eb2 = wreg[0:1, 5120:5120 + E1 * P]
        eb2_part = wreg[0:1, 6400:6400 + E1 * P // 2].bitcast(BF16)

        def view(lane, at, n, rows=P):
            return work[0:rows, lane * LANE_COLS + at:lane * LANE_COLS + at + n]

        class Lane:
            pass

        lanes = []
        for ln in range(LANES):
            v = Lane()
            v.xT = view(ln, 0, T)
            v.h1 = view(ln, 768, T + 2)
            v.h2 = view(ln, 1536, T)
            v.norm = view(ln, 2304, 768).rearrange("p (j d) -> p j d", d=P)
            v.y1T = view(ln, 3072, T)
            v.g = view(ln, 3072, L)
            v.y2T = view(ln, 3840, T)
            v.hs = view(ln, 3840, L)
            v.tmp = view(ln, 4608, T)
            v.nT = view(ln, 4608, L)
            v.h1tok = view(ln, 5376, 768).rearrange("p (j d) -> p j d", d=P)
            v.a = view(ln, 6144, L)
            v.bc = view(ln, 6912, L)
            v.Y = [view(ln, 768 * k, 768).rearrange("p (j d) -> p j d", d=P) for k in range(2)]
            v.QK = [view(ln, a, L) for a in (0, 768, 3072, 3840)]
            v.oT = view(ln, 4608, L)
            v.V = view(ln, 5376, 816).rearrange("p (j h e) -> p j h e", h=HEADS, e=DH + 1)
            v.AT = view(ln, 6192, 1024).rearrange("p (r g i) -> p r g i", r=4, g=2)
            v.ktok = view(ln, 7216, 256)
            v.state = view(ln, 7472, 136)
            v.rden = view(ln, 7608, 8)
            v.rcT = view(ln, 3072, L + 2)
            v.sT = [view(ln, 3072 + 768 * m, L) for m in range(4)]
            v.st = sb(f"stats{ln}", [P, TILES, 6])
            v.mv = sb(f"mean_var{ln}", [P, TILES, 2])
            v.ve = sb(f"var_eps{ln}", [P, TILES])
            v.rstd = sb(f"rstd{ln}", [P, TILES])
            v.upd = sb(f"upd{ln}", [P, 136])
            lanes.append(v)

        slots = []
        for u in range(SLOTS):
            v = Lane()
            at = 10240 + u * 1300
            v.x = work[:, at:at + P]
            v.xT = work[:, at + 128:at + 256]
            v.e = work[:, at + 256:at + 768]
            v.uT = work[:, at + 768:at + 1280]
            v.y = sb(f"expert_y{u}", [P, P])[:]
            slots.append(v)
        assert 10240 + SLOTS * 1300 <= LANES * LANE_COLS

        def route_buf(n, ne):
            return work[:, 10240 + 480 * n:10240 + 480 * n + NTILE * ne].rearrange("p (t e) -> p t e", e=ne)

        def route_small(at, n):
            return work[:, 14560 + at:14560 + at + n]

        top_vals = route_small(48, 2 * NTILE)
        for v in lanes:
            v.gk = sb(f"gate_b{lanes.index(v)}", [P, 2, TILES])
            v.ix = sb(f"slot_b{lanes.index(v)}", [P, 2, TILES], U32)
        minus_one = sb("minus_one", [P, 1])

        psum = ctx.enter_context(nc.psum_tensor("psum", [P, 8, 512], F32))
        for ln, v in enumerate(lanes):
            v.P = psum[:, 4 * ln:4 * ln + 2, :]
            v.TK = psum[:, 4 * ln + 2:4 * ln + 4, :].rearrange("p b (j d) -> p (b j) d", d=P)
            v.TKf = psum[:, 4 * ln + 2:4 * ln + 4, :]
            v.bank = [psum[:, 4 * ln + r, :] for r in range(4)]
        for u, v in enumerate(slots):
            v.ps1 = psum[:, 2 * u, :]
            v.psx = psum[:, 2 * u, 0:P]
            v.psy = psum[:, 2 * u + 1, 0:P]

        def chunk_steps(names):
            return [f"{n}{c}" for c in range(TILES) for n in names]

        pe_done = [sem(f"pe_done{k}") for k in range(4)]
        pe = Steps({
            "mixer": (ITERS, LANES, ["compress", "main", "r1", "norm1T", "ff1", "r2", "norm2T", "h1tok", "norm3T",
                              "Wg", "xB", "y", "norm4T", "scores"]),
            "route0": (1, 1, ["counts"]),
            "shared0": (ITERS, LANES, ["up0_0", "up0_1", "up1_0", "up1_1", "down"]),
            "experts0": (EITERS, SLOTS, ["xT", "up", "uT", "down"]),
            "attention": (ITERS, LANES, ["norm5T", "q0", "q1", "k0", "k1", "v"]
                          + chunk_steps(["sc", "cx"]) + ["oT", "out", "norm6T", "rc1", "scores"]),
            "route1": (1, 1, ["counts", "colsum"]),
            "experts1": (EITERS, SLOTS, ["xT", "up", "uT", "down"]),
            "output": (ITERS, LANES, ["c0", "c1", "c2", "c3", "down"]),
        })
        act_done = [sem(f"act_done{k}") for k in range(4)]
        act = Steps({
            "mixer": (ITERS, LANES, ["h1", "h2", "y1T", "ff", "y2T", "h1tok", "n1T", "g", "n4T"]),
            "route0": (1, 1, ["sigmoid"]),
            "shared0": (ITERS, LANES, ["s0_0", "s0_1", "s1_0", "s1_1"]),
            "experts0": (EITERS, SLOTS, ["silu", "uT"]),
            "attention": (ITERS, LANES, ["n5T", "q0", "q1", "k0", "k1", "v"] + chunk_steps(["kt"])
                          + ["oT", "n6T", "rc1"]),
            "route1": (1, 1, ["exp"]),
            "experts1": (EITERS, SLOTS, ["exp", "uT"]),
            "output": (ITERS, LANES, ["s0", "s1", "s2", "s3"]),
        })
        dve_done = [sem(f"dve_done{k}") for k in range(4)]
        dve = Steps({
            "mixer": (ITERS, LANES, ["var1", "norm1", "var2", "norm2", "pool", "var3", "norm3", "gates", "b", "scan",
                              "h2", "var4", "norm4", "scores"]),
            "route0": (1, 1, ["onehot", "values", "done"]),
            "shared0": (ITERS, LANES, ["u0_0", "u0_1", "u1_0", "u1_1", "h"]),
            "experts0": (EITERS, SLOTS, ["xT", "u", "y"]),
            "attention": (ITERS, LANES, ["h3", "var5", "norm5", "q0", "q1", "k0", "k1"]
                          + chunk_steps(["at", "st"]) + ["otok", "h4", "var6", "norm6", "scores"]),
            "route1": (1, 1, ["onehot", "values", "done", "bias"]),
            "experts1": (EITERS, SLOTS, ["xT", "u", "y"]),
            "output": (ITERS, LANES, ["z", "var7", "norm7", "h5"]),
        })
        pool_done = [sem(f"pool_done{k}") for k in range(2)]
        pool = Steps({
            "mixer": (ITERS, LANES, ["rstd1", "rstd2", "rstd3", "rstd4"]),
            "attention": (ITERS, LANES, ["rstd5", "rstd6"]),
            "output": (ITERS, LANES, ["rstd7"]),
        })

        def barrier(eng, phase):
            for lane, value in pe.end(phase):
                eng.wait_ge(pe_done[lane], value)
            for lane, value in act.end(phase):
                eng.wait_ge(act_done[lane], value)
            for lane, value in dve.end(phase):
                eng.wait_ge(dve_done[lane], value)
            for lane, value in pool.end(phase):
                eng.wait_ge(pool_done[lane], value)

        inputs_in = sem("inputs_in")
        shared_in = sem("shared_weights_in")
        zero_set = sem("zeros_set")
        rows_zeroed = sem("rows_zeroed")
        x_in = [sem(f"x_in{k}") for k in range(LANES)]
        scattered = [sem(f"rows_scattered{m}") for m in range(2)]
        row_in = [sem(f"expert_row_in{u}") for u in range(SLOTS)]
        row_stored = [sem(f"expert_row_stored{u}") for u in range(SLOTS)]
        gathered = [sem(f"rows_gathered{k}") for k in range(LANES)]
        experts1_in = sem("experts1_in")
        conv_in = sem("conv_in")
        out_stored = [sem(f"out_stored{k}") for k in range(LANES)]
        SCATTERS = 2 * NTILE
        GATHERS = 2 * TILES

        block = ctx.enter_context(nc.Block())
        HP = [(0, 5, P), (5, 6, WIDTH[5])]

        def batch_tiles(b):
            return bass.ds(b * TILES, TILES)

        @block.sync
        def _(sp):
            sp.dma_start(pack[:], d["pack"]).then_inc(inputs_in, 16)
            sp.dma_start(eb1_f[:], d["eb1"]).then_inc(inputs_in, 16)
            for name, dst in (("ew_0", ew_0), ("sw13", sw13), ("sw2", sw2)):
                sp.dma_start(dst, d[name]).then_inc(shared_in, 16)
            sp.wait_ge(eb1_split, 1)
            for q in range(3):
                sp.dma_start(eb1_dram[q].rearrange("(p c) -> p c", p=P), eb1_part[:, q, :]).then_inc(eb1_stored, 16)
            sp.wait_ge(eb1_stored, 48)
            sp.dma_start(eb_v[:, :, 0:HID1], eb1_dram.rearrange("q (x c) -> q x c", x=E1)).then_inc(shared_in, 16)
            sp.wait_ge(zero_set, 1)
            for m in range(2):
                sp.dma_start(rows_in[m].rearrange("(p r) d -> p r d", p=P),
                             zeros[:].unsqueeze(1).broadcast_to([P, EXPERT_TILES, P])).then_inc(rows_zeroed, 16)
            with sp.Fori(0, ITERS) as i:
                for k in range(LANES):
                    sp.wait_ge(pe_done[k], pe.at("mixer", "r1", k, i - 1))
                    sp.dma_start(lanes[k].xT, d["xT"][bass.ds(i * LANES + k, 1)].rearrange("a p t -> p (a t)")
                                 ).then_inc(x_in[k], 16)

            def expert_tiles(m, phase):
                sp.wait_ge(scattered[m], 16 * SCATTERS)
                sp.wait_ge(dve_done[0], dve.at(("route0", "route1")[m], "done", 0, 0))
                with sp.Fori(0, EITERS) as i:
                    for u in range(SLOTS):
                        sp.wait_ge(pe_done[u], pe.at(phase, "xT", u, i - 1))
                        sp.dma_start(slots[u].x, rows_in[m].rearrange("(t p) d -> t p d", p=P)[
                            bass.ds(i * SLOTS + u, 1)].rearrange("a p d -> p (a d)")).then_inc(row_in[u], 16)

            barrier(sp, "shared0")
            expert_tiles(0, "experts0")
            barrier(sp, "experts0")
            for name, dst in (("conv1", conv1), ("conv2", conv2)):
                sp.dma_start(dst, d[name]).then_inc(conv_in, 16)
            barrier(sp, "attention")
            for name, dst in (("ew_1", ew_1), ("eb2", eb2)):
                sp.dma_start(dst, d[name]).then_inc(experts1_in, 16)
            for q in range(3):
                sp.wait_ge(eb2_split, q + 1)
                sp.dma_start(eb2_dram[q:q + 1], eb2_part).then_inc(eb2_stored, 16)
            sp.wait_ge(eb2_stored, 48)
            sp.dma_start(eb_v[:, :, HID1:HID1 + P], eb2_dram.rearrange("q (x c) -> q x c", x=E1)).then_inc(eb2_in, 16)
            expert_tiles(1, "experts1")
            with sp.Fori(0, ITERS) as i:
                for k in range(LANES):
                    sp.wait_ge(dve_done[k], dve.at("output", "h5", k, i))
                    b = i * LANES + k
                    ob = out[bass.ds(b, 1)].rearrange("a t d -> (a t) d")
                    hb = H[:, batch_tiles(b), :]
                    sp.dma_start(ob[0:5 * P].rearrange("(j p) d -> p j d", p=P), hb[:, 0:5, :]
                                 ).then_inc(out_stored[k], 16)
                    sp.dma_start(ob[5 * P:L], hb[0:WIDTH[5], 5, :]).then_inc(out_stored[k], 16)
            for k in range(LANES):
                sp.wait_ge(out_stored[k], 32 * ITERS)

        @block.tensor
        def _(e):
            mm = nc.tensor.matmul
            for done in pe_done:
                e.sem_inc(done, Steps.CREDIT)
            e.wait_ge(inputs_in, 32)

            def transposes(v, src, widths):
                for j in range(TILES):
                    c0 = sum(widths[:j % 3]) if j < 3 else sum(widths[3:j])
                    r = nc.tensor.transpose(v.P[:, j // 3, c0:c0 + widths[j]], src(j), ident[0:widths[j], 0:widths[j]])
                return r

            TOKW = [TOK_ROWS] * TILES

            def mixer_compress(k, i):
                v = lanes[k]
                e.wait_ge(x_in[k], i * 16 + 16)
                e.wait_ge(act_done[k], act.at("mixer", "n4T", k, i - 1))
                for h in range(2):
                    r = mm(v.P[:, h, 0:HALF_T], w("compress"), v.xT[:, h * HALF_T:(h + 1) * HALF_T], start=True, stop=True)
                r.then_inc(pe_done[k], pe.step("mixer", "compress", k))

            def mixer_main(k, i):
                v = lanes[k]
                e.wait_ge(act_done[k], act.at("mixer", "h1", k, i))
                for h in range(2):
                    c = h * HALF_T
                    mm(v.P[0:64, h, 0:HALF_T], w("main01"), v.h1[:, c:c + HALF_T], start=True, stop=False)
                    r = mm(v.P[0:64, h, 0:HALF_T], w("main2"), v.h1[0:64, c + 2:c + 2 + HALF_T], start=False, stop=True)
                r.then_inc(pe_done[k], pe.step("mixer", "main", k))

            def mixer_r1(k, i):
                v = lanes[k]
                e.wait_ge(act_done[k], act.at("mixer", "h2", k, i))
                e.wait_ge(dve_done[k], dve.at("mixer", "scores", k, i - 1))
                for j in range(TILES):
                    c = slice(j * TOK_ROWS, (j + 1) * TOK_ROWS)
                    mm(v.TK[0:TOK_ROWS, j, :], v.h2[0:65, c], w("expand"), start=True, stop=False)
                    r = mm(v.TK[0:TOK_ROWS, j, :], v.xT[:, c], ident, start=False, stop=True)
                r.then_inc(pe_done[k], pe.step("mixer", "r1", k))

            def norm_T(step, norm_step, widths, phase="mixer"):
                def f(k, i):
                    v = lanes[k]
                    e.wait_ge(dve_done[k], dve.at(phase, norm_step, k, i))
                    r = transposes(v, lambda j: v.norm[0:widths[j], j, :], widths)
                    r.then_inc(pe_done[k], pe.step(phase, step, k))
                return f

            def mixer_ff1(k, i):
                v = lanes[k]
                e.wait_ge(act_done[k], act.at("mixer", "y1T", k, i))
                for h in range(2):
                    r = mm(v.P[0:64, h, 0:HALF_T], w("ff1"), v.y1T[:, h * HALF_T:(h + 1) * HALF_T], start=True, stop=True)
                r.then_inc(pe_done[k], pe.step("mixer", "ff1", k))

            def mixer_r2(k, i):
                v = lanes[k]
                e.wait_ge(act_done[k], act.at("mixer", "ff", k, i))
                for j in range(TILES):
                    c = slice(j * TOK_ROWS, (j + 1) * TOK_ROWS)
                    mm(v.TK[0:TOK_ROWS, j, :], v.h2[0:65, c], w("ff2"), start=True, stop=False)
                    r = mm(v.TK[0:TOK_ROWS, j, :], v.y1T[:, c], ident, start=False, stop=True)
                r.then_inc(pe_done[k], pe.step("mixer", "r2", k))

            def mixer_h1tok(k, i):
                v = lanes[k]
                e.wait_ge(dve_done[k], dve.at("mixer", "pool", k, i))
                for j in range(TILES):
                    r = nc.tensor.transpose(v.TK[0:WIDTH[j], j, :], v.y2T[:, j * P:j * P + WIDTH[j]], ident)
                r.then_inc(pe_done[k], pe.step("mixer", "h1tok", k))

            def mixer_Wg(k, i):
                v = lanes[k]
                e.wait_ge(act_done[k], act.at("mixer", "n1T", k, i))
                for h, (c0, c1) in enumerate(SPAN):
                    r = mm(v.P[:, h, 0:c1 - c0], w("Wg"), v.nT[:, c0:c1], start=True, stop=True)
                r.then_inc(pe_done[k], pe.step("mixer", "Wg", k))

            def mixer_xB(k, i):
                v = lanes[k]
                for h, (c0, c1) in enumerate(SPAN):
                    r = mm(v.TKf[:, h, 0:c1 - c0], w("Bm"), v.nT[:, c0:c1], start=True, stop=True)
                r.then_inc(pe_done[k], pe.step("mixer", "xB", k))

            def mixer_y(k, i):
                v = lanes[k]
                e.wait_ge(dve_done[k], dve.at("mixer", "scan", k, i))
                for j in range(TILES):
                    n = WIDTH[j]
                    c = slice(j * P, j * P + n)
                    mm(v.TK[0:n, j, :], v.hs[:, c], w("C"), start=True, stop=False)
                    mm(v.TK[0:n, j, :], v.nT[:, c], w("D"), start=False, stop=False)
                    r = mm(v.TK[0:n, j, :], w("ones")[0:1, 0:n], w("bias_y"), start=False, stop=True)
                r.then_inc(pe_done[k], pe.step("mixer", "y", k))

            def mixer_scores(k, i):
                v = lanes[k]
                e.wait_ge(act_done[k], act.at("mixer", "n4T", k, i))
                for j in range(TILES):
                    r = mm(v.TK[0:WIDTH[j], j, 0:E0], v.nT[:, j * P:j * P + WIDTH[j]], w("gate"), start=True, stop=True)
                r.then_inc(pe_done[k], pe.step("mixer", "scores", k))

            with e.Fori(0, ITERS) as i:
                for f in (mixer_compress, mixer_main, mixer_r1, norm_T("norm1T", "norm1", TOKW), mixer_ff1, mixer_r2,
                          norm_T("norm2T", "norm2", TOKW), mixer_h1tok, norm_T("norm3T", "norm3", WIDTH),
                          mixer_Wg, mixer_xB, mixer_y,
                          norm_T("norm4T", "norm4", WIDTH),
                          mixer_scores):
                    for k in range(LANES):
                        f(k, i)

            def route(phase, ne):
                e.wait_ge(dve_done[0], dve.at(phase, "onehot", 0, 0))
                both = route_buf(4, ne).rearrange("p t e -> p (t e)")
                mm(psum[:, 0, 0:NTILE * ne], w("earlier"), both, start=True, stop=True)
                r = mm(psum[:, 1, 0:NTILE * ne], w("ones"), both, start=True, stop=True)
                r.then_inc(pe_done[0], pe.step(phase, "counts", 0))

            def expert_tiles(m, phase):
                hid = (HID0, HID1)[m]
                nh = hid // P
                weights = (wreg, work)[m]

                stride = (STRIDE0, STRIDE1)[m]
                regs = [e.alloc_register(f"{phase}_expert{t}") for t in range(SLOTS + 2)]
                which = {}

                def load(u, i, t):
                    e.reg_load(regs[t], tile_expert[0:1, bass.ds(i * SLOTS + u, 1)])
                    which[t] = e.snap(regs[t], min_val=0, max_val=stride * ((E0, E1)[m] - 1))

                def begin():
                    for t in range(2):
                        which[t] = e.snap(regs[t], min_val=0, max_val=stride * ((E0, E1)[m] - 1))

                def end():
                    for t in range(2):
                        e.reg_mov(regs[t], regs[SLOTS + t])

                def xT(u, i, t):
                    v = slots[u]
                    e.wait_ge(row_in[u], i * 16 + (16 + m * 16 * EITERS))
                    nc.tensor.transpose(v.psx, v.x, ident).then_inc(pe_done[u], pe.step(phase, "xT", u))

                def up(u, i, t):
                    v = slots[u]
                    e.wait_ge(dve_done[u], dve.at(phase, "xT", u, i))
                    if m == 0:
                        r = mm(v.ps1, v.xT, wreg[:, bass.ds(which[t], 512)], start=True, stop=True)
                    else:
                        mm(v.ps1, v.xT, work[:, bass.ds(which[t], 512)], start=True, stop=False)
                        r = mm(v.ps1, ones3[:], eb[:, bass.ds(which[t], 512)], start=False, stop=True)
                    r.then_inc(pe_done[u], pe.step(phase, "up", u))

                def uT(u, i, t):
                    v = slots[u]
                    e.wait_ge(dve_done[u], dve.at(phase, "u", u, i))
                    for c in range(nh):
                        r = nc.tensor.transpose(v.ps1[:, c * P:(c + 1) * P], v.e[:, c * P:(c + 1) * P], ident)
                    r.then_inc(pe_done[u], pe.step(phase, "uT", u))

                def down(u, i, t):
                    v = slots[u]
                    e.wait_ge(act_done[u], act.at(phase, "uT", u, i))
                    for c in range(nh):
                        r = mm(v.psy, v.uT[:, c * P:(c + 1) * P],
                               weights[:, bass.ds(which[t] + (512 + c * P), P)], start=(c == 0), stop=(m == 0 and c == nh - 1))
                    if m == 1:
                        r = mm(v.psy, ones3[:], eb[:, bass.ds(which[t] + HID1, P)], start=False, stop=True)
                    r.then_inc(pe_done[u], pe.step(phase, "down", u))

                turns(e, [("xT", xT), ("load", load), ("up", up), ("uT", uT), ("down", down)], begin, end)

            route("route0", E0)
            e.wait_ge(dve_done[0], dve.at("route0", "done", 0, 0))

            e.wait_ge(shared_in, 64)

            def shared_up(m, h):
                def f(k, i):
                    v = lanes[k]
                    nt = NT[:, bass.ds(i * LANES + k, 1), :]
                    c0, c1 = SPAN[h]
                    n = c1 - c0
                    if (m, h) == (0, 0):
                        e.wait_ge(dve_done[k], dve.at("shared0", "u1_1", k, i - 1))
                    elif h == 0:
                        e.wait_ge(dve_done[k], dve.at("shared0", "u0_1", k, i))
                    else:
                        e.wait_ge(dve_done[k], dve.at("shared0", f"u{m}_0", k, i))
                    mm(v.P[:, 0, 0:n], sw13[:, m * P:(m + 1) * P], nt[:, 0, PAD + c0:PAD + c1], start=True, stop=True)
                    r = mm(v.P[:, 1, 0:n], sw13[:, 256 + m * P:256 + (m + 1) * P], nt[:, 0, PAD + c0:PAD + c1], start=True, stop=True)
                    r.then_inc(pe_done[k], pe.step("shared0", f"up{m}_{h}", k))
                return f

            def shared_down(k, i):
                v = lanes[k]
                e.wait_ge(dve_done[k], dve.at("shared0", "u1_1", k, i))
                e.wait_ge(dve_done[k], dve.at("shared0", "h", k, i - 1))
                for j in range(TILES):
                    n = WIDTH[j]
                    for m in range(2):
                        r = mm(v.TK[0:n, j, :], v.QK[m][:, j * P:j * P + n], sw2[:, m * P:(m + 1) * P],
                               start=(m == 0), stop=(m == 1))
                r.then_inc(pe_done[k], pe.step("shared0", "down", k))

            with e.Fori(0, ITERS) as i:
                for m in range(2):
                    for h in range(2):
                        for k in range(LANES):
                            shared_up(m, h)(k, i)
                for k in range(LANES):
                    shared_down(k, i)
            barrier(e, "shared0")
            expert_tiles(0, "experts0")

            def qk(n):
                def f(k, i):
                    v = lanes[k]
                    name = ("q0", "q1", "k0", "k1")[n]
                    if n == 0:
                        e.wait_ge(act_done[k], act.at("attention", "n5T", k, i))
                    else:
                        e.wait_ge(act_done[k], act.at("attention", ("q0", "q1", "k0")[n - 1], k, i))
                    for h, (c0, c1) in enumerate(SPAN):
                        r = mm(v.P[:, h, 0:c1 - c0], w(name), v.nT[:, c0:c1], start=True, stop=True)
                    r.then_inc(pe_done[k], pe.step("attention", name, k))
                return f

            def vproj(k, i):
                v = lanes[k]
                e.wait_ge(dve_done[k], dve.at("attention", "scores", k, i - 1))
                for j in range(TILES):
                    n = WIDTH[j]
                    mm(v.TK[0:n, j, :], v.nT[:, j * P:j * P + n], w("v"), start=True, stop=False)
                    r = mm(v.TK[0:n, j, :], w("ones")[0:1, 0:n], w("b_v"), start=False, stop=True)
                r.then_inc(pe_done[k], pe.step("attention", "v", k))

            def chunk_scores(c):
                def f(k, i):
                    v = lanes[k]
                    n = WIDTH[c]
                    col = slice(c * P, c * P + n)
                    if c == 0:
                        e.wait_ge(dve_done[k], dve.at("attention", "k1", k, i))
                        e.wait_ge(act_done[k], act.at("attention", "v", k, i))
                    else:
                        e.wait_ge(dve_done[k], dve.at("attention", f"st{c - 1}", k, i))
                        e.wait_ge(act_done[k], act.at("attention", f"kt{c - 1}", k, i))
                    for g in range(2):
                        for r4 in range(4):
                            rows = slice(32 * r4, 32 * r4 + 32)
                            mm(v.bank[r4][0:n, g * P:g * P + n], v.QK[2 + g][rows, col], v.QK[g][rows, col],
                               start=True, stop=True)
                    for g in range(2):
                        r = nc.tensor.transpose(v.bank[1][0:n, 256 + g * P:256 + (g + 1) * P], v.QK[2 + g][:, col], ident)
                    r.then_inc(pe_done[k], pe.step("attention", f"sc{c}", k))
                return f

            def chunk_context(c):
                def f(k, i):
                    v = lanes[k]
                    n = WIDTH[c]
                    col = slice(c * P, c * P + n)
                    e.wait_ge(dve_done[k], dve.at("attention", f"at{c}", k, i))
                    e.wait_ge(act_done[k], act.at("attention", f"kt{c}", k, i))
                    ctxp = v.bank[3]
                    for g in range(2):
                        mm(ctxp[0:n, 256 + g * 68:256 + (g + 1) * 68], v.QK[g][:, col], v.state[:, g * 68:(g + 1) * 68],
                           start=(g == 0), stop=False, skip_group_check=True)
                    for h in range(HEADS):
                        r = mm(ctxp[0:n, 256 + h * 17:256 + (h + 1) * 17], v.AT[0:n, h % 4, h // 4, 0:n], v.V[0:n, c, h, :],
                               start=False, stop=(h == HEADS - 1), skip_group_check=True)
                    if c < TILES - 1:
                        for g in range(2):
                            r = mm(v.bank[0][:, 256 + g * 68:256 + (g + 1) * 68], v.ktok[0:n, g * P:(g + 1) * P],
                                   v.V[0:n, c, 4 * g:4 * g + 4, :].rearrange("p h e -> p (h e)"), start=True, stop=True)
                    r.then_inc(pe_done[k], pe.step("attention", f"cx{c}", k))
                return f

            def o_T(k, i):
                v = lanes[k]
                e.wait_ge(dve_done[k], dve.at("attention", "otok", k, i))
                r = transposes(v, lambda j: v.norm[0:WIDTH[j], j, :], WIDTH)
                r.then_inc(pe_done[k], pe.step("attention", "oT", k))

            def attn_out(k, i):
                v = lanes[k]
                e.wait_ge(act_done[k], act.at("attention", "oT", k, i))
                for j in range(TILES):
                    n = WIDTH[j]
                    mm(v.TK[0:n, j, :], v.oT[:, j * P:j * P + n], w("out"), start=True, stop=False)
                    r = mm(v.TK[0:n, j, :], w("ones")[0:1, 0:n], w("b_out"), start=False, stop=True)
                r.then_inc(pe_done[k], pe.step("attention", "out", k))

            def rc1(k, i):
                v = lanes[k]
                e.wait_ge(act_done[k], act.at("attention", "n6T", k, i))
                nt = NT[:, bass.ds(i * LANES + k, 1), :]
                for h, (c0, c1) in enumerate(SPAN):
                    for t in range(3):
                        r = mm(v.P[:, h, 0:c1 - c0], w("rc1", (t * P, t * P + P)),
                               nt[:, 0, PAD - 1 + t + c0:PAD - 1 + t + c1], start=(t == 0), stop=(t == 2))
                r.then_inc(pe_done[k], pe.step("attention", "rc1", k))

            def rc2(k, i):
                v = lanes[k]
                e.wait_ge(act_done[k], act.at("attention", "rc1", k, i))
                for j in range(TILES):
                    n = WIDTH[j]
                    for t in range(3):
                        mm(v.TK[0:n, j, 0:E1], v.rcT[:, j * P + t:j * P + t + n], w("rc2", (t * E1, t * E1 + E1)),
                           start=(t == 0), stop=False)
                    r = mm(v.TK[0:n, j, 0:E1], w("ones")[0:1, 0:n], w("b_rc2"), start=False, stop=True)
                r.then_inc(pe_done[k], pe.step("attention", "scores", k))

            barrier(e, "experts0")
            with e.Fori(0, ITERS) as i:
                steps = [norm_T("norm5T", "norm5", WIDTH, phase="attention"), qk(0), qk(1), qk(2), qk(3), vproj]
                for c in range(TILES):
                    steps += [chunk_scores(c), chunk_context(c)]
                steps += [o_T, attn_out,
                          norm_T("norm6T", "norm6", WIDTH, phase="attention"),
                          rc1, rc2]
                for f in steps:
                    for k in range(LANES):
                        f(k, i)

            route("route1", E1)
            e.wait_ge(experts1_in, 32)
            ew2_v = ew_1.rearrange("p (x c d) -> p x c d", x=E1, c=8)[:, :, 4:8, :]
            for q, (x0, x1) in enumerate(((0, 4), (4, 8), (8, E1))):
                for c in range(4):
                    r = mm(psum[0:1, 2 + q, 0:(x1 - x0) * P], w("ones")[:, 0:1], ew2_v[:, x0:x1, c, :],
                           start=(c == 0), stop=(c == 3))
            r.then_inc(pe_done[0], pe.step("route1", "colsum", 0))
            barrier(e, "route1")
            e.wait_ge(eb2_in, 16)
            expert_tiles(1, "experts1")
            barrier(e, "experts1")

            e.wait_ge(conv_in, 32)

            def conv(m):
                def f(k, i):
                    v = lanes[k]
                    nt = NT[:, bass.ds(i * LANES + k, 1), :]
                    if m == 0:
                        e.wait_ge(act_done[k], act.at("output", "s3", k, i - 1))
                    else:
                        e.wait_ge(act_done[k], act.at("output", f"s{m - 1}", k, i))
                    for t in range(KTAPS):
                        for h, (c0, c1) in enumerate(SPAN):
                            r = mm(v.P[:, h, 0:c1 - c0], conv1[:, t * 512 + m * P:t * 512 + (m + 1) * P],
                                   nt[:, 0, t + c0:t + c1], start=(t == 0), stop=(t == KTAPS - 1))
                    r.then_inc(pe_done[k], pe.step("output", f"c{m}", k))
                return f

            def conv_down(k, i):
                v = lanes[k]
                e.wait_ge(act_done[k], act.at("output", "s3", k, i))
                e.wait_ge(dve_done[k], dve.at("output", "z", k, i - 1))
                for j in range(TILES):
                    n = WIDTH[j]
                    for m in range(4):
                        mm(v.TK[0:n, j, :], v.sT[m][:, j * P:j * P + n], conv2[:, m * P:(m + 1) * P], start=(m == 0), stop=False)
                    r = mm(v.TK[0:n, j, :], w("ones")[0:1, 0:n], w("b_sh2"), start=False, stop=True)
                r.then_inc(pe_done[k], pe.step("output", "down", k))

            with e.Fori(0, ITERS) as i:
                for f in (conv(0), conv(1), conv(2), conv(3), conv_down):
                    for k in range(LANES):
                        f(k, i)

        @block.scalar
        def _(e):
            A = nc.scalar.activation
            for done in act_done:
                e.sem_inc(done, Steps.CREDIT)
            e.wait_ge(inputs_in, 32)
            e.wait_ge(zero_set, 1)

            def spans(f, n0=None):
                for h, (c0, c1) in enumerate(SPAN):
                    r = f(h, c0, c1)
                return r

            def evac(step, src, dst, after=()):
                def f(k, i):
                    v = lanes[k]
                    e.wait_ge(pe_done[k], pe.at("mixer", src, k, i))
                    dst(v, i, k).then_inc(act_done[k], act.step("mixer", step, k))
                return f

            def h1(v, i, k):
                A(v.h1[0:64, 1:T + 1].rearrange("p (h c) -> p h c", h=2), v.P[0:64, :, 0:HALF_T], ACT.Silu, bias=w("b_compress")[0:64])
                return A(v.h1[64:128, 0:T].rearrange("p (h c) -> p h c", h=2), v.P[64:128, :, 0:HALF_T], ACT.Silu, bias=w("b_compress")[64:128])

            def h2(v, i, k):
                return A(v.h2[0:64, :].rearrange("p (h c) -> p h c", h=2), v.P[0:64, :, 0:HALF_T], ACT.Silu, bias=w("b_main"))

            def y1T(v, i, k):
                return A(v.y1T.rearrange("p (h c) -> p h c", h=2), v.P[:, :, 0:HALF_T], ACT.Identity, bias=w("b_conv"), scale=w("g_conv"))

            def ff(v, i, k):
                return A(v.h2[0:64, :].rearrange("p (h c) -> p h c", h=2), v.P[0:64, :, 0:HALF_T], ACT.Gelu, bias=w("b_ff1"))

            def y2T(v, i, k):
                return A(v.y2T.rearrange("p (h c) -> p h c", h=2), v.P[:, :, 0:HALF_T], ACT.Identity, bias=w("b_ff"), scale=w("g_ff"))

            def h1tok(v, i, k):
                for a, b, n in HP:
                    r = nc.scalar.copy(v.h1tok[0:n, a:b, :], v.TK[0:n, a:b, :])
                return r

            def to_nT(v, i, k):
                return spans(lambda h, c0, c1: nc.scalar.copy(v.nT[:, c0:c1], v.P[:, h, 0:c1 - c0]))

            def g(v, i, k):
                return spans(lambda h, c0, c1: A(v.g[:, c0:c1], v.P[:, h, 0:c1 - c0], ACT.Sigmoid))

            def to_NT(v, i, k):
                nt = NT[:, bass.ds(i * LANES + k, 1), :]
                return spans(lambda h, c0, c1: nc.scalar.copy(nt[:, 0, PAD + c0:PAD + c1], v.P[:, h, 0:c1 - c0]))

            def n4T(v, i, k):
                nb = N[:, batch_tiles(i * LANES + k), :]
                for a, b, n in HP:
                    nc.scalar.copy(nb[0:n, a:b, :], v.norm[0:n, a:b, :])
                to_NT(v, i, k)
                return to_nT(v, i, k)

            with e.Fori(0, ITERS) as i:
                for step, src, f in (("h1", "compress", h1), ("h2", "main", h2), ("y1T", "norm1T", y1T), ("ff", "ff1", ff),
                                     ("y2T", "norm2T", y2T), ("h1tok", "h1tok", h1tok), ("n1T", "norm3T", to_nT),
                                     ("g", "Wg", g), ("n4T", "norm4T", n4T)):
                    for k in range(LANES):
                        if step == "h1tok":
                            e.wait_ge(dve_done[k], dve.at("mixer", "norm3", k, i))
                        if step == "n1T":
                            e.wait_ge(dve_done[k], dve.at("mixer", "pool", k, i))
                        evac(step, src, f)(k, i)

            e.wait_ge(dve_done[0], dve.at("route0", "values", 0, 0))
            A(top_vals, top_vals, ACT.Sigmoid).then_inc(act_done[0], act.step("route0", "sigmoid", 0))

            with e.Fori(0, ITERS) as i:
                for m in range(2):
                    for h, (c0, c1) in enumerate(SPAN):
                        for k in range(LANES):
                            v = lanes[k]
                            e.wait_ge(pe_done[k], pe.at("shared0", f"up{m}_{h}", k, i))
                            A(v.y2T[:, 0:c1 - c0], v.P[:, 0, 0:c1 - c0], ACT.Silu).then_inc(act_done[k], act.step("shared0", f"s{m}_{h}", k))
            barrier(e, "shared0")

            def expert_tiles(m, phase):
                n = (HID0, HID1)[m]

                def silu(u, i, t):
                    v = slots[u]
                    e.wait_ge(pe_done[u], pe.at(phase, "up", u, i))
                    A(v.e[:, 0:HID0], v.ps1[:, 0:HID0], ACT.Silu).then_inc(act_done[u], act.step(phase, "silu", u))

                def exp(u, i, t):
                    v = slots[u]
                    e.wait_ge(pe_done[u], pe.at(phase, "up", u, i))
                    A(v.e, v.ps1, ACT.Exp, bias=minus_one[:]).then_inc(act_done[u], act.step(phase, "exp", u))

                def uT(u, i, t):
                    v = slots[u]
                    e.wait_ge(pe_done[u], pe.at(phase, "uT", u, i))
                    nc.scalar.copy(v.uT[:, 0:n], v.ps1[:, 0:n]).then_inc(act_done[u], act.step(phase, "uT", u))

                turns(e, [("silu", silu) if m == 0 else ("exp", exp), ("uT", uT)])

            expert_tiles(0, "experts0")
            barrier(e, "experts0")

            def attn(step, src, f):
                def g(k, i):
                    if step.startswith("kt"):
                        e.wait_ge(dve_done[k], dve.at("attention", "at" + step[2:], k, i))
                    e.wait_ge(pe_done[k], pe.at("attention", src, k, i))
                    f(lanes[k], i, k).then_inc(act_done[k], act.step("attention", step, k))
                return g

            def relu(n):
                return lambda v, i, k: spans(lambda h, c0, c1: A(v.QK[n][:, c0:c1], v.P[:, h, 0:c1 - c0], ACT.Relu,
                                                                 bias=w("b_qk", (n, n + 1))))

            def v_rows(v, i, k):
                for a, b, n in HP:
                    for j in range(a, b):
                        r = nc.scalar.copy(v.V[0:n, j, :, 0:DH], v.TK[0:n, j, :].rearrange("p (h e) -> p h e", e=DH))
                return r

            def keys(c):
                return lambda v, i, k: nc.scalar.copy(v.ktok[0:WIDTH[c], :], v.bank[1][0:WIDTH[c], 256:512])

            def oT(v, i, k):
                return spans(lambda h, c0, c1: nc.scalar.copy(v.oT[:, c0:c1], v.P[:, h, 0:c1 - c0]))

            def rc1(v, i, k):
                return spans(lambda h, c0, c1: A(v.rcT[:, 1 + c0:1 + c1], v.P[:, h, 0:c1 - c0], ACT.Gelu, bias=w("b_rc1")))

            def norm_kept(v, i, k):
                nb = N[:, batch_tiles(i * LANES + k), :]
                for a, b, n in HP:
                    nc.scalar.copy(nb[0:n, a:b, :], v.norm[0:n, a:b, :])
                return to_NT(v, i, k)

            with e.Fori(0, ITERS) as i:
                steps = [attn("n5T", "norm5T", to_nT)]
                steps += [attn(x, x, relu(n)) for n, x in enumerate(("q0", "q1", "k0", "k1"))]
                steps += [attn("v", "v", v_rows)]
                steps += [attn(f"kt{c}", f"sc{c}", keys(c)) for c in range(TILES)]
                steps += [attn("oT", "oT", oT), attn("n6T", "norm6T", norm_kept), attn("rc1", "rc1", rc1)]
                for f in steps:
                    for k in range(LANES):
                        if f is steps[1] or f is steps[2]:
                            e.wait_ge(dve_done[k], dve.at("attention", "h3", k, i))
                        if f is steps[-1]:
                            e.wait_ge(dve_done[k], dve.at("attention", "h4", k, i))
                        f(k, i)

            e.wait_ge(dve_done[0], dve.at("route1", "values", 0, 0))
            A(top_vals[:, 0:NTILE], top_vals[:, 0:NTILE], ACT.Exp).then_inc(act_done[0], act.step("route1", "exp", 0))
            barrier(e, "route1")
            expert_tiles(1, "experts1")
            barrier(e, "experts1")

            with e.Fori(0, ITERS) as i:
                for m in range(4):
                    for k in range(LANES):
                        v = lanes[k]
                        e.wait_ge(pe_done[k], pe.at("output", f"c{m}", k, i))
                        if m == 0:
                            e.wait_ge(pe_done[k], pe.at("output", "down", k, i - 1))
                        r = spans(lambda h, c0, c1: A(v.sT[m][:, c0:c1], v.P[:, h, 0:c1 - c0], ACT.Silu,
                                                      bias=w("b_sh1", (m, m + 1))))
                        r.then_inc(act_done[k], act.step("output", f"s{m}", k))

        @block.vector
        def _(e):
            V = nc.vector
            for done in dve_done:
                e.sem_inc(done, Steps.CREDIT)
            for t in (zeros, NT, S):
                V.memset(t[:], 0.0)
            for v in lanes:
                V.memset(v.h1, 0.0)
                V.memset(v.h2[64:65, :], 1.0)
                V.memset(v.mv[:], 1.0)
            V.memset(minus_one[:], -1.0)
            e.drain().then_inc(zero_set, 1)
            e.wait_ge(inputs_in, 32)
            V.tensor_scalar(a_minus_1[:], w("A"), -1.0, None, ALU.add)
            V.tensor_scalar(eb1_f[:], eb1_f[:], 1.0, None, ALU.add)
            V.memset(ones3[:], 1.0)
            for q in range(3):
                e.drain()
                V.tensor_copy(eb1_part[:, q, :], eb1_f[:])
                if q < 2:
                    e.drain()
                    V.tensor_tensor(eb1_f[:], eb1_f[:], eb1_part[:, q, :], ALU.subtract)
            e.drain().then_inc(eb1_split, 1)

            def var(n, phase, src, widths, after=None):
                def f(k, i):
                    v = lanes[k]
                    if after:
                        e.wait_ge(pe_done[k], pe.at(phase, after, k, i))
                    s = src(v, i, k)
                    for j in range(TILES):
                        V.bn_stats(v.st[0:widths[j], j, :], s[0:widths[j], j, :])
                    e.drain()
                    for j in range(TILES):
                        V.bn_aggr(v.mv[0:widths[j], j, :], v.st[0:widths[j], j, :])
                    e.drain()
                    V.tensor_scalar(v.ve[:], v.mv[:, :, 1], EPS, None, ALU.add).then_inc(dve_done[k], dve.step(phase, f"var{n}", k))
                return f

            def norm(n, phase, src, widths):
                def f(k, i):
                    v = lanes[k]
                    e.wait_ge(pool_done[k], pool.at(phase, f"rstd{n}", k, i))
                    s = src(v, i, k)
                    for j in range(TILES):
                        m = widths[j]
                        r = V.tensor_scalar(v.norm[0:m, j, :], s[0:m, j, :], v.mv[0:m, j, 0:1], v.rstd[0:m, j:j + 1],
                                            ALU.subtract, ALU.mult)
                    r.then_inc(dve_done[k], dve.step(phase, f"norm{n}", k))
                return f

            TOKW = [TOK_ROWS] * TILES

            def TK(v, i, k):
                return v.TK

            def Hb(v, i, k):
                return H[:, batch_tiles(i * LANES + k), :]

            def pooled(k, i):
                v = lanes[k]
                e.wait_ge(act_done[k], act.at("mixer", "y2T", k, i))
                V.tensor_tensor(v.tmp[:, 0:T - 1], v.y2T[:, 0:T - 1], v.y2T[:, 1:T], ALU.max)
                e.drain()
                V.tensor_tensor(v.y2T[:, 0:L], v.tmp[:, 0:L], v.y2T[:, 2:T], ALU.max).then_inc(dve_done[k], dve.step("mixer", "pool", k))

            def decay(k, i):
                v = lanes[k]
                e.wait_ge(act_done[k], act.at("mixer", "g", k, i))
                V.tensor_scalar(v.g, v.g, 0.05, 0.95, ALU.max, ALU.min)
                e.drain()
                V.tensor_scalar(v.a, v.g, a_minus_1[:], 1.0, ALU.mult, ALU.add).then_inc(dve_done[k], dve.step("mixer", "gates", k))

            def drive(k, i):
                v = lanes[k]
                e.wait_ge(pe_done[k], pe.at("mixer", "xB", k, i))
                for h, (c0, c1) in enumerate(SPAN):
                    r = V.scalar_tensor_tensor(v.bc[:, c0:c1], v.TKf[:, h, 0:c1 - c0], w("bias_h"), v.g[:, c0:c1], ALU.add, ALU.mult)
                r.then_inc(dve_done[k], dve.step("mixer", "b", k))

            def scan(k, i):
                v = lanes[k]
                e.drain()
                V.tensor_tensor_scan(v.hs, v.a, v.bc, 0.0, ALU.mult, ALU.add).then_inc(dve_done[k], dve.step("mixer", "scan", k))

            def add_recurrence(k, i):
                v = lanes[k]
                e.wait_ge(pe_done[k], pe.at("mixer", "y", k, i))
                e.wait_ge(act_done[k], act.at("mixer", "h1tok", k, i))
                hb = Hb(v, i, k)
                for a, b, n in HP:
                    V.scalar_tensor_tensor(hb[0:n, a:b, :], v.TK[0:n, a:b, :], P ** -0.5, v.h1tok[0:n, a:b, :], ALU.mult, ALU.add)
                e.drain().then_inc(dve_done[k], dve.step("mixer", "h2", k))

            def keep_scores(phase, ne):
                def f(k, i):
                    v = lanes[k]
                    e.wait_ge(pe_done[k], pe.at(phase, "scores", k, i))
                    sb_ = S[:, batch_tiles(i * LANES + k), :]
                    for a, b, n in HP:
                        r = V.tensor_copy(sb_[0:n, a:b, 0:ne], v.TK[0:n, a:b, 0:ne])
                    r.then_inc(dve_done[k], dve.step(phase, "scores", k))
                return f

            with e.Fori(0, ITERS) as i:
                for f in (var(1, "mixer", TK, TOKW, "r1"), norm(1, "mixer", TK, TOKW),
                          var(2, "mixer", TK, TOKW, "r2"), norm(2, "mixer", TK, TOKW), pooled,
                          var(3, "mixer", TK, WIDTH, "h1tok"), norm(3, "mixer", TK, WIDTH), decay, drive, scan,
                          add_recurrence, var(4, "mixer", Hb, WIDTH), norm(4, "mixer", Hb, WIDTH),
                          keep_scores("mixer", E0)):
                    for k in range(LANES):
                        f(k, i)

            def over_experts(x, ne):
                return x.unsqueeze(2).broadcast_to([P, NTILE, ne])

            def over_tiles(x, ne):
                return x.unsqueeze(1).broadcast_to([P, NTILE, ne])

            def top2(x, ne, first, second, vals, tag):
                best = route_small(0, NTILE)
                for n, hot in enumerate((first, second)):
                    V.tensor_reduce(vals[n], x, AX.X, ALU.max)
                    e.drain()
                    V.tensor_tensor(tag, x, over_experts(vals[n], ne), ALU.is_equal)
                    e.drain()
                    V.tensor_tensor(tag, tag, over_tiles(w("descend", (E1 - ne, E1)), ne), ALU.mult)
                    e.drain()
                    V.tensor_reduce(best, tag, AX.X, ALU.max)
                    e.drain()
                    V.tensor_tensor(hot, tag, over_experts(best, ne), ALU.is_equal)
                    e.drain()
                    if n == 0:
                        V.scalar_tensor_tensor(x, hot, -3e38, x, ALU.mult, ALU.add)
                        e.drain()

            def route(m, phase):
                ne = (E0, E1)[m]
                x, tag, first, second, both, total, upto, pos, spare = (route_buf(n, ne) for n in range(9))
                vals = [top_vals[:, 0:NTILE], top_vals[:, NTILE:2 * NTILE]]
                barrier(e, ("mixer", "attention")[m])
                scores = S[:, :, 0:ne]
                if m == 0:
                    V.tensor_tensor(x, scores, over_tiles(w("gate_bias"), ne), ALU.add)
                else:
                    V.tensor_copy(x, scores)
                e.drain()
                top2(x, ne, first, second, vals, tag)
                if m == 0:
                    V.tensor_copy(x, scores)
                    e.drain()
                    top2(x, ne, pos, spare, vals, tag)
                for hot in (first, second):
                    V.tensor_tensor(hot, hot, over_experts(w("valid"), ne), ALU.mult)
                e.drain()
                V.tensor_tensor(both, first, second, ALU.add).then_inc(dve_done[0], dve.step(phase, "onehot", 0))
                if m == 1:
                    V.tensor_tensor(vals[0], vals[1], vals[0], ALU.subtract)
                e.drain().then_inc(dve_done[0], dve.step(phase, "values", 0))

                e.wait_ge(pe_done[0], pe.at(phase, "counts", 0, 0))
                V.tensor_copy(total.rearrange("p t e -> p (t e)"), psum[:, 1, 0:NTILE * ne])
                e.drain()
                for x_ in range(ne):
                    V.tensor_tensor_scan(upto[:, :, x_], w("ones")[:, 0:NTILE], total[:, :, x_], 0.0, ALU.mult, ALU.add)
                e.drain()
                V.tensor_tensor(pos, upto, total, ALU.subtract)
                e.drain()
                V.tensor_tensor(pos.rearrange("p t e -> p (t e)"), psum[:, 0, 0:NTILE * ne],
                                pos.rearrange("p t e -> p (t e)"), ALU.add)
                n_rows = w("tile_rows")
                cmp = work[:, 10240:10240 + ne * 47].rearrange("p (e j) -> p e j", j=47)
                tiles_of, tiles_upto, first_slot = (route_small(144 + 16 * q, ne) for q in range(3))
                V.tensor_tensor(cmp, upto[:, NTILE - 1, :].unsqueeze(2).broadcast_to([P, ne, 47]),
                                n_rows.unsqueeze(1).broadcast_to([P, ne, 47]), ALU.is_gt)
                e.drain()
                V.tensor_reduce(tiles_of, cmp, AX.X, ALU.add)
                e.drain()
                V.tensor_tensor_scan(tiles_upto, w("ones")[:, 0:ne], tiles_of, 0.0, ALU.mult, ALU.add)
                e.drain()
                V.tensor_tensor(first_slot, tiles_upto, tiles_of, ALU.subtract)
                e.drain()
                V.scalar_tensor_tensor(pos, over_tiles(first_slot, ne), float(P), pos, ALU.mult, ALU.add)
                e.drain()
                slot_f = route_small(200, NTILE)
                for n, hot in enumerate((first, second)):
                    V.tensor_tensor(tag, hot, pos, ALU.mult)
                    e.drain()
                    V.tensor_reduce(slot_f, tag, AX.X, ALU.add)
                    e.drain()
                    V.tensor_copy(slot_u[:, n, :], slot_f)
                    e.drain()
                cmp = work[:, 10240:10240 + EXPERT_TILES * ne].rearrange("p (t e) -> p t e", e=ne)
                V.tensor_tensor(cmp, tiles_upto.unsqueeze(1).broadcast_to([P, EXPERT_TILES, ne]),
                                w("tile_id").unsqueeze(2).broadcast_to([P, EXPERT_TILES, ne]), ALU.is_le)
                e.drain()
                which = route_small(256, EXPERT_TILES)
                V.tensor_reduce(which, cmp, AX.X, ALU.add)
                e.drain()
                V.tensor_scalar(tile_expert[:], which, float(ne - 1), float((STRIDE0, STRIDE1)[m]), ALU.min, ALU.mult)
                e.wait_ge(act_done[0], act.at(phase, ("sigmoid", "exp")[m], 0, 0))
                rs = route_small(0, NTILE)
                if m == 0:
                    V.tensor_tensor(rs, vals[0], vals[1], ALU.add)
                    e.drain()
                    V.reciprocal(rs, rs)
                    e.drain()
                    for n in range(2):
                        V.tensor_tensor(gates[:, n, :], vals[n], rs, ALU.mult)
                else:
                    V.tensor_scalar(rs, vals[0], 1.0, None, ALU.add)
                    e.drain()
                    V.reciprocal(gates[:, 0, :], rs)
                    e.drain()
                    V.tensor_tensor(gates[:, 1, :], gates[:, 0, :], vals[0], ALU.mult)
                e.drain().then_inc(dve_done[0], dve.step(phase, "done", 0))

            route(0, "route0")

            with e.Fori(0, ITERS) as i:
                for m in range(2):
                    for h, (c0, c1) in enumerate(SPAN):
                        for k in range(LANES):
                            v = lanes[k]
                            e.wait_ge(act_done[k], act.at("shared0", f"s{m}_{h}", k, i))
                            V.tensor_tensor(v.QK[m][:, c0:c1], v.y2T[:, 0:c1 - c0], v.P[:, 1, 0:c1 - c0], ALU.mult
                            ).then_inc(dve_done[k], dve.step("shared0", f"u{m}_{h}", k))
                for k in range(LANES):
                    v = lanes[k]
                    e.wait_ge(pe_done[k], pe.at("shared0", "down", k, i))
                    hb = Hb(v, i, k)
                    for a, b, n in HP:
                        r = V.tensor_tensor(hb[0:n, a:b, :], v.TK[0:n, a:b, :], hb[0:n, a:b, :], ALU.add)
                    r.then_inc(dve_done[k], dve.step("shared0", "h", k))
            barrier(e, "shared0")

            def expert_tiles(m, phase):
                def xT(u, i, t):
                    v = slots[u]
                    e.wait_ge(pe_done[u], pe.at(phase, "xT", u, i))
                    V.tensor_copy(v.xT, v.psx).then_inc(dve_done[u], dve.step(phase, "xT", u))

                def gated(u, i, t):
                    v = slots[u]
                    e.wait_ge(act_done[u], act.at(phase, "silu", u, i))
                    V.tensor_tensor(v.e[:, 0:HID0], v.e[:, 0:HID0], v.ps1[:, HID0:2 * HID0], ALU.mult
                                    ).then_inc(dve_done[u], dve.step(phase, "u", u))

                def elu(u, i, t):
                    v = slots[u]
                    e.wait_ge(act_done[u], act.at(phase, "exp", u, i))
                    V.scalar_tensor_tensor(v.e, v.e, 1.0, v.ps1, ALU.min, ALU.max
                                           ).then_inc(dve_done[u], dve.step(phase, "u", u))

                def y(u, i, t):
                    v = slots[u]
                    e.wait_ge(pe_done[u], pe.at(phase, "down", u, i))
                    e.wait_ge(row_stored[u], 16 * i + 16 * EITERS * m)
                    V.tensor_copy(v.y, v.psy).then_inc(dve_done[u], dve.step(phase, "y", u))

                turns(e, [("xT", xT), ("u", gated if m == 0 else elu), ("y", y)])

            expert_tiles(0, "experts0")
            barrier(e, "experts0")

            for v in lanes:
                V.memset(v.V, 1.0)
            e.drain()

            def weigh_rows(v, i, k, n_gather, phase):
                e.wait_ge(gathered[k], 16 * GATHERS * i + (16 * GATHERS + 16 * GATHERS * ITERS * n_gather))
                V.tensor_copy(v.gk[:], gates[:, :, batch_tiles(i * LANES + k)])
                e.drain()
                for j in range(TILES):
                    n = WIDTH[j]
                    V.tensor_scalar(v.Y[0][0:n, j, :], v.Y[0][0:n, j, :], v.gk[0:n, 0, j:j + 1], None, ALU.mult)
                e.drain()
                for j in range(TILES):
                    n = WIDTH[j]
                    V.scalar_tensor_tensor(v.Y[0][0:n, j, :], v.Y[1][0:n, j, :], v.gk[0:n, 1, j:j + 1], v.Y[0][0:n, j, :],
                                           ALU.mult, ALU.add)
                e.drain()

            def add_experts(k, i):
                v = lanes[k]
                weigh_rows(v, i, k, 0, "attention")
                hb = Hb(v, i, k)
                for a, b, n in HP:
                    V.tensor_tensor(hb[0:n, a:b, :], v.Y[0][0:n, a:b, :], hb[0:n, a:b, :], ALU.add)
                V.memset(v.state, 0.0)
                e.drain().then_inc(dve_done[k], dve.step("attention", "h3", k))

            def cos_sin(n):
                def f(k, i):
                    v = lanes[k]
                    name = ("q0", "q1", "k0", "k1")[n]
                    e.wait_ge(act_done[k], act.at("attention", name, k, i))
                    V.tensor_tensor(v.QK[n], v.QK[n], w("cos_sin"), ALU.mult).then_inc(dve_done[k], dve.step("attention", name, k))
                return f

            def mask(c):
                def f(k, i):
                    v = lanes[k]
                    n = WIDTH[c]
                    e.wait_ge(pe_done[k], pe.at("attention", f"sc{c}", k, i))
                    cz = w("causal").rearrange("p (g i) -> p g i", g=2)
                    for r4 in range(4):
                        bk = v.bank[r4][:, 0:2 * P].rearrange("p (g i) -> p g i", g=2)
                        r = V.tensor_tensor(v.AT[0:n, r4, :, 0:n], bk[0:n, :, 0:n], cz[0:n, :, 0:n], ALU.mult)
                    r.then_inc(dve_done[k], dve.step("attention", f"at{c}", k))
                return f

            def context(c):
                def f(k, i):
                    v = lanes[k]
                    n = WIDTH[c]
                    e.wait_ge(pe_done[k], pe.at("attention", f"cx{c}", k, i))
                    cx = v.bank[3][:, 256:256 + 136].rearrange("p (h e) -> p h e", e=DH + 1)
                    V.tensor_scalar(v.rden[0:n], cx[0:n, :, DH], 1e-6, None, ALU.add)
                    if c < TILES - 1:
                        V.tensor_tensor(v.upd[:], v.bank[0][:, 256:256 + 136], w("block"), ALU.mult)
                    e.drain()
                    V.reciprocal(v.rden[0:n], v.rden[0:n])
                    if c < TILES - 1:
                        V.tensor_tensor(v.state, v.state, v.upd[:], ALU.add)
                    e.drain()
                    V.tensor_tensor(v.norm[0:n, c, :].rearrange("p (h e) -> p h e", e=DH), cx[0:n, :, 0:DH], 
                                    v.rden[0:n].unsqueeze(2).broadcast_to([n, HEADS, DH]), ALU.mult).then_inc(dve_done[k], dve.step("attention", f"st{c}", k))
                return f

            def otok(k, i):
                e.drain().then_inc(dve_done[k], dve.step("attention", "otok", k))

            def add_attention(k, i):
                v = lanes[k]
                e.wait_ge(pe_done[k], pe.at("attention", "out", k, i))
                hb = Hb(v, i, k)
                for a, b, n in HP:
                    V.tensor_tensor(hb[0:n, a:b, :], v.TK[0:n, a:b, :], hb[0:n, a:b, :], ALU.add)
                V.memset(v.rcT[:, 0:1], 0.0)
                V.memset(v.rcT[:, L + 1:L + 2], 0.0)
                e.drain().then_inc(dve_done[k], dve.step("attention", "h4", k))

            with e.Fori(0, ITERS) as i:
                steps = [add_experts, var(5, "attention", Hb, WIDTH), norm(5, "attention", Hb, WIDTH)]
                steps += [cos_sin(n) for n in range(4)]
                for c in range(TILES):
                    steps += [mask(c), context(c)]
                steps += [otok, add_attention, var(6, "attention", Hb, WIDTH), norm(6, "attention", Hb, WIDTH),
                          keep_scores("attention", E1)]
                for f in steps:
                    for k in range(LANES):
                        f(k, i)

            route(1, "route1")
            e.wait_ge(pe_done[0], pe.at("route1", "colsum", 0, 0))
            e.wait_ge(experts1_in, 32)
            for q, (x0, x1) in enumerate(((0, 4), (4, 8), (8, E1))):
                r = V.tensor_tensor(eb2[0:1, x0 * P:x1 * P], eb2[0:1, x0 * P:x1 * P], psum[0:1, 2 + q, 0:(x1 - x0) * P], ALU.subtract)
            r.then_inc(dve_done[0], dve.step("route1", "bias", 0))
            for q in range(3):
                e.drain()
                if q:
                    e.wait_ge(eb2_stored, 16 * q)
                V.tensor_copy(eb2_part, eb2)
                e.drain().then_inc(eb2_split, 1)
                if q < 2:
                    V.tensor_tensor(eb2, eb2, eb2_part, ALU.subtract)
            barrier(e, "route1")
            expert_tiles(1, "experts1")
            barrier(e, "experts1")

            def z(k, i):
                v = lanes[k]
                weigh_rows(v, i, k, 1, "output")
                e.wait_ge(pe_done[k], pe.at("output", "down", k, i))
                nb = N[:, batch_tiles(i * LANES + k), :]
                for a, b, n in HP:
                    V.tensor_tensor(v.Y[0][0:n, a:b, :], v.Y[0][0:n, a:b, :], v.TK[0:n, a:b, :], ALU.add)
                e.drain()
                for a, b, n in HP:
                    V.tensor_tensor(v.Y[0][0:n, a:b, :], v.Y[0][0:n, a:b, :], nb[0:n, a:b, :], ALU.add)
                e.drain().then_inc(dve_done[k], dve.step("output", "z", k))

            def Yb(v, i, k):
                return v.Y[0]

            def final(k, i):
                v = lanes[k]
                hb = Hb(v, i, k)
                e.drain()
                for a, b, n in HP:
                    V.tensor_tensor(v.norm[0:n, a:b, :], v.norm[0:n, a:b, :],
                                    w("ln_g")[0:n].unsqueeze(1).broadcast_to([n, b - a, P]), ALU.mult)
                    V.tensor_tensor(hb[0:n, a:b, :], hb[0:n, a:b, :],
                                    w("ln_b")[0:n].unsqueeze(1).broadcast_to([n, b - a, P]), ALU.add)
                e.drain()
                for a, b, n in HP:
                    r = V.tensor_tensor(hb[0:n, a:b, :], hb[0:n, a:b, :], v.norm[0:n, a:b, :], ALU.add)
                r.then_inc(dve_done[k], dve.step("output", "h5", k))

            with e.Fori(0, ITERS) as i:
                for f in (z, var(7, "output", Yb, WIDTH), norm(7, "output", Yb, WIDTH), final):
                    for k in range(LANES):
                        f(k, i)

        @block.gpsimd
        def _(e):
            G = nc.gpsimd
            for done in pool_done:
                e.sem_inc(done, Steps.CREDIT)
            e.wait_ge(inputs_in, 32)

            def rstd(phase, n, k, i):
                e.wait_ge(dve_done[k], dve.at(phase, f"var{n}", k, i))
                G.tensor_tensor(lanes[k].rstd[:], lanes[k].ve[:], w("minus_half"), ALU.pow).then_inc(pool_done[k], pool.step(phase, f"rstd{n}", k))

            def scatter(m):
                e.wait_ge(rows_zeroed, 32)
                e.wait_ge(dve_done[0], dve.at(("route0", "route1")[m], "done", 0, 0))
                for t in range(NTILE):
                    n = WIDTH[t % TILES]
                    for q in range(2):
                        G.indirect_dma_start(rows_in[m], bass.IndirectOffsetOnAxis(ap=slot_u[0:n, q, t:t + 1], axis=0),
                                             N[0:n, t, :], None).then_inc(scattered[m], 16)

            def gather(m, k, i):
                v = lanes[k]
                G.tensor_copy(v.ix[:], slot_u[:, :, batch_tiles(i * LANES + k)])
                e.drain()
                for j in range(TILES):
                    n = WIDTH[j]
                    for q in range(2):
                        G.indirect_dma_start(v.Y[q][0:n, j, :], None, rows_out[m],
                                             bass.IndirectOffsetOnAxis(ap=v.ix[0:n, q, j:j + 1], axis=0)).then_inc(gathered[k], 16)

            with e.Fori(0, ITERS) as i:
                for n in range(1, 5):
                    for k in range(LANES):
                        rstd("mixer", n, k, i)
            def store_rows(m, phase):
                with e.Fori(0, EITERS) as i:
                    for u in range(SLOTS):
                        e.wait_ge(dve_done[u], dve.at(phase, "y", u, i))
                        e.dma_start(rows_out[m].rearrange("(t p) d -> t p d", p=P)[
                            bass.ds(i * SLOTS + u, 1)].rearrange("a p d -> p (a d)"), slots[u].y).then_inc(row_stored[u], 16)

            scatter(0)
            store_rows(0, "experts0")
            for s in row_stored:
                e.wait_ge(s, 16 * EITERS)
            barrier(e, "experts0")
            with e.Fori(0, ITERS) as i:
                for k in range(LANES):
                    e.wait_ge(pe_done[k], pe.at("attention", "cx5", k, i - 1))
                    gather(0, k, i)
                for n in (5, 6):
                    for k in range(LANES):
                        rstd("attention", n, k, i)
            scatter(1)
            store_rows(1, "experts1")
            for s in row_stored:
                e.wait_ge(s, 32 * EITERS)
            barrier(e, "experts1")
            with e.Fori(0, ITERS) as i:
                for k in range(LANES):
                    e.wait_ge(dve_done[k], dve.at("output", "norm7", k, i - 1))
                    gather(1, k, i)
                for k in range(LANES):
                    rstd("output", 7, k, i)


def _layout(x):
    f = {k: np.asarray(v) for k, v in x.items()}
    pack = np.zeros((P, PACK_COLS), np.float32)

    def put(name, a, col=0):
        at, rows, n = PACK[name]
        a = np.asarray(a)
        pack[0:a.shape[0], at + col:at + col + a.shape[1]] = a

    wc = f["L0_tok_w_compress"][:, :, 0].T
    put("compress", wc)
    put("compress", wc, 64)
    wm = f["L0_tok_w_main"]
    put("main01", np.concatenate([wm[:, :, 0].T, wm[:, :, 1].T]))
    put("main2", wm[:, :, 2].T)
    put("expand", np.concatenate([f["L0_tok_w_expand"][:, :, 0].T, f["L0_tok_b_expand"][None]]))
    put("ff1", f["L0_tok_w_ff1"].T)
    put("ff2", np.concatenate([f["L0_tok_w_ff2"].T, f["L0_tok_b_ff2"][None]]))
    put("b_compress", np.concatenate([f["L0_tok_b_compress"]] * 2)[:, None])
    for name, src in (("b_main", "L0_tok_b_main"), ("b_ff1", "L0_tok_b_ff1"), ("g_conv", "L0_tok_g_conv_norm"),
                      ("b_conv", "L0_tok_b_conv_norm"), ("g_ff", "L0_tok_g_ff_norm"), ("b_ff", "L0_tok_b_ff_norm"),
                      ("A", "L0_attn_A"), ("bias_h", "L0_attn_bias_h"), ("b_rc1", "L1_ffn_rc_b1")):
        put(name, f[src][:, None])
    for name, src in (("Wg", "L0_attn_Wg"), ("Bm", "L0_attn_B"), ("C", "L0_attn_C"), ("D", "L0_attn_D"), ("gate", "L0_ffn_gate_w")):
        put(name, f[src].T)
    put("gate_bias", np.broadcast_to(f["L0_ffn_biases"], (P, E0)))
    for name, src in (("bias_y", "L0_attn_bias_y"), ("b_out", "L1_attn_b_out"), ("b_rc2", "L1_ffn_rc_b2"), ("b_sh2", "L1_ffn_sh_b2")):
        put(name, f[src][None])
    wqkv, bqkv = f["L1_attn_W_qkv"], f["L1_attn_b_qkv"]
    twice = np.concatenate([np.concatenate([np.arange(DH * h, DH * h + DH)] * 2) for h in range(HEADS)])
    for s in range(2):
        for g in range(2):
            cols = s * P + twice[g * P:(g + 1) * P]
            put("qk"[s] + str(g), wqkv[:, cols])
            put("b_qk", bqkv[cols][:, None], 2 * s + g)
    put("v", wqkv[:, 2 * P:])
    put("b_v", bqkv[2 * P:][None])
    put("out", f["L1_attn_W_out"])
    put("rc1", f["L1_ffn_rc_w1"].transpose(1, 2, 0).reshape(P, 3 * P))
    put("rc2", f["L1_ffn_rc_w2"].transpose(1, 2, 0).reshape(P, 3 * E1))
    put("b_sh1", f["L1_ffn_sh_b1"].reshape(4, P).T)
    put("ln_g", np.broadcast_to(f["L1_ffn_ln_g"], (P, P)))
    put("ln_b", np.broadcast_to(f["L1_ffn_ln_b"], (P, P)))
    r = np.arange(P)
    put("ident", np.eye(P, dtype=np.float32))
    put("ones", np.ones((P, P), np.float32))
    put("earlier", (r[:, None] < r[None]).astype(np.float32))
    put("causal", np.tile((r[:, None] <= r[None]).astype(np.float32), (1, 2)))
    angle = (np.float32(np.pi / 2) * np.arange(L, dtype=np.float32) / np.float32(L))[None]
    put("cos_sin", np.where((r // DH % 2 == 0)[:, None], np.cos(angle), np.sin(angle)).astype(np.float32))
    put("block", np.tile((r[:, None] // 32 == np.arange(68)[None] // 17), (1, 2)).astype(np.float32))
    put("valid", (r[:, None] < np.array(WIDTH * B)[None]).astype(np.float32))
    put("descend", np.broadcast_to(np.arange(E1, 0, -1, dtype=np.float32), (P, E1)))
    put("tile_rows", np.broadcast_to(P * np.arange(47, dtype=np.float32), (P, 47)))
    put("tile_id", np.broadcast_to(np.arange(EXPERT_TILES, dtype=np.float32), (P, EXPERT_TILES)))
    put("minus_half", np.full((P, TILES), -0.5, np.float32))

    def rows(a, hid):
        return a.reshape(-1, hid // P, P, P).transpose(2, 0, 1, 3).reshape(P, -1)

    big = {
        "xT": f["x"].transpose(0, 2, 1),
        "pack": pack,
        "ew_0": np.concatenate([f["L0_ffn_w1"].transpose(1, 0, 2), f["L0_ffn_w3"].transpose(1, 0, 2),
                                rows(f["L0_ffn_w2"], HID0).reshape(P, E0, -1)], 2).reshape(P, -1),
        "sw13": np.concatenate([f["L0_ffn_sw1"], f["L0_ffn_sw3"]], 1),
        "sw2": rows(f["L0_ffn_sw2"][None], HID0),
        "ew_1": np.concatenate([f["L1_ffn_e_w1"].transpose(1, 0, 2), rows(f["L1_ffn_e_w2"], HID1).reshape(P, E1, -1)],
                               2).reshape(P, -1),
        "eb1": f["L1_ffn_e_b1"].reshape(P, -1),
        "eb2": f["L1_ffn_e_b2"].reshape(1, -1),
        "conv1": f["L1_ffn_sh_w1"].transpose(1, 2, 0).reshape(P, -1),
        "conv2": rows(f["L1_ffn_sh_w2"][:, :, 0].T[None], HID1),
    }
    return {k: np.ascontiguousarray(v) for k, v in big.items()}


def build(nc, arrays):
    d = {k: nc.dram_tensor(f"in_{k}", a.shape, mybir.dt.from_np(a.dtype), kind="ExternalInput").ap() for k, a in arrays.items()}
    out = nc.dram_tensor("out_0", (B, L, P), F32, kind="ExternalOutput").ap()
    audio_tower(nc, d, out)


def kernel(**inputs):
    import concourse.bacc as bacc
    from concourse.bass_utils import run_bass_kernel_spmd

    arrays = _layout(inputs)
    nc = bacc.Bacc("TRN2", target_bir_lowering=False, num_devices=1)
    build(nc, arrays)
    r = run_bass_kernel_spmd(nc, [{f"in_{k}": a for k, a in arrays.items()}], core_ids=[0])
    return r.results[0]["out_0"]
```

```python
from contextlib import ExitStack

import numpy as np
import concourse.bass as bass
from concourse import mybir

F32 = mybir.dt.float32
U32 = mybir.dt.uint32
BF16 = mybir.dt.bfloat16
I32 = mybir.dt.int32
ALU = mybir.AluOpType
ACT = mybir.ActivationFunctionType
AX = mybir.AxisListType

P = 128
B, T = 8, 750
L = T - 2
HALF_T = T // 2
TOK_ROWS = T // 6
TILES = 6
WIDTH = [min(P, L - P * j) for j in range(TILES)]
SPAN = [(0, 384), (384, L)]
NTILE = B * TILES
PAIRS = 2 * B * L
EXPERT_TILES = 104
E0, HID0 = 8, 256
E1, HID1 = 10, 512
assert (PAIRS + (E1 - 1 + 1) * (P - 1)) // P <= EXPERT_TILES
PAD = 4
NCOL = L + 2 * PAD
HEADS, DH = 8, 16
LANES = 2
ITERS = B // LANES
OUT_LANES = 4
OUT_ITERS = B // OUT_LANES
STRIDE0 = 2 * HID0 + (HID0 // P) * P
STRIDE1 = HID1 + (HID1 // P) * P
SLOTS = 4
EITERS = EXPERT_TILES // SLOTS
KTAPS = 9
EPS = 1e-5

BIAS_ROWS = ["bias_y", "b_v", "b_out", "b_rc2", "b_sh2"]

PACK = {}
PACK_COLS = 0


def _place(name, rows, cols):
    global PACK_COLS
    PACK[name] = (PACK_COLS, rows, cols)
    PACK_COLS += cols


for _n, _r, _c in [
    ("compress", P, P), ("main01", P, 64), ("main2", 64, 64), ("expand", 65, P), ("ff1", P, 64), ("ff2", 65, P),
    ("b_compress", P, 1), ("b_main", 64, 1), ("b_ff1", 64, 1), ("g_conv", P, 1), ("b_conv", P, 1),
    ("g_ff", P, 1), ("b_ff", P, 1), ("A", P, 1), ("bias_h", P, 1),
    ("Wg", P, P), ("Bm", P, P), ("C", P, P), ("D", P, P), ("gate", P, E0), ("gate_bias", P, E0), 
    ("q0", P, P), ("q1", P, P), ("k0", P, P), ("k1", P, P), ("b_qk", P, 4), ("v", P, P),
    ("out", P, P),
    ("rc1", P, 3 * P), ("b_rc1", P, 1), ("rc2", P, 3 * E1), ("b_sh1", P, 4), ("head_of", P, 2),
    ("ln_g", P, P), ("ln_b", P, P),
    ("ident", P, P), ("ones", P, P), ("earlier", P, P), ("causal", P, 2 * P), ("cos_sin", P, L), ("block", P, 136),
    ("valid", P, NTILE), ("descend", P, E1), ("tile_rows", P, 47), ("tile_id", P, EXPERT_TILES), ("minus_half", P, TILES),
]:
    _place(_n, _r, _c)

AHEAD = {"xT": 3, "load": 2, "up": 2, "silu": 2, "exp": 2, "u": 2, "uT": 1, "down": 0, "y": 0}


def turns(eng, stages, begin=None, end=None):
    def run(i, u, first=False, last=False):
        for name, f in stages:
            t = u + AHEAD[name]
            if first and t < 0 or last and t >= SLOTS:
                continue
            f(t % SLOTS, i + t // SLOTS, t)

    for u in range(-3, 0):
        run(0, u, first=True)
    with eng.Fori(0, EITERS - 1) as i:
        if begin:
            begin()
        for u in range(SLOTS):
            run(i, u)
        if end:
            end()
    if begin:
        begin()
    for u in range(SLOTS):
        run(EITERS - 1, u, last=True)




class Steps:

    CREDIT = 32

    def __init__(self, phases):
        self.phases, self.base, self.next = phases, {}, {}
        at = {}
        for phase, (iters, count, names) in phases.items():
            assert len(names) <= self.CREDIT
            for lane in range(count):
                self.base[phase, lane] = at.get(lane, self.CREDIT)
                at[lane] = self.base[phase, lane] + iters * len(names)

    def step(self, phase, step, lane):
        names = self.phases[phase][2]
        n = self.next.get((phase, lane), 0)
        assert names[n] == step, (phase, lane, step, names[n])
        self.next[phase, lane] = (n + 1) % len(names)
        return 1

    def at(self, phase, step, lane, i):
        names = self.phases[phase][2]
        return i * len(names) + (self.base[phase, lane] + names.index(step) + 1)

    def end(self, phase):
        if phase not in self.phases:
            return []
        iters, count, names = self.phases[phase]
        return [(lane, self.base[phase, lane] + iters * len(names)) for lane in range(count)]


def audio_tower(nc, d, out):
    with ExitStack() as ctx:
        def sb(name, shape, dt=F32):
            return ctx.enter_context(nc.sbuf_tensor(name, shape, dt))

        def sem(name):
            return ctx.enter_context(nc.semaphore(name))

        rows_in = [nc.dram_tensor(f"rows_in{m}", (EXPERT_TILES * P, P), F32, kind="Internal").ap() for m in range(2)]
        rows_out = [nc.dram_tensor(f"rows_out{m}", (EXPERT_TILES * P, P), F32, kind="Internal").ap() for m in range(2)]

        pack = sb("pack", [P, PACK_COLS])
        H = sb("H", [P, NTILE, P])
        N = sb("N", [P, NTILE, P])
        NT = sb("NT", [P, B, NCOL])
        S = sb("S", [P, NTILE, E1])
        gates = sb("gates", [P, 2, NTILE])
        slot_u = sb("slot_u", [P, 2, NTILE], U32)
        tile_expert = sb("tile_expert", [P, EXPERT_TILES], I32)
        zeros = sb("zeros", [P, P])
        a_minus_1 = sb("a_minus_1", [P, 1])

        def w(name, cols=None):
            at, rows, n = PACK[name]
            lo, hi = cols or (0, n)
            return pack[0:rows, at + lo:at + hi]

        ident = w("ident")

        W_COLS = 7040
        wreg = sb("wreg", [P, W_COLS])
        ew_0 = wreg[:, 0:E0 * STRIDE0]
        sw13 = wreg[:, 6144:6144 + 512]
        sw2 = wreg[:, 6656:6656 + 256]
        conv1 = wreg[:, 0:KTAPS * 512]
        conv2 = wreg[:, 4608:4608 + 512]

        LANE_COLS = 7776
        work = sb("work", [P, LANES * LANE_COLS])
        ew_1 = work[:, 0:E1 * STRIDE1]
        eb = wreg[0:3, 0:E1 * STRIDE1 // 2].bitcast(BF16)
        eb_v = eb.rearrange("q (x c) -> q x c", x=E1)
        ones3 = sb("ones3", [3, P], BF16)
        EB1 = E1 * HID1 // P
        EB = EB1 + len(BIAS_ROWS)
        rows3 = sb("rows3", [3, len(BIAS_ROWS) * P], BF16)
        rows_dram = nc.dram_tensor("bias_rows", (3, len(BIAS_ROWS) * P), BF16, kind="Internal").ap()

        def add_bias(acc, name, n, cols=P):
            at = BIAS_ROWS.index(name) * P
            return nc.tensor.matmul(acc, ones3[:, 0:n], rows3[:, at:at + cols], start=False, stop=True)

        eb1_f = sb("eb1_f", [P, EB])
        eb1_part = sb("eb1_part", [P, 3, EB], BF16)
        eb1_dram = nc.dram_tensor("eb1_parts", (3, E1 * HID1), BF16, kind="Internal").ap()
        eb1_split = sem("eb1_split")
        eb1_stored = sem("eb1_stored")
        eb2_dram = nc.dram_tensor("eb2_parts", (3, E1 * P), BF16, kind="Internal").ap()
        rows_in_sb = sem("bias_rows_in")
        eb2_split = sem("eb2_split")
        eb2_stored = sem("eb2_stored")
        eb2_in = sem("eb2_in")
        eb2 = wreg[0:1, 5120:5120 + E1 * P]
        eb2_part = wreg[0:1, 6400:6400 + E1 * P // 2].bitcast(BF16)

        def view(lane, at, n, rows=P):
            return work[0:rows, lane * LANE_COLS + at:lane * LANE_COLS + at + n]

        class Lane:
            pass

        lanes = []
        for ln in range(LANES):
            v = Lane()
            v.xT = view(ln, 0, T)
            v.h1 = view(ln, 768, T + 2)
            v.h2 = view(ln, 1536, T)
            v.norm = view(ln, 2304, 768).rearrange("p (j d) -> p j d", d=P)
            v.y1T = view(ln, 3072, T)
            v.g = view(ln, 3072, L)
            v.y2T = view(ln, 3840, T)
            v.hs = view(ln, 3840, L)
            v.tmp = view(ln, 4608, T)
            v.nT = view(ln, 4608, L)
            v.h1tok = view(ln, 5376, 768).rearrange("p (j d) -> p j d", d=P)
            v.a = view(ln, 6144, L)
            v.bc = view(ln, 6912, L)
            v.Y = [view(ln, 768 * k, 768).rearrange("p (j d) -> p j d", d=P) for k in range(2)]
            v.QK = [view(ln, a, L) for a in (0, 768, 3072, 3840)]
            v.oT = view(ln, 4608, L)
            v.V = view(ln, 5376, 816).rearrange("p (j h e) -> p j h e", h=HEADS, e=DH + 1)
            v.AT = view(ln, 6192, 1024).rearrange("p (r g i) -> p r g i", r=4, g=2)
            v.ktok = view(ln, 7216, 256)
            v.state = view(ln, 7472, 136)
            v.rden = view(ln, 7608, 8)
            v.rcT = view(ln, 3072, L + 2)
            v.sT = [view(ln, 3072 + 768 * m, L) for m in range(4)]
            v.st = sb(f"stats{ln}", [P, TILES, 6])
            v.mv = sb(f"mean_var{ln}", [P, TILES, 2])
            v.ve = sb(f"var_eps{ln}", [P, TILES])
            v.rstd = sb(f"rstd{ln}", [P, TILES])
            v.upd = sb(f"upd{ln}", [P, 136])
            lanes.append(v)

        slots = []
        for u in range(SLOTS):
            v = Lane()
            at = 10240 + u * 1300
            v.x = work[:, at:at + P]
            v.xT = work[:, at + 128:at + 256]
            v.e = work[:, at + 256:at + 768]
            v.uT = work[:, at + 768:at + 1280]
            v.y = sb(f"expert_y{u}", [P, P])[:]
            slots.append(v)
        assert 10240 + SLOTS * 1300 <= LANES * LANE_COLS

        conv_h = sb("conv_h", [P, 4, SPAN[0][1]])
        conv_rows = [sb(f"conv_rows{q}", [P, 3 * P]) for q in range(2)]
        shared_rows = nc.dram_tensor("shared_rows", (B, 2, P, 3 * P), F32, kind="Internal").ap()

        def route_buf(n, ne):
            return work[:, 10240 + 480 * n:10240 + 480 * n + NTILE * ne].rearrange("p (t e) -> p t e", e=ne)

        def route_small(at, n):
            return work[:, 14560 + at:14560 + at + n]

        top_vals = route_small(48, 2 * NTILE)
        for v in lanes:
            v.gk = sb(f"gate_b{lanes.index(v)}", [P, 2, TILES])
            v.ix = sb(f"slot_b{lanes.index(v)}", [P, 2, TILES], U32)
        minus_one = sb("minus_one", [P, 1])

        psum = ctx.enter_context(nc.psum_tensor("psum", [P, 8, 512], F32))
        for ln, v in enumerate(lanes):
            v.P = psum[:, 4 * ln:4 * ln + 2, :]
            v.TK = psum[:, 4 * ln + 2:4 * ln + 4, :].rearrange("p b (j d) -> p (b j) d", d=P)
            v.TKf = psum[:, 4 * ln + 2:4 * ln + 4, :]
            v.bank = [psum[:, 4 * ln + r, :] for r in range(4)]
            v.AB = psum[:, 3 * ln:3 * ln + 2, :]
            v.ABt = v.AB.rearrange("p b (j d) -> p (b j) d", d=P)
            v.C = psum[:, 3 * ln + 2, :]
            v.QB = view(ln, 4608, 512).rearrange("p (g s i) -> p g s i", g=2, s=2)
            v.Q2 = view(ln, 0, 2 * 768).rearrange("p (g c) -> p g c", g=2)
            v.AT2 = view(ln, 6192, 1024).rearrange("p (x i) -> p x i", i=P)
        outs = []
        for ln in range(OUT_LANES):
            v = Lane()
            at = ln * (LANES * LANE_COLS // OUT_LANES)
            v.Y = [work[:, at + 768 * q:at + 768 * (q + 1)].rearrange("p (j d) -> p j d", d=P) for q in range(2)]
            v.norm = work[:, at + 1536:at + 2304].rearrange("p (j d) -> p j d", d=P)
            v.sh = work[:, at + 2304:at + 3072].rearrange("p (h c) -> p h c", h=2)
            v.st = sb(f"out_stats{ln}", [P, TILES, 6])
            v.mv = sb(f"out_mean_var{ln}", [P, TILES, 2])
            v.ve = sb(f"out_var_eps{ln}", [P, TILES])
            v.rstd = sb(f"out_rstd{ln}", [P, TILES])
            v.gk = sb(f"out_gate_b{ln}", [P, 2, TILES])
            v.ix = sb(f"out_slot_b{ln}", [P, 2, TILES], U32)
            outs.append(v)

        def lane(phase, k):
            return (outs if phase == "output" else lanes)[k]

        def batch(phase, k, i):
            return i * (OUT_LANES if phase == "output" else LANES) + k

        conv_bank = [psum[:, 6 + q, :] for q in range(2)]
        for u, v in enumerate(slots):
            v.ps1 = psum[:, 2 * u, :]
            v.psx = psum[:, 2 * u, 0:P]
            v.psy = psum[:, 2 * u + 1, 0:P]

        def chunk_steps(names):
            return [f"{n}{c}" for c in range(TILES) for n in names]

        pe_done = [sem(f"pe_done{k}") for k in range(4)]
        pe = Steps({
            "mixer": (ITERS, LANES, ["compress", "main", "r1", "norm1T", "ff1", "r2", "norm2T", "h1tok", "norm3T",
                              "Wg", "xB", "y", "norm4T", "scores"]),
            "route0": (1, 1, ["counts"]),
            "shared0": (ITERS, LANES, ["up0_0", "up0_1", "up1_0", "up1_1", "down"]),
            "experts0": (EITERS, SLOTS, ["xT", "up", "uT", "down"]),
            "attention": (ITERS, LANES, ["norm5T", "q0", "q1", "k0", "k1", "v"]
                          + chunk_steps(["sc", "cx"]) + ["oT", "out", "norm6T", "rc1", "scores"]),
            "route1": (1, 1, ["counts"]),
            "colsum": (1, 1, ["colsum"]),
            "experts1": (EITERS, SLOTS, ["xT", "up", "uT", "down"]),
        })
        act_done = [sem(f"act_done{k}") for k in range(4)]
        act = Steps({
            "mixer": (ITERS, LANES, ["h1", "h2", "y1T", "ff", "y2T", "h1tok", "n1T", "g", "n4T"]),
            "route0": (1, 1, ["sigmoid"]),
            "shared0": (ITERS, LANES, ["s0_0", "s0_1", "s1_0", "s1_1"]),
            "experts0": (EITERS, SLOTS, ["silu", "uT"]),
            "attention": (ITERS, LANES, ["n5T", "q0", "q1", "k0", "k1", "v"] + chunk_steps(["kt"])
                          + ["oT", "n6T", "rc1"]),
            "route1": (1, 1, ["exp"]),
            "experts1": (EITERS, SLOTS, ["exp", "uT"]),
        })
        dve_done = [sem(f"dve_done{k}") for k in range(4)]
        dve = Steps({
            "mixer": (ITERS, LANES, ["var1", "norm1", "var2", "norm2", "pool", "var3", "norm3", "gates", "b", "scan",
                              "h2", "var4", "norm4", "scores"]),
            "route0": (1, 1, ["onehot", "values", "slots", "done"]),
            "shared0": (ITERS, LANES, ["u0_0", "u0_1", "u1_0", "u1_1", "h"]),
            "experts0": (EITERS, SLOTS, ["xT", "u", "y"]),
            "attention": (ITERS, LANES, ["h3", "var5", "norm5", "q0", "q1", "k0", "k1", "qb"]
                          + chunk_steps(["at", "st"]) + ["otok", "h4", "var6", "norm6", "scores"]),
            "route1": (1, 1, ["onehot", "values", "slots", "done"]),
            "colsum": (1, 1, ["bias"]),
            "experts1": (EITERS, SLOTS, ["xT", "u", "y"]),
            "output": (OUT_ITERS, OUT_LANES, ["z", "var7", "norm7", "h5"]),
        })
        pool_done = [sem(f"pool_done{k}") for k in range(4)]
        pool = Steps({
            "mixer": (ITERS, LANES, ["rstd1", "rstd2", "rstd3", "rstd4"]),
            "attention": (ITERS, LANES, ["rstd5", "rstd6"]),
            "output": (OUT_ITERS, OUT_LANES, ["rstd7"]),
        })

        UNITS = 2 * LANES
        pe_conv_done, act_conv_done = sem("pe_conv_done"), sem("act_conv_done")
        pe_conv = Steps({"conv": (ITERS, 1, [f"{x}{q}" for q in range(UNITS) for x in ("c0_", "c1_", "c2_", "c3_", "rows")])})
        act_conv = Steps({"conv": (ITERS, 1, [f"{x}{q}" for q in range(UNITS) for x in ("s0_", "s1_", "s2_", "s3_", "rows")])})
        conv_stored = [sem(f"conv_rows_stored{q}") for q in range(2)]
        shared_rows_in = [sem(f"shared_rows_in{k}") for k in range(OUT_LANES)]
        PARTS = [("taps", q, m, t) for q in range(UNITS) for m in range(4) for t in range(3)]
        for q in range(UNITS):
            PARTS.insert(min(13 * q + 13, len(PARTS)), ("rows", q, 0, 0))
        ATT_STEPS = 6 + 2 * TILES + 5

        def interleaved(conv):
            order, n = [], 0
            total = ATT_STEPS * LANES
            for x in range(total):
                order.append(("attention", x // LANES, x % LANES))
                while conv and n * total < (x + 1) * len(PARTS) and n < len(PARTS):
                    order.append(("conv", n, 0))
                    n += 1
            return order

        def barrier(eng, phase):
            for lane, value in pe.end(phase):
                eng.wait_ge(pe_done[lane], value)
            for lane, value in act.end(phase):
                eng.wait_ge(act_done[lane], value)
            for lane, value in dve.end(phase):
                eng.wait_ge(dve_done[lane], value)
            for lane, value in pool.end(phase):
                eng.wait_ge(pool_done[lane], value)

        inputs_in = sem("inputs_in")
        shared_in = sem("shared_weights_in")
        zero_set = sem("zeros_set")
        rows_zeroed = sem("rows_zeroed")
        x_in = [sem(f"x_in{k}") for k in range(LANES)]
        scattered = [sem(f"rows_scattered{m}") for m in range(2)]
        row_in = [sem(f"expert_row_in{u}") for u in range(SLOTS)]
        row_stored = [sem(f"expert_row_stored{u}") for u in range(SLOTS)]
        gathered = {"attention": [sem(f"rows_gathered{k}") for k in range(LANES)],
                    "output": [sem(f"out_rows_gathered{k}") for k in range(OUT_LANES)]}
        experts1_in = sem("experts1_in")
        conv_in = sem("conv_in")
        out_stored = [sem(f"out_stored{k}") for k in range(OUT_LANES)]
        SCATTERS = 2 * NTILE
        GATHERS = 2 * TILES

        block = ctx.enter_context(nc.Block())
        HP = [(0, 5, P), (5, 6, WIDTH[5])]

        def batch_tiles(b):
            return bass.ds(b * TILES, TILES)

        @block.sync
        def _(sp):
            sp.dma_start(pack[:], d["pack"]).then_inc(inputs_in, 16)
            sp.dma_start(eb1_f[:], d["bias"]).then_inc(inputs_in, 16)

            def load_x(k, i):
                sp.dma_start(lanes[k].xT, d["xT"][bass.ds(i * LANES + k, 1)].rearrange("a p t -> p (a t)")
                             ).then_inc(x_in[k], 16)

            for k in range(LANES):
                load_x(k, 0)
            for name, dst in (("ew_0", ew_0), ("sw13", sw13), ("sw2", sw2)):
                sp.dma_start(dst, d[name]).then_inc(shared_in, 16)
            sp.wait_ge(eb1_split, 1)
            for q in range(3):
                sp.dma_start(eb1_dram[q].rearrange("(p c) -> p c", p=P), eb1_part[:, q, 0:EB1]).then_inc(eb1_stored, 16)
                sp.dma_start(rows_dram[q].rearrange("(p c) -> p c", p=P), eb1_part[:, q, EB1:EB]).then_inc(eb1_stored, 16)
            sp.wait_ge(eb1_stored, 96)
            sp.dma_start(rows3[:], rows_dram).then_inc(rows_in_sb, 16)
            sp.wait_ge(zero_set, 1)
            for m in range(2):
                sp.dma_start(rows_in[m].rearrange("(p r) d -> p r d", p=P),
                             zeros[:].unsqueeze(1).broadcast_to([P, EXPERT_TILES, P])).then_inc(rows_zeroed, 16)
            with sp.Fori(1, ITERS) as i:
                for k in range(LANES):
                    sp.wait_ge(pe_done[k], pe.at("mixer", "r1", k, i - 1))
                    load_x(k, i)

            def expert_tiles(m, phase):
                sp.wait_ge(scattered[m], 16 * SCATTERS)
                sp.wait_ge(dve_done[0], dve.at(("route0", "route1")[m], "done", 0, 0))
                if m == 1:
                    sp.wait_ge(dve_done[0], dve.at("colsum", "bias", 0, 0))
                with sp.Fori(0, EITERS) as i:
                    for u in range(SLOTS):
                        sp.wait_ge(pe_done[u], pe.at(phase, "xT", u, i - 1))
                        sp.dma_start(slots[u].x, rows_in[m].rearrange("(t p) d -> t p d", p=P)[
                            bass.ds(i * SLOTS + u, 1)].rearrange("a p d -> p (a d)")).then_inc(row_in[u], 16)

            barrier(sp, "shared0")
            expert_tiles(0, "experts0")
            barrier(sp, "experts0")
            for name, dst in (("conv1", conv1), ("conv2", conv2)):
                sp.dma_start(dst, d[name]).then_inc(conv_in, 16)

            def store_conv_rows(i):
                for q in range(UNITS):
                    sp.wait_ge(act_conv_done, act_conv.at("conv", f"rows{q}", 0, i))
                    sp.dma_start(shared_rows[bass.ds(i * LANES + q // 2, 1), q % 2].rearrange("a p c -> (a p) c"),
                                 conv_rows[q % 2][:]).then_inc(conv_stored[q % 2], 16)

            with sp.Fori(0, ITERS - 1) as i:
                store_conv_rows(i)
            barrier(sp, "attention")
            for name, dst in (("ew_1", ew_1), ("eb2", eb2)):
                sp.dma_start(dst, d[name]).then_inc(experts1_in, 16)
            store_conv_rows(ITERS - 1)
            for q in range(3):
                sp.wait_ge(eb2_split, q + 1)
                sp.dma_start(eb2_dram[q:q + 1], eb2_part).then_inc(eb2_stored, 16)
            sp.dma_start(eb_v[:, :, 0:HID1], eb1_dram.rearrange("q (x c) -> q x c", x=E1)).then_inc(eb2_in, 16)
            sp.wait_ge(eb2_stored, 48)
            sp.dma_start(eb_v[:, :, HID1:HID1 + P], eb2_dram.rearrange("q (x c) -> q x c", x=E1)).then_inc(eb2_in, 16)
            expert_tiles(1, "experts1")
            for s_ in conv_stored:
                sp.wait_ge(s_, 16 * UNITS // 2 * ITERS)
            barrier(sp, "experts1")

            def load_shared(k, i):
                sp.dma_start(outs[k].sh, shared_rows[bass.ds(batch("output", k, i), 1)].rearrange("a h p c -> p (a h) c")
                             ).then_inc(shared_rows_in[k], 16)

            def store_out(k, i):
                sp.wait_ge(dve_done[k], dve.at("output", "h5", k, i))
                b = batch("output", k, i)
                ob = out[bass.ds(b, 1)].rearrange("a t d -> (a t) d")
                hb = H[:, batch_tiles(b), :]
                sp.dma_start(ob[0:5 * P].rearrange("(j p) d -> p j d", p=P), hb[:, 0:5, :]).then_inc(out_stored[k], 16)
                sp.dma_start(ob[5 * P:L], hb[0:WIDTH[5], 5, :]).then_inc(out_stored[k], 16)

            for k in range(OUT_LANES):
                load_shared(k, 0)
            with sp.Fori(0, OUT_ITERS - 1) as i:
                for k in range(OUT_LANES):
                    store_out(k, i)
                    load_shared(k, i + 1)
            for k in range(OUT_LANES):
                store_out(k, OUT_ITERS - 1)
            for k in range(OUT_LANES):
                sp.wait_ge(out_stored[k], 32 * OUT_ITERS)

        @block.tensor
        def _(e):
            mm = nc.tensor.matmul
            for done in pe_done:
                e.sem_inc(done, Steps.CREDIT)
            e.sem_inc(pe_conv_done, Steps.CREDIT)
            e.wait_ge(inputs_in, 32)

            def transposes(v, src, widths, P_=None):
                for j in range(TILES):
                    c0 = sum(widths[:j % 3]) if j < 3 else sum(widths[3:j])
                    r = nc.tensor.transpose((P_ or v.P)[:, j // 3, c0:c0 + widths[j]], src(j), ident[0:widths[j], 0:widths[j]])
                return r

            TOKW = [TOK_ROWS] * TILES

            def mixer_compress(k, i):
                v = lanes[k]
                e.wait_ge(x_in[k], i * 16 + 16)
                e.wait_ge(act_done[k], act.at("mixer", "n4T", k, i - 1))
                for h in range(2):
                    r = mm(v.P[:, h, 0:HALF_T], w("compress"), v.xT[:, h * HALF_T:(h + 1) * HALF_T], start=True, stop=True)
                r.then_inc(pe_done[k], pe.step("mixer", "compress", k))

            def mixer_main(k, i):
                v = lanes[k]
                e.wait_ge(act_done[k], act.at("mixer", "h1", k, i))
                for h in range(2):
                    c = h * HALF_T
                    mm(v.P[0:64, h, 0:HALF_T], w("main01"), v.h1[:, c:c + HALF_T], start=True, stop=False)
                    r = mm(v.P[0:64, h, 0:HALF_T], w("main2"), v.h1[0:64, c + 2:c + 2 + HALF_T], start=False, stop=True)
                r.then_inc(pe_done[k], pe.step("mixer", "main", k))

            def mixer_r1(k, i):
                v = lanes[k]
                e.wait_ge(act_done[k], act.at("mixer", "h2", k, i))
                e.wait_ge(dve_done[k], dve.at("mixer", "scores", k, i - 1))
                for j in range(TILES):
                    c = slice(j * TOK_ROWS, (j + 1) * TOK_ROWS)
                    mm(v.TK[0:TOK_ROWS, j, :], v.h2[0:65, c], w("expand"), start=True, stop=False)
                    r = mm(v.TK[0:TOK_ROWS, j, :], v.xT[:, c], ident, start=False, stop=True)
                r.then_inc(pe_done[k], pe.step("mixer", "r1", k))

            def norm_T(step, norm_step, widths, phase="mixer"):
                def f(k, i):
                    v = lanes[k]
                    e.wait_ge(dve_done[k], dve.at(phase, norm_step, k, i))
                    r = transposes(v, lambda j: v.norm[0:widths[j], j, :], widths)
                    r.then_inc(pe_done[k], pe.step(phase, step, k))
                return f

            def mixer_ff1(k, i):
                v = lanes[k]
                e.wait_ge(act_done[k], act.at("mixer", "y1T", k, i))
                for h in range(2):
                    r = mm(v.P[0:64, h, 0:HALF_T], w("ff1"), v.y1T[:, h * HALF_T:(h + 1) * HALF_T], start=True, stop=True)
                r.then_inc(pe_done[k], pe.step("mixer", "ff1", k))

            def mixer_r2(k, i):
                v = lanes[k]
                e.wait_ge(act_done[k], act.at("mixer", "ff", k, i))
                for j in range(TILES):
                    c = slice(j * TOK_ROWS, (j + 1) * TOK_ROWS)
                    mm(v.TK[0:TOK_ROWS, j, :], v.h2[0:65, c], w("ff2"), start=True, stop=False)
                    r = mm(v.TK[0:TOK_ROWS, j, :], v.y1T[:, c], ident, start=False, stop=True)
                r.then_inc(pe_done[k], pe.step("mixer", "r2", k))

            def mixer_h1tok(k, i):
                v = lanes[k]
                e.wait_ge(dve_done[k], dve.at("mixer", "pool", k, i))
                for j in range(TILES):
                    r = nc.tensor.transpose(v.TK[0:WIDTH[j], j, :], v.y2T[:, j * P:j * P + WIDTH[j]], ident)
                r.then_inc(pe_done[k], pe.step("mixer", "h1tok", k))

            def mixer_Wg(k, i):
                v = lanes[k]
                e.wait_ge(act_done[k], act.at("mixer", "n1T", k, i))
                for h, (c0, c1) in enumerate(SPAN):
                    r = mm(v.P[:, h, 0:c1 - c0], w("Wg"), v.nT[:, c0:c1], start=True, stop=True)
                r.then_inc(pe_done[k], pe.step("mixer", "Wg", k))

            def mixer_xB(k, i):
                v = lanes[k]
                for h, (c0, c1) in enumerate(SPAN):
                    r = mm(v.TKf[:, h, 0:c1 - c0], w("Bm"), v.nT[:, c0:c1], start=True, stop=True)
                r.then_inc(pe_done[k], pe.step("mixer", "xB", k))

            def mixer_y(k, i):
                v = lanes[k]
                e.wait_ge(rows_in_sb, 16)
                e.wait_ge(dve_done[k], dve.at("mixer", "scan", k, i))
                for j in range(TILES):
                    n = WIDTH[j]
                    c = slice(j * P, j * P + n)
                    mm(v.TK[0:n, j, :], v.hs[:, c], w("C"), start=True, stop=False)
                    mm(v.TK[0:n, j, :], v.nT[:, c], w("D"), start=False, stop=False)
                    r = add_bias(v.TK[0:n, j, :], "bias_y", n)
                r.then_inc(pe_done[k], pe.step("mixer", "y", k))

            def mixer_scores(k, i):
                v = lanes[k]
                e.wait_ge(act_done[k], act.at("mixer", "n4T", k, i))
                for j in range(TILES):
                    r = mm(v.TK[0:WIDTH[j], j, 0:E0], v.nT[:, j * P:j * P + WIDTH[j]], w("gate"), start=True, stop=True)
                r.then_inc(pe_done[k], pe.step("mixer", "scores", k))

            with e.Fori(0, ITERS) as i:
                for f in (mixer_compress, mixer_main, mixer_r1, norm_T("norm1T", "norm1", TOKW), mixer_ff1, mixer_r2,
                          norm_T("norm2T", "norm2", TOKW), mixer_h1tok, norm_T("norm3T", "norm3", WIDTH),
                          mixer_Wg, mixer_xB, mixer_y,
                          norm_T("norm4T", "norm4", WIDTH),
                          mixer_scores):
                    for k in range(LANES):
                        f(k, i)

            def route(phase, ne):
                e.wait_ge(dve_done[0], dve.at(phase, "onehot", 0, 0))
                both = route_buf(4, ne).rearrange("p t e -> p (t e)")
                mm(psum[:, 0, 0:NTILE * ne], w("earlier"), both, start=True, stop=True)
                r = mm(psum[:, 1, 0:NTILE * ne], w("ones"), both, start=True, stop=True)
                r.then_inc(pe_done[0], pe.step(phase, "counts", 0))

            def expert_tiles(m, phase):
                hid = (HID0, HID1)[m]
                nh = hid // P
                weights = (wreg, work)[m]

                stride = (STRIDE0, STRIDE1)[m]
                regs = [e.alloc_register(f"{phase}_expert{t}") for t in range(SLOTS + 2)]
                which = {}

                def load(u, i, t):
                    e.reg_load(regs[t], tile_expert[0:1, bass.ds(i * SLOTS + u, 1)])
                    which[t] = e.snap(regs[t], min_val=0, max_val=stride * ((E0, E1)[m] - 1))

                def begin():
                    for t in range(2):
                        which[t] = e.snap(regs[t], min_val=0, max_val=stride * ((E0, E1)[m] - 1))

                def end():
                    for t in range(2):
                        e.reg_mov(regs[t], regs[SLOTS + t])

                def xT(u, i, t):
                    v = slots[u]
                    e.wait_ge(row_in[u], i * 16 + (16 + m * 16 * EITERS))
                    nc.tensor.transpose(v.psx, v.x, ident).then_inc(pe_done[u], pe.step(phase, "xT", u))

                def up(u, i, t):
                    v = slots[u]
                    e.wait_ge(dve_done[u], dve.at(phase, "xT", u, i))
                    if m == 0:
                        r = mm(v.ps1, v.xT, wreg[:, bass.ds(which[t], 512)], start=True, stop=True)
                    else:
                        mm(v.ps1, v.xT, work[:, bass.ds(which[t], 512)], start=True, stop=False)
                        r = mm(v.ps1, ones3[:], eb[:, bass.ds(which[t], 512)], start=False, stop=True)
                    r.then_inc(pe_done[u], pe.step(phase, "up", u))

                def uT(u, i, t):
                    v = slots[u]
                    e.wait_ge(dve_done[u], dve.at(phase, "u", u, i))
                    for c in range(nh):
                        r = nc.tensor.transpose(v.ps1[:, c * P:(c + 1) * P], v.e[:, c * P:(c + 1) * P], ident)
                    r.then_inc(pe_done[u], pe.step(phase, "uT", u))

                def down(u, i, t):
                    v = slots[u]
                    e.wait_ge(act_done[u], act.at(phase, "uT", u, i))
                    for c in range(nh):
                        r = mm(v.psy, v.uT[:, c * P:(c + 1) * P],
                               weights[:, bass.ds(which[t] + (512 + c * P), P)], start=(c == 0), stop=(m == 0 and c == nh - 1))
                    if m == 1:
                        r = mm(v.psy, ones3[:], eb[:, bass.ds(which[t] + HID1, P)], start=False, stop=True)
                    r.then_inc(pe_done[u], pe.step(phase, "down", u))

                turns(e, [("xT", xT), ("load", load), ("up", up), ("uT", uT), ("down", down)], begin, end)

            route("route0", E0)
            e.wait_ge(dve_done[0], dve.at("route0", "done", 0, 0))

            e.wait_ge(shared_in, 48)

            def shared_up(m, h):
                def f(k, i):
                    v = lanes[k]
                    nt = NT[:, bass.ds(i * LANES + k, 1), :]
                    c0, c1 = SPAN[h]
                    n = c1 - c0
                    if (m, h) == (0, 0):
                        e.wait_ge(dve_done[k], dve.at("shared0", "u1_1", k, i - 1))
                    elif h == 0:
                        e.wait_ge(dve_done[k], dve.at("shared0", "u0_1", k, i))
                    else:
                        e.wait_ge(dve_done[k], dve.at("shared0", f"u{m}_0", k, i))
                    mm(v.P[:, 0, 0:n], sw13[:, m * P:(m + 1) * P], nt[:, 0, PAD + c0:PAD + c1], start=True, stop=True)
                    r = mm(v.P[:, 1, 0:n], sw13[:, 256 + m * P:256 + (m + 1) * P], nt[:, 0, PAD + c0:PAD + c1], start=True, stop=True)
                    r.then_inc(pe_done[k], pe.step("shared0", f"up{m}_{h}", k))
                return f

            def shared_down(k, i):
                v = lanes[k]
                e.wait_ge(dve_done[k], dve.at("shared0", "u1_1", k, i))
                e.wait_ge(dve_done[k], dve.at("shared0", "h", k, i - 1))
                for j in range(TILES):
                    n = WIDTH[j]
                    for m in range(2):
                        r = mm(v.TK[0:n, j, :], v.QK[m][:, j * P:j * P + n], sw2[:, m * P:(m + 1) * P],
                               start=(m == 0), stop=(m == 1))
                r.then_inc(pe_done[k], pe.step("shared0", "down", k))

            with e.Fori(0, ITERS) as i:
                for m in range(2):
                    for h in range(2):
                        for k in range(LANES):
                            shared_up(m, h)(k, i)
                for k in range(LANES):
                    shared_down(k, i)
            barrier(e, "shared0")
            expert_tiles(0, "experts0")

            def att_norm_T(step, norm_step):
                def f(k, i):
                    v = lanes[k]
                    e.wait_ge(dve_done[k], dve.at("attention", norm_step, k, i))
                    r = transposes(v, lambda j: v.norm[0:WIDTH[j], j, :], WIDTH, v.AB)
                    r.then_inc(pe_done[k], pe.step("attention", step, k))
                return f

            def qk(n):
                def f(k, i):
                    v = lanes[k]
                    name = ("q0", "q1", "k0", "k1")[n]
                    e.wait_ge(act_done[k], act.at("attention", ("n5T", "q0", "q1", "k0")[n], k, i))
                    for h, (c0, c1) in enumerate(SPAN):
                        r = mm(v.AB[:, h, 0:c1 - c0], w(name), v.nT[:, c0:c1], start=True, stop=True)
                    r.then_inc(pe_done[k], pe.step("attention", name, k))
                return f

            def vproj(k, i):
                v = lanes[k]
                e.wait_ge(act_done[k], act.at("attention", "k1", k, i))
                for j in range(TILES):
                    n = WIDTH[j]
                    mm(v.ABt[0:n, j, :], v.nT[:, j * P:j * P + n], w("v"), start=True, stop=False)
                    r = add_bias(v.ABt[0:n, j, :], "b_v", n)
                r.then_inc(pe_done[k], pe.step("attention", "v", k))

            def chunk_scores(c):
                def f(k, i):
                    v = lanes[k]
                    n = WIDTH[c]
                    col = slice(c * P, c * P + n)
                    if c == 0:
                        e.wait_ge(dve_done[k], dve.at("attention", "qb", k, i))
                        e.wait_ge(act_done[k], act.at("attention", "v", k, i))
                        e.wait_ge(dve_done[k], dve.at("attention", "scores", k, i - 1))
                    else:
                        e.wait_ge(dve_done[k], dve.at("attention", f"st{c - 1}", k, i))
                    for g in range(2):
                        for r2 in range(2):
                            rows = slice(64 * r2, 64 * r2 + 64)
                            acc = v.AB[0:n, r2, g * 256:g * 256 + 256].rearrange("p (s i) -> p s i", s=2)
                            mm(acc[:, :, 0:n], v.QK[2 + g][rows, col], v.QB[rows, g, :, 0:n], start=True, stop=True)
                    for g in range(2):
                        r = nc.tensor.transpose(v.C[0:n, g * P:(g + 1) * P], v.QK[2 + g][:, col], ident)
                    r.then_inc(pe_done[k], pe.step("attention", f"sc{c}", k))
                return f

            def chunk_context(c):
                def f(k, i):
                    v = lanes[k]
                    n = WIDTH[c]
                    col = slice(c * P, c * P + n)
                    e.wait_ge(dve_done[k], dve.at("attention", f"at{c}", k, i))
                    e.wait_ge(act_done[k], act.at("attention", f"kt{c}", k, i))
                    ctxp = v.C[0:n, 256:392]
                    for g in range(2):
                        mm(ctxp[:, g * 68:(g + 1) * 68], v.QK[g][:, col], v.state[:, g * 68:(g + 1) * 68],
                           start=(g == 0), stop=False, skip_group_check=True)
                    for h in range(HEADS):
                        g, r2, s2 = h // 4, h // 2 % 2, h % 2
                        r = mm(ctxp[:, h * 17:(h + 1) * 17], v.AT2[0:n, 4 * r2 + 2 * g + s2, 0:n], v.V[0:n, c, h, :],
                               start=False, stop=(h == HEADS - 1), skip_group_check=True)
                    if c < TILES - 1:
                        for g in range(2):
                            r = mm(v.AB[:, 0, g * 68:(g + 1) * 68], v.ktok[0:n, g * P:(g + 1) * P],
                                   v.V[0:n, c, 4 * g:4 * g + 4, :].rearrange("p h e -> p (h e)"), start=True, stop=True)
                    r.then_inc(pe_done[k], pe.step("attention", f"cx{c}", k))
                return f

            def attn_out(k, i):
                v = lanes[k]
                e.wait_ge(act_done[k], act.at("attention", "oT", k, i))
                for j in range(TILES):
                    n = WIDTH[j]
                    mm(v.ABt[0:n, j, :], v.oT[:, j * P:j * P + n], w("out"), start=True, stop=False)
                    r = add_bias(v.ABt[0:n, j, :], "b_out", n)
                r.then_inc(pe_done[k], pe.step("attention", "out", k))

            def rc1(k, i):
                v = lanes[k]
                e.wait_ge(act_done[k], act.at("attention", "n6T", k, i))
                nt = NT[:, bass.ds(i * LANES + k, 1), :]
                for h, (c0, c1) in enumerate(SPAN):
                    for t in range(3):
                        r = mm(v.AB[:, h, 0:c1 - c0], w("rc1", (t * P, t * P + P)),
                               nt[:, 0, PAD - 1 + t + c0:PAD - 1 + t + c1], start=(t == 0), stop=(t == 2))
                r.then_inc(pe_done[k], pe.step("attention", "rc1", k))

            def rc2(k, i):
                v = lanes[k]
                e.wait_ge(act_done[k], act.at("attention", "rc1", k, i))
                for j in range(TILES):
                    n = WIDTH[j]
                    acc = v.C[0:n, 16 * j:16 * j + E1]
                    for t in range(3):
                        mm(acc, v.rcT[:, j * P + t:j * P + t + n], w("rc2", (t * E1, t * E1 + E1)), start=(t == 0), stop=False)
                    r = add_bias(acc, "b_rc2", n, E1)
                r.then_inc(pe_done[k], pe.step("attention", "scores", k))

            def conv_part(n, i):
                what, q, m, t3 = PARTS[n]
                if what == "taps":
                    if t3 == 0:
                        before = (f"s2_{q - 1}", f"rows{q - 1}", f"s0_{q}", f"s1_{q}")[m]
                        before_i = i
                        if q == 0 and m < 2:
                            before, before_i = (f"s2_{UNITS - 1}", f"rows{UNITS - 1}")[m], i - 1
                        e.wait_ge(act_conv_done, act_conv.at("conv", before, 0, before_i))
                    nt = NT[:, bass.ds(i * LANES + q // 2, 1), :]
                    c0, c1 = SPAN[q % 2]
                    for t in range(3 * t3, 3 * t3 + 3):
                        r = mm(conv_bank[m % 2][:, 0:c1 - c0], conv1[:, t * 512 + m * P:t * 512 + (m + 1) * P],
                               nt[:, 0, t + c0:t + c1], start=(t == 0), stop=(t == KTAPS - 1))
                    if t3 == 2:
                        r.then_inc(pe_conv_done, pe_conv.step("conv", f"c{m}_{q}", 0))
                else:
                    e.wait_ge(act_conv_done, act_conv.at("conv", f"s3_{q}", 0, i))
                    for j in range(3):
                        n_ = WIDTH[3 * (q % 2) + j]
                        acc = conv_bank[1][0:n_, j * P:(j + 1) * P]
                        for m in range(4):
                            mm(acc, conv_h[:, m, j * P:j * P + n_], conv2[:, m * P:(m + 1) * P], start=(m == 0), stop=False)
                        r = add_bias(acc, "b_sh2", n_)
                    r.then_inc(pe_conv_done, pe_conv.step("conv", f"rows{q}", 0))

            att = [att_norm_T("norm5T", "norm5"), qk(0), qk(1), qk(2), qk(3), vproj]
            for c in range(TILES):
                att += [chunk_scores(c), chunk_context(c)]
            att += [att_norm_T("oT", "otok"), attn_out, att_norm_T("norm6T", "norm6"), rc1, rc2]
            assert len(att) == ATT_STEPS

            def attention(i, conv):
                for what, n, k in interleaved(conv):
                    if what == "attention":
                        att[n](k, i)
                    else:
                        conv_part(n, i - 1)

            barrier(e, "experts0")
            e.wait_ge(conv_in, 32)
            attention(0, False)
            with e.Fori(1, ITERS) as i:
                attention(i, True)

            for n in range(12):
                conv_part(n, ITERS - 1)
            route("route1", E1)
            for n in range(12, len(PARTS)):
                conv_part(n, ITERS - 1)
            e.wait_ge(experts1_in, 32)
            barrier(e, "route1")
            ew2_v = ew_1.rearrange("p (x c d) -> p x c d", x=E1, c=8)[:, :, 4:8, :]
            for q, (x0, x1) in enumerate(((0, 4), (4, 8), (8, E1))):
                for c in range(4):
                    r = mm(psum[0:1, 2 + q, 0:(x1 - x0) * P], w("ones")[:, 0:1], ew2_v[:, x0:x1, c, :],
                           start=(c == 0), stop=(c == 3))
            r.then_inc(pe_done[0], pe.step("colsum", "colsum", 0))
            barrier(e, "colsum")
            e.wait_ge(act_conv_done, act_conv.end("conv")[0][1])
            e.wait_ge(eb2_in, 32)
            expert_tiles(1, "experts1")

        @block.scalar
        def _(e):
            A = nc.scalar.activation
            for done in act_done:
                e.sem_inc(done, Steps.CREDIT)
            e.sem_inc(act_conv_done, Steps.CREDIT)
            e.wait_ge(inputs_in, 32)
            e.wait_ge(zero_set, 1)

            def spans(f, n0=None):
                for h, (c0, c1) in enumerate(SPAN):
                    r = f(h, c0, c1)
                return r

            def evac(step, src, dst, after=()):
                def f(k, i):
                    v = lanes[k]
                    e.wait_ge(pe_done[k], pe.at("mixer", src, k, i))
                    dst(v, i, k).then_inc(act_done[k], act.step("mixer", step, k))
                return f

            def h1(v, i, k):
                A(v.h1[0:64, 1:T + 1].rearrange("p (h c) -> p h c", h=2), v.P[0:64, :, 0:HALF_T], ACT.Silu, bias=w("b_compress")[0:64])
                return A(v.h1[64:128, 0:T].rearrange("p (h c) -> p h c", h=2), v.P[64:128, :, 0:HALF_T], ACT.Silu, bias=w("b_compress")[64:128])

            def h2(v, i, k):
                return A(v.h2[0:64, :].rearrange("p (h c) -> p h c", h=2), v.P[0:64, :, 0:HALF_T], ACT.Silu, bias=w("b_main"))

            def y1T(v, i, k):
                return A(v.y1T.rearrange("p (h c) -> p h c", h=2), v.P[:, :, 0:HALF_T], ACT.Identity, bias=w("b_conv"), scale=w("g_conv"))

            def ff(v, i, k):
                return A(v.h2[0:64, :].rearrange("p (h c) -> p h c", h=2), v.P[0:64, :, 0:HALF_T], ACT.Gelu, bias=w("b_ff1"))

            def y2T(v, i, k):
                return A(v.y2T.rearrange("p (h c) -> p h c", h=2), v.P[:, :, 0:HALF_T], ACT.Identity, bias=w("b_ff"), scale=w("g_ff"))

            def h1tok(v, i, k):
                for a, b, n in HP:
                    r = nc.scalar.copy(v.h1tok[0:n, a:b, :], v.TK[0:n, a:b, :])
                return r

            def to_nT(v, i, k):
                return spans(lambda h, c0, c1: nc.scalar.copy(v.nT[:, c0:c1], v.P[:, h, 0:c1 - c0]))

            def g(v, i, k):
                return spans(lambda h, c0, c1: A(v.g[:, c0:c1], v.P[:, h, 0:c1 - c0], ACT.Sigmoid))

            def to_NT(v, i, k):
                nt = NT[:, bass.ds(i * LANES + k, 1), :]
                return spans(lambda h, c0, c1: nc.scalar.copy(nt[:, 0, PAD + c0:PAD + c1], v.P[:, h, 0:c1 - c0]))

            def n4T(v, i, k):
                nb = N[:, batch_tiles(i * LANES + k), :]
                for a, b, n in HP:
                    nc.scalar.copy(nb[0:n, a:b, :], v.norm[0:n, a:b, :])
                to_NT(v, i, k)
                return to_nT(v, i, k)

            with e.Fori(0, ITERS) as i:
                for step, src, f in (("h1", "compress", h1), ("h2", "main", h2), ("y1T", "norm1T", y1T), ("ff", "ff1", ff),
                                     ("y2T", "norm2T", y2T), ("h1tok", "h1tok", h1tok), ("n1T", "norm3T", to_nT),
                                     ("g", "Wg", g), ("n4T", "norm4T", n4T)):
                    for k in range(LANES):
                        if step == "h1tok":
                            e.wait_ge(dve_done[k], dve.at("mixer", "norm3", k, i))
                        if step == "n1T":
                            e.wait_ge(dve_done[k], dve.at("mixer", "pool", k, i))
                        evac(step, src, f)(k, i)

            e.wait_ge(dve_done[0], dve.at("route0", "values", 0, 0))
            A(top_vals, top_vals, ACT.Sigmoid).then_inc(act_done[0], act.step("route0", "sigmoid", 0))

            with e.Fori(0, ITERS) as i:
                for m in range(2):
                    for h, (c0, c1) in enumerate(SPAN):
                        for k in range(LANES):
                            v = lanes[k]
                            e.wait_ge(pe_done[k], pe.at("shared0", f"up{m}_{h}", k, i))
                            A(v.y2T[:, 0:c1 - c0], v.P[:, 0, 0:c1 - c0], ACT.Silu).then_inc(act_done[k], act.step("shared0", f"s{m}_{h}", k))
            barrier(e, "shared0")

            def expert_tiles(m, phase):
                n = (HID0, HID1)[m]

                def silu(u, i, t):
                    v = slots[u]
                    e.wait_ge(pe_done[u], pe.at(phase, "up", u, i))
                    A(v.e[:, 0:HID0], v.ps1[:, 0:HID0], ACT.Silu).then_inc(act_done[u], act.step(phase, "silu", u))

                def exp(u, i, t):
                    v = slots[u]
                    e.wait_ge(pe_done[u], pe.at(phase, "up", u, i))
                    A(v.e, v.ps1, ACT.Exp, bias=minus_one[:]).then_inc(act_done[u], act.step(phase, "exp", u))

                def uT(u, i, t):
                    v = slots[u]
                    e.wait_ge(pe_done[u], pe.at(phase, "uT", u, i))
                    nc.scalar.copy(v.uT[:, 0:n], v.ps1[:, 0:n]).then_inc(act_done[u], act.step(phase, "uT", u))

                turns(e, [("silu", silu) if m == 0 else ("exp", exp), ("uT", uT)])

            expert_tiles(0, "experts0")
            barrier(e, "experts0")

            def attn(step, src, f):
                def g(k, i):
                    v = lanes[k]
                    if step in ("q0", "q1"):
                        e.wait_ge(dve_done[k], dve.at("attention", "h3", k, i))
                    if step == "rc1":
                        e.wait_ge(dve_done[k], dve.at("attention", "h4", k, i))
                    e.wait_ge(pe_done[k], pe.at("attention", src, k, i))
                    f(v, i, k).then_inc(act_done[k], act.step("attention", step, k))
                return g

            def from_AB(dst_of):
                return lambda v, i, k: spans(lambda h, c0, c1: nc.scalar.copy(dst_of(v, i, k)[:, c0:c1], v.AB[:, h, 0:c1 - c0]))

            def relu(n):
                return lambda v, i, k: spans(lambda h, c0, c1: A(v.QK[n][:, c0:c1], v.AB[:, h, 0:c1 - c0], ACT.Relu,
                                                                 bias=w("b_qk", (n, n + 1))))

            def v_rows(v, i, k):
                for a, b, n in HP:
                    for j in range(a, b):
                        r = nc.scalar.copy(v.V[0:n, j, :, 0:DH], v.ABt[0:n, j, :].rearrange("p (h e) -> p h e", e=DH))
                return r

            def keys(c):
                return lambda v, i, k: nc.scalar.copy(v.ktok[0:WIDTH[c], :], v.C[0:WIDTH[c], 0:256])

            def rc1(v, i, k):
                return spans(lambda h, c0, c1: A(v.rcT[:, 1 + c0:1 + c1], v.AB[:, h, 0:c1 - c0], ACT.Gelu, bias=w("b_rc1")))

            def norm_kept(v, i, k):
                nb = N[:, batch_tiles(i * LANES + k), :]
                for a, b, n in HP:
                    nc.scalar.copy(nb[0:n, a:b, :], v.norm[0:n, a:b, :])
                return from_AB(lambda v, i, k: NT[:, bass.ds(i * LANES + k, 1), PAD:PAD + L].rearrange("p a c -> p (a c)"))(v, i, k)

            att = {0: attn("n5T", "norm5T", from_AB(lambda v, i, k: v.nT)), 5: attn("v", "v", v_rows)}
            for n, x in enumerate(("q0", "q1", "k0", "k1")):
                att[1 + n] = attn(x, x, relu(n))
            for c in range(TILES):
                att[6 + 2 * c] = attn(f"kt{c}", f"sc{c}", keys(c))
            after = 6 + 2 * TILES
            att[after] = attn("oT", "oT", from_AB(lambda v, i, k: v.oT))
            att[after + 2] = attn("n6T", "norm6T", norm_kept)
            att[after + 3] = attn("rc1", "rc1", rc1)

            def conv_part(n, i):
                what, q, m, t3 = PARTS[n]
                if what == "taps":
                    if t3 == 2:
                        c0, c1 = SPAN[q % 2]
                        e.wait_ge(pe_conv_done, pe_conv.at("conv", f"c{m}_{q}", 0, i))
                        A(conv_h[:, m, 0:c1 - c0], conv_bank[m % 2][:, 0:c1 - c0], ACT.Silu, bias=w("b_sh1", (m, m + 1))
                          ).then_inc(act_conv_done, act_conv.step("conv", f"s{m}_{q}", 0))
                else:
                    e.wait_ge(pe_conv_done, pe_conv.at("conv", f"rows{q}", 0, i))
                    e.wait_ge(conv_stored[q % 2], i * (16 * UNITS // 2) + 16 * (q // 2))
                    n_ = WIDTH[3 * (q % 2) + 2]
                    nc.scalar.copy(conv_rows[q % 2][:, 0:2 * P], conv_bank[1][:, 0:2 * P])
                    nc.scalar.copy(conv_rows[q % 2][0:n_, 2 * P:3 * P], conv_bank[1][0:n_, 2 * P:3 * P]
                                   ).then_inc(act_conv_done, act_conv.step("conv", f"rows{q}", 0))

            def attention(i, conv):
                for what, n, k in interleaved(conv):
                    if what == "conv":
                        conv_part(n, i - 1)
                    elif n in att:
                        att[n](k, i)

            attention(0, False)
            with e.Fori(1, ITERS) as i:
                attention(i, True)
            for n in range(len(PARTS)):
                conv_part(n, ITERS - 1)

            e.wait_ge(dve_done[0], dve.at("route1", "values", 0, 0))
            A(top_vals[:, 0:NTILE], top_vals[:, 0:NTILE], ACT.Exp).then_inc(act_done[0], act.step("route1", "exp", 0))
            barrier(e, "route1")
            barrier(e, "colsum")
            expert_tiles(1, "experts1")

        @block.vector
        def _(e):
            V = nc.vector
            for done in dve_done:
                e.sem_inc(done, Steps.CREDIT)
            for t in (zeros, NT, S):
                V.memset(t[:], 0.0)
            for v in lanes:
                V.memset(v.h1, 0.0)
                V.memset(v.h2[64:65, :], 1.0)
                V.memset(v.mv[:], 1.0)
            for v in outs:
                V.memset(v.mv[:], 1.0)
            for t in conv_rows:
                V.memset(t[:], 0.0)
            V.memset(minus_one[:], -1.0)
            e.drain().then_inc(zero_set, 1)
            e.wait_ge(inputs_in, 32)
            V.tensor_scalar(a_minus_1[:], w("A"), -1.0, None, ALU.add)
            V.tensor_scalar(eb1_f[:, 0:EB1], eb1_f[:, 0:EB1], 1.0, None, ALU.add)
            V.memset(ones3[:], 1.0)
            for q in range(3):
                e.drain()
                V.tensor_copy(eb1_part[:, q, :], eb1_f[:])
                if q < 2:
                    e.drain()
                    V.tensor_tensor(eb1_f[:], eb1_f[:], eb1_part[:, q, :], ALU.subtract)
            e.drain().then_inc(eb1_split, 1)

            def var(n, phase, src, widths, after=None):
                def f(k, i):
                    v = lane(phase, k)
                    if after:
                        e.wait_ge(pe_done[k], pe.at(phase, after, k, i))
                    s = src(v, i, k)
                    for j in range(TILES):
                        V.bn_stats(v.st[0:widths[j], j, :], s[0:widths[j], j, :])
                    e.drain()
                    for j in range(TILES):
                        V.bn_aggr(v.mv[0:widths[j], j, :], v.st[0:widths[j], j, :])
                    e.drain()
                    V.tensor_scalar(v.ve[:], v.mv[:, :, 1], EPS, None, ALU.add).then_inc(dve_done[k], dve.step(phase, f"var{n}", k))
                return f

            def norm(n, phase, src, widths):
                def f(k, i):
                    v = lane(phase, k)
                    e.wait_ge(pool_done[k], pool.at(phase, f"rstd{n}", k, i))
                    s = src(v, i, k)
                    for j in range(TILES):
                        m = widths[j]
                        r = V.tensor_scalar(v.norm[0:m, j, :], s[0:m, j, :], v.mv[0:m, j, 0:1], v.rstd[0:m, j:j + 1],
                                            ALU.subtract, ALU.mult)
                    r.then_inc(dve_done[k], dve.step(phase, f"norm{n}", k))
                return f

            TOKW = [TOK_ROWS] * TILES

            def TK(v, i, k):
                return v.TK

            def Hb(v, i, k):
                return H[:, batch_tiles(i * LANES + k), :]

            def pooled(k, i):
                v = lanes[k]
                e.wait_ge(act_done[k], act.at("mixer", "y2T", k, i))
                V.tensor_tensor(v.tmp[:, 0:T - 1], v.y2T[:, 0:T - 1], v.y2T[:, 1:T], ALU.max)
                e.drain()
                V.tensor_tensor(v.y2T[:, 0:L], v.tmp[:, 0:L], v.y2T[:, 2:T], ALU.max).then_inc(dve_done[k], dve.step("mixer", "pool", k))

            def decay(k, i):
                v = lanes[k]
                e.wait_ge(act_done[k], act.at("mixer", "g", k, i))
                V.tensor_scalar(v.g, v.g, 0.05, 0.95, ALU.max, ALU.min)
                e.drain()
                V.tensor_scalar(v.a, v.g, a_minus_1[:], 1.0, ALU.mult, ALU.add).then_inc(dve_done[k], dve.step("mixer", "gates", k))

            def drive(k, i):
                v = lanes[k]
                e.wait_ge(pe_done[k], pe.at("mixer", "xB", k, i))
                for h, (c0, c1) in enumerate(SPAN):
                    r = V.scalar_tensor_tensor(v.bc[:, c0:c1], v.TKf[:, h, 0:c1 - c0], w("bias_h"), v.g[:, c0:c1], ALU.add, ALU.mult)
                r.then_inc(dve_done[k], dve.step("mixer", "b", k))

            def scan(k, i):
                v = lanes[k]
                e.drain()
                V.tensor_tensor_scan(v.hs, v.a, v.bc, 0.0, ALU.mult, ALU.add).then_inc(dve_done[k], dve.step("mixer", "scan", k))

            def add_recurrence(k, i):
                v = lanes[k]
                e.wait_ge(pe_done[k], pe.at("mixer", "y", k, i))
                e.wait_ge(act_done[k], act.at("mixer", "h1tok", k, i))
                hb = Hb(v, i, k)
                for a, b, n in HP:
                    V.scalar_tensor_tensor(hb[0:n, a:b, :], v.TK[0:n, a:b, :], P ** -0.5, v.h1tok[0:n, a:b, :], ALU.mult, ALU.add)
                e.drain().then_inc(dve_done[k], dve.step("mixer", "h2", k))

            def keep_scores(phase, ne):
                def f(k, i):
                    v = lanes[k]
                    e.wait_ge(pe_done[k], pe.at(phase, "scores", k, i))
                    sb_ = S[:, batch_tiles(i * LANES + k), :]
                    for a, b, n in HP:
                        src = v.TK if phase == "mixer" else v.C[:, 0:16 * TILES].rearrange("p (j x) -> p j x", x=16)
                        r = V.tensor_copy(sb_[0:n, a:b, 0:ne], src[0:n, a:b, 0:ne])
                    r.then_inc(dve_done[k], dve.step(phase, "scores", k))
                return f

            with e.Fori(0, ITERS) as i:
                for f in (var(1, "mixer", TK, TOKW, "r1"), norm(1, "mixer", TK, TOKW),
                          var(2, "mixer", TK, TOKW, "r2"), norm(2, "mixer", TK, TOKW), pooled,
                          var(3, "mixer", TK, WIDTH, "h1tok"), norm(3, "mixer", TK, WIDTH), decay, drive, scan,
                          add_recurrence, var(4, "mixer", Hb, WIDTH), norm(4, "mixer", Hb, WIDTH),
                          keep_scores("mixer", E0)):
                    for k in range(LANES):
                        f(k, i)

            def over_experts(x, ne):
                return x.unsqueeze(2).broadcast_to([P, NTILE, ne])

            def over_tiles(x, ne):
                return x.unsqueeze(1).broadcast_to([P, NTILE, ne])

            def top2(x, ne, first, second, vals, tag):
                best = route_small(0, NTILE)
                for n, hot in enumerate((first, second)):
                    V.tensor_reduce(vals[n], x, AX.X, ALU.max)
                    e.drain()
                    V.tensor_tensor(tag, x, over_experts(vals[n], ne), ALU.is_equal)
                    e.drain()
                    V.tensor_tensor(tag, tag, over_tiles(w("descend", (E1 - ne, E1)), ne), ALU.mult)
                    e.drain()
                    V.tensor_reduce(best, tag, AX.X, ALU.max)
                    e.drain()
                    V.tensor_tensor(hot, tag, over_experts(best, ne), ALU.is_equal)
                    e.drain()
                    if n == 0:
                        V.scalar_tensor_tensor(x, hot, -3e38, x, ALU.mult, ALU.add)
                        e.drain()

            def route(m, phase):
                ne = (E0, E1)[m]
                x, tag, first, second, both, total, upto, pos, spare = (route_buf(n, ne) for n in range(9))
                vals = [top_vals[:, 0:NTILE], top_vals[:, NTILE:2 * NTILE]]
                barrier(e, ("mixer", "attention")[m])
                scores = S[:, :, 0:ne]
                if m == 0:
                    V.tensor_tensor(x, scores, over_tiles(w("gate_bias"), ne), ALU.add)
                else:
                    V.tensor_copy(x, scores)
                e.drain()
                top2(x, ne, first, second, vals, tag)
                if m == 0:
                    V.tensor_copy(x, scores)
                    e.drain()
                    top2(x, ne, pos, spare, vals, tag)
                for hot in (first, second):
                    V.tensor_tensor(hot, hot, over_experts(w("valid"), ne), ALU.mult)
                e.drain()
                V.tensor_tensor(both, first, second, ALU.add).then_inc(dve_done[0], dve.step(phase, "onehot", 0))
                if m == 1:
                    V.tensor_tensor(vals[0], vals[1], vals[0], ALU.subtract)
                e.drain().then_inc(dve_done[0], dve.step(phase, "values", 0))

                e.wait_ge(pe_done[0], pe.at(phase, "counts", 0, 0))
                V.tensor_copy(total.rearrange("p t e -> p (t e)"), psum[:, 1, 0:NTILE * ne])
                e.drain()
                for x_ in range(ne):
                    V.tensor_tensor_scan(upto[:, :, x_], w("ones")[:, 0:NTILE], total[:, :, x_], 0.0, ALU.mult, ALU.add)
                e.drain()
                V.tensor_tensor(pos, upto, total, ALU.subtract)
                e.drain()
                V.tensor_tensor(pos.rearrange("p t e -> p (t e)"), psum[:, 0, 0:NTILE * ne],
                                pos.rearrange("p t e -> p (t e)"), ALU.add)
                n_rows = w("tile_rows")
                cmp = work[:, 10240:10240 + ne * 47].rearrange("p (e j) -> p e j", j=47)
                tiles_of, tiles_upto, first_slot = (route_small(144 + 16 * q, ne) for q in range(3))
                V.tensor_tensor(cmp, upto[:, NTILE - 1, :].unsqueeze(2).broadcast_to([P, ne, 47]),
                                n_rows.unsqueeze(1).broadcast_to([P, ne, 47]), ALU.is_gt)
                e.drain()
                V.tensor_reduce(tiles_of, cmp, AX.X, ALU.add)
                e.drain()
                V.tensor_tensor_scan(tiles_upto, w("ones")[:, 0:ne], tiles_of, 0.0, ALU.mult, ALU.add)
                e.drain()
                V.tensor_tensor(first_slot, tiles_upto, tiles_of, ALU.subtract)
                e.drain()
                V.scalar_tensor_tensor(pos, over_tiles(first_slot, ne), float(P), pos, ALU.mult, ALU.add)
                e.drain()
                slot_f = route_small(200, NTILE)
                for n, hot in enumerate((first, second)):
                    V.tensor_tensor(tag, hot, pos, ALU.mult)
                    e.drain()
                    V.tensor_reduce(slot_f, tag, AX.X, ALU.add)
                    e.drain()
                    V.tensor_copy(slot_u[:, n, :], slot_f)
                    e.drain()
                e.drain().then_inc(dve_done[0], dve.step(phase, "slots", 0))
                cmp = work[:, 10240:10240 + EXPERT_TILES * ne].rearrange("p (t e) -> p t e", e=ne)
                V.tensor_tensor(cmp, tiles_upto.unsqueeze(1).broadcast_to([P, EXPERT_TILES, ne]),
                                w("tile_id").unsqueeze(2).broadcast_to([P, EXPERT_TILES, ne]), ALU.is_le)
                e.drain()
                which = route_small(256, EXPERT_TILES)
                V.tensor_reduce(which, cmp, AX.X, ALU.add)
                e.drain()
                V.tensor_scalar(tile_expert[:], which, float(ne - 1), float((STRIDE0, STRIDE1)[m]), ALU.min, ALU.mult)
                e.wait_ge(act_done[0], act.at(phase, ("sigmoid", "exp")[m], 0, 0))
                rs = route_small(0, NTILE)
                if m == 0:
                    V.tensor_tensor(rs, vals[0], vals[1], ALU.add)
                    e.drain()
                    V.reciprocal(rs, rs)
                    e.drain()
                    for n in range(2):
                        V.tensor_tensor(gates[:, n, :], vals[n], rs, ALU.mult)
                else:
                    V.tensor_scalar(rs, vals[0], 1.0, None, ALU.add)
                    e.drain()
                    V.reciprocal(gates[:, 0, :], rs)
                    e.drain()
                    V.tensor_tensor(gates[:, 1, :], gates[:, 0, :], vals[0], ALU.mult)
                e.drain().then_inc(dve_done[0], dve.step(phase, "done", 0))

            route(0, "route0")

            with e.Fori(0, ITERS) as i:
                for m in range(2):
                    for h, (c0, c1) in enumerate(SPAN):
                        for k in range(LANES):
                            v = lanes[k]
                            e.wait_ge(act_done[k], act.at("shared0", f"s{m}_{h}", k, i))
                            V.tensor_tensor(v.QK[m][:, c0:c1], v.y2T[:, 0:c1 - c0], v.P[:, 1, 0:c1 - c0], ALU.mult
                            ).then_inc(dve_done[k], dve.step("shared0", f"u{m}_{h}", k))
                for k in range(LANES):
                    v = lanes[k]
                    e.wait_ge(pe_done[k], pe.at("shared0", "down", k, i))
                    hb = Hb(v, i, k)
                    for a, b, n in HP:
                        r = V.tensor_tensor(hb[0:n, a:b, :], v.TK[0:n, a:b, :], hb[0:n, a:b, :], ALU.add)
                    r.then_inc(dve_done[k], dve.step("shared0", "h", k))
            barrier(e, "shared0")

            def expert_tiles(m, phase):
                def xT(u, i, t):
                    v = slots[u]
                    e.wait_ge(pe_done[u], pe.at(phase, "xT", u, i))
                    V.tensor_copy(v.xT, v.psx).then_inc(dve_done[u], dve.step(phase, "xT", u))

                def gated(u, i, t):
                    v = slots[u]
                    e.wait_ge(act_done[u], act.at(phase, "silu", u, i))
                    V.tensor_tensor(v.e[:, 0:HID0], v.e[:, 0:HID0], v.ps1[:, HID0:2 * HID0], ALU.mult
                                    ).then_inc(dve_done[u], dve.step(phase, "u", u))

                def elu(u, i, t):
                    v = slots[u]
                    e.wait_ge(act_done[u], act.at(phase, "exp", u, i))
                    V.scalar_tensor_tensor(v.e, v.e, 1.0, v.ps1, ALU.min, ALU.max
                                           ).then_inc(dve_done[u], dve.step(phase, "u", u))

                def y(u, i, t):
                    v = slots[u]
                    e.wait_ge(pe_done[u], pe.at(phase, "down", u, i))
                    e.wait_ge(row_stored[u], 16 * i + 16 * EITERS * m)
                    V.tensor_copy(v.y, v.psy).then_inc(dve_done[u], dve.step(phase, "y", u))

                turns(e, [("xT", xT), ("u", gated if m == 0 else elu), ("y", y)])

            expert_tiles(0, "experts0")
            barrier(e, "experts0")

            for v in lanes:
                V.memset(v.V, 1.0)
            e.drain()

            def weigh_rows(v, i, k, phase):
                e.wait_ge(gathered[phase][k], 16 * GATHERS * i + 16 * GATHERS)
                V.tensor_copy(v.gk[:], gates[:, :, batch_tiles(batch(phase, k, i))])
                e.drain()
                for j in range(TILES):
                    n = WIDTH[j]
                    V.tensor_scalar(v.Y[0][0:n, j, :], v.Y[0][0:n, j, :], v.gk[0:n, 0, j:j + 1], None, ALU.mult)
                e.drain()
                for j in range(TILES):
                    n = WIDTH[j]
                    V.scalar_tensor_tensor(v.Y[0][0:n, j, :], v.Y[1][0:n, j, :], v.gk[0:n, 1, j:j + 1], v.Y[0][0:n, j, :],
                                           ALU.mult, ALU.add)
                e.drain()

            def add_experts(k, i):
                v = lanes[k]
                weigh_rows(v, i, k, "attention")
                hb = Hb(v, i, k)
                for a, b, n in HP:
                    V.tensor_tensor(hb[0:n, a:b, :], v.Y[0][0:n, a:b, :], hb[0:n, a:b, :], ALU.add)
                V.memset(v.state, 0.0)
                e.drain().then_inc(dve_done[k], dve.step("attention", "h3", k))

            def cos_sin(n):
                def f(k, i):
                    v = lanes[k]
                    name = ("q0", "q1", "k0", "k1")[n]
                    e.wait_ge(act_done[k], act.at("attention", name, k, i))
                    V.tensor_tensor(v.QK[n], v.QK[n], w("cos_sin"), ALU.mult).then_inc(dve_done[k], dve.step("attention", name, k))
                return f

            def spread_queries(v, c):
                n = WIDTH[c]
                return V.tensor_tensor(v.QB[:, :, :, 0:n], v.Q2[:, :, c * P:c * P + n].unsqueeze(2).broadcast_to([P, 2, 2, n]),
                                       w("head_of").unsqueeze(1).unsqueeze(3).broadcast_to([P, 2, 2, n]), ALU.mult)

            def first_queries(k, i):
                v = lanes[k]
                e.drain()
                e.wait_ge(pe_done[k], pe.at("attention", "v", k, i))
                spread_queries(v, 0).then_inc(dve_done[k], dve.step("attention", "qb", k))

            def mask(c):
                def f(k, i):
                    v = lanes[k]
                    n = WIDTH[c]
                    e.wait_ge(pe_done[k], pe.at("attention", f"sc{c}", k, i))
                    r = V.tensor_tensor(v.AT2[0:n, :, 0:n], v.AB.rearrange("p b (x i) -> p (b x) i", i=P)[0:n, :, 0:n],
                                        w("causal")[0:n, 0:n].unsqueeze(1).broadcast_to([n, 8, n]), ALU.mult)
                    r.then_inc(dve_done[k], dve.step("attention", f"at{c}", k))
                    if c < TILES - 1:
                        spread_queries(v, c + 1)
                return f

            def context(c):
                def f(k, i):
                    v = lanes[k]
                    n = WIDTH[c]
                    e.wait_ge(pe_done[k], pe.at("attention", f"cx{c}", k, i))
                    cx = v.C[:, 256:256 + 136].rearrange("p (h e) -> p h e", e=DH + 1)
                    V.tensor_scalar(v.rden[0:n], cx[0:n, :, DH], 1e-6, None, ALU.add)
                    if c < TILES - 1:
                        V.tensor_tensor(v.upd[:], v.AB[:, 0, 0:136], w("block"), ALU.mult)
                    e.drain()
                    V.reciprocal(v.rden[0:n], v.rden[0:n])
                    if c < TILES - 1:
                        V.tensor_tensor(v.state, v.state, v.upd[:], ALU.add)
                    e.drain()
                    V.tensor_tensor(v.norm[0:n, c, :].rearrange("p (h e) -> p h e", e=DH), cx[0:n, :, 0:DH], 
                                    v.rden[0:n].unsqueeze(2).broadcast_to([n, HEADS, DH]), ALU.mult).then_inc(dve_done[k], dve.step("attention", f"st{c}", k))
                return f

            def otok(k, i):
                e.drain().then_inc(dve_done[k], dve.step("attention", "otok", k))

            def add_attention(k, i):
                v = lanes[k]
                e.wait_ge(pe_done[k], pe.at("attention", "out", k, i))
                hb = Hb(v, i, k)
                for a, b, n in HP:
                    V.tensor_tensor(hb[0:n, a:b, :], v.ABt[0:n, a:b, :], hb[0:n, a:b, :], ALU.add)
                V.memset(v.rcT[:, 0:1], 0.0)
                V.memset(v.rcT[:, L + 1:L + 2], 0.0)
                e.drain().then_inc(dve_done[k], dve.step("attention", "h4", k))

            with e.Fori(0, ITERS) as i:
                steps = [add_experts, var(5, "attention", Hb, WIDTH), norm(5, "attention", Hb, WIDTH)]
                steps += [cos_sin(n) for n in range(4)] + [first_queries]
                for c in range(TILES):
                    steps += [mask(c), context(c)]
                steps += [otok, add_attention, var(6, "attention", Hb, WIDTH), norm(6, "attention", Hb, WIDTH),
                          keep_scores("attention", E1)]
                for f in steps:
                    for k in range(LANES):
                        f(k, i)

            route(1, "route1")
            barrier(e, "route1")
            e.wait_ge(pe_done[0], pe.at("colsum", "colsum", 0, 0))
            e.wait_ge(experts1_in, 32)
            for q, (x0, x1) in enumerate(((0, 4), (4, 8), (8, E1))):
                r = V.tensor_tensor(eb2[0:1, x0 * P:x1 * P], eb2[0:1, x0 * P:x1 * P], psum[0:1, 2 + q, 0:(x1 - x0) * P], ALU.subtract)
            r.then_inc(dve_done[0], dve.step("colsum", "bias", 0))
            for q in range(3):
                e.drain()
                if q:
                    e.wait_ge(eb2_stored, 16 * q)
                V.tensor_copy(eb2_part, eb2)
                e.drain().then_inc(eb2_split, 1)
                if q < 2:
                    V.tensor_tensor(eb2, eb2, eb2_part, ALU.subtract)
            expert_tiles(1, "experts1")
            barrier(e, "experts1")

            def z(k, i):
                v = outs[k]
                weigh_rows(v, i, k, "output")
                e.wait_ge(shared_rows_in[k], i * 16 + 16)
                nb = N[:, batch_tiles(batch("output", k, i)), :]
                sh = v.sh.rearrange("p h (j d) -> p (h j) d", d=P)
                for a, b, n in HP:
                    V.tensor_tensor(v.Y[0][0:n, a:b, :], v.Y[0][0:n, a:b, :], sh[0:n, a:b, :], ALU.add)
                e.drain()
                for a, b, n in HP:
                    V.tensor_tensor(v.Y[0][0:n, a:b, :], v.Y[0][0:n, a:b, :], nb[0:n, a:b, :], ALU.add)
                e.drain().then_inc(dve_done[k], dve.step("output", "z", k))

            def Yb(v, i, k):
                return v.Y[0]

            def final(k, i):
                v = outs[k]
                hb = H[:, batch_tiles(batch("output", k, i)), :]
                e.drain()
                for a, b, n in HP:
                    V.tensor_tensor(v.norm[0:n, a:b, :], v.norm[0:n, a:b, :],
                                    w("ln_g")[0:n].unsqueeze(1).broadcast_to([n, b - a, P]), ALU.mult)
                    V.tensor_tensor(hb[0:n, a:b, :], hb[0:n, a:b, :],
                                    w("ln_b")[0:n].unsqueeze(1).broadcast_to([n, b - a, P]), ALU.add)
                e.drain()
                for a, b, n in HP:
                    r = V.tensor_tensor(hb[0:n, a:b, :], hb[0:n, a:b, :], v.norm[0:n, a:b, :], ALU.add)
                r.then_inc(dve_done[k], dve.step("output", "h5", k))

            var7, norm7 = var(7, "output", Yb, WIDTH), norm(7, "output", Yb, WIDTH)
            with e.Fori(0, OUT_ITERS) as i:
                for k in range(OUT_LANES + 1):
                    if k < OUT_LANES:
                        z(k, i)
                        var7(k, i)
                    if k > 0:
                        norm7(k - 1, i)
                        final(k - 1, i)

        @block.gpsimd
        def _(e):
            G = nc.gpsimd
            for done in pool_done:
                e.sem_inc(done, Steps.CREDIT)
            e.wait_ge(inputs_in, 32)

            def rstd(phase, n, k, i):
                e.wait_ge(dve_done[k], dve.at(phase, f"var{n}", k, i))
                v = lane(phase, k)
                G.tensor_tensor(v.rstd[:], v.ve[:], w("minus_half"), ALU.pow).then_inc(pool_done[k], pool.step(phase, f"rstd{n}", k))

            def scatter(m):
                e.wait_ge(rows_zeroed, 32)
                e.wait_ge(dve_done[0], dve.at(("route0", "route1")[m], "slots", 0, 0))
                for t in range(NTILE):
                    n = WIDTH[t % TILES]
                    for q in range(2):
                        G.indirect_dma_start(rows_in[m], bass.IndirectOffsetOnAxis(ap=slot_u[0:n, q, t:t + 1], axis=0),
                                             N[0:n, t, :], None).then_inc(scattered[m], 16)

            def gather(m, phase, k, i):
                v = lane(phase, k)
                G.tensor_copy(v.ix[:], slot_u[:, :, batch_tiles(batch(phase, k, i))])
                e.drain()
                for j in range(TILES):
                    n = WIDTH[j]
                    for q in range(2):
                        G.indirect_dma_start(v.Y[q][0:n, j, :], None, rows_out[m],
                                             bass.IndirectOffsetOnAxis(ap=v.ix[0:n, q, j:j + 1], axis=0)).then_inc(gathered[phase][k], 16)

            with e.Fori(0, ITERS) as i:
                for n in range(1, 5):
                    for k in range(LANES):
                        rstd("mixer", n, k, i)
            def store_rows(m, phase):
                with e.Fori(0, EITERS) as i:
                    for u in range(SLOTS):
                        e.wait_ge(dve_done[u], dve.at(phase, "y", u, i))
                        e.dma_start(rows_out[m].rearrange("(t p) d -> t p d", p=P)[
                            bass.ds(i * SLOTS + u, 1)].rearrange("a p d -> p (a d)"), slots[u].y).then_inc(row_stored[u], 16)

            scatter(0)
            store_rows(0, "experts0")
            for s in row_stored:
                e.wait_ge(s, 16 * EITERS)
            barrier(e, "experts0")
            with e.Fori(0, ITERS) as i:
                for k in range(LANES):
                    e.wait_ge(pe_done[k], pe.at("attention", "cx5", k, i - 1))
                    gather(0, "attention", k, i)
                for n in (5, 6):
                    for k in range(LANES):
                        rstd("attention", n, k, i)
            scatter(1)
            store_rows(1, "experts1")
            for s in row_stored:
                e.wait_ge(s, 32 * EITERS)
            barrier(e, "experts1")
            for k in range(OUT_LANES):
                gather(1, "output", k, 0)
            with e.Fori(0, OUT_ITERS - 1) as i:
                for k in range(OUT_LANES):
                    rstd("output", 7, k, i)
                    e.wait_ge(dve_done[k], dve.at("output", "norm7", k, i))
                    gather(1, "output", k, i + 1)
            for k in range(OUT_LANES):
                rstd("output", 7, k, OUT_ITERS - 1)


def _layout(x):
    f = {k: np.asarray(v) for k, v in x.items()}
    pack = np.zeros((P, PACK_COLS), np.float32)

    def put(name, a, col=0):
        at, rows, n = PACK[name]
        a = np.asarray(a)
        pack[0:a.shape[0], at + col:at + col + a.shape[1]] = a

    wc = f["L0_tok_w_compress"][:, :, 0].T
    put("compress", wc)
    put("compress", wc, 64)
    wm = f["L0_tok_w_main"]
    put("main01", np.concatenate([wm[:, :, 0].T, wm[:, :, 1].T]))
    put("main2", wm[:, :, 2].T)
    put("expand", np.concatenate([f["L0_tok_w_expand"][:, :, 0].T, f["L0_tok_b_expand"][None]]))
    put("ff1", f["L0_tok_w_ff1"].T)
    put("ff2", np.concatenate([f["L0_tok_w_ff2"].T, f["L0_tok_b_ff2"][None]]))
    put("b_compress", np.concatenate([f["L0_tok_b_compress"]] * 2)[:, None])
    for name, src in (("b_main", "L0_tok_b_main"), ("b_ff1", "L0_tok_b_ff1"), ("g_conv", "L0_tok_g_conv_norm"),
                      ("b_conv", "L0_tok_b_conv_norm"), ("g_ff", "L0_tok_g_ff_norm"), ("b_ff", "L0_tok_b_ff_norm"),
                      ("A", "L0_attn_A"), ("bias_h", "L0_attn_bias_h"), ("b_rc1", "L1_ffn_rc_b1")):
        put(name, f[src][:, None])
    for name, src in (("Wg", "L0_attn_Wg"), ("Bm", "L0_attn_B"), ("C", "L0_attn_C"), ("D", "L0_attn_D"), ("gate", "L0_ffn_gate_w")):
        put(name, f[src].T)
    put("gate_bias", np.broadcast_to(f["L0_ffn_biases"], (P, E0)))
    wqkv, bqkv = f["L1_attn_W_qkv"], f["L1_attn_b_qkv"]
    twice = np.concatenate([np.concatenate([np.arange(DH * h, DH * h + DH)] * 2) for h in range(HEADS)])
    for s in range(2):
        for g in range(2):
            cols = s * P + twice[g * P:(g + 1) * P]
            put("qk"[s] + str(g), wqkv[:, cols])
            put("b_qk", bqkv[cols][:, None], 2 * s + g)
    put("v", wqkv[:, 2 * P:])
    put("out", f["L1_attn_W_out"])
    put("rc1", f["L1_ffn_rc_w1"].transpose(1, 2, 0).reshape(P, 3 * P))
    put("rc2", f["L1_ffn_rc_w2"].transpose(1, 2, 0).reshape(P, 3 * E1))
    put("b_sh1", f["L1_ffn_sh_b1"].reshape(4, P).T)
    put("ln_g", np.broadcast_to(f["L1_ffn_ln_g"], (P, P)))
    put("ln_b", np.broadcast_to(f["L1_ffn_ln_b"], (P, P)))
    r = np.arange(P)
    put("ident", np.eye(P, dtype=np.float32))
    put("ones", np.ones((P, P), np.float32))
    put("earlier", (r[:, None] < r[None]).astype(np.float32))
    put("causal", np.tile((r[:, None] <= r[None]).astype(np.float32), (1, 2)))
    angle = (np.float32(np.pi / 2) * np.arange(L, dtype=np.float32) / np.float32(L))[None]
    put("cos_sin", np.where((r // DH % 2 == 0)[:, None], np.cos(angle), np.sin(angle)).astype(np.float32))
    put("head_of", (r[:, None] // 32 % 2 == np.arange(2)[None]).astype(np.float32))
    put("block", np.tile((r[:, None] // 32 == np.arange(68)[None] // 17), (1, 2)).astype(np.float32))
    put("valid", (r[:, None] < np.array(WIDTH * B)[None]).astype(np.float32))
    put("descend", np.broadcast_to(np.arange(E1, 0, -1, dtype=np.float32), (P, E1)))
    put("tile_rows", np.broadcast_to(P * np.arange(47, dtype=np.float32), (P, 47)))
    put("tile_id", np.broadcast_to(np.arange(EXPERT_TILES, dtype=np.float32), (P, EXPERT_TILES)))
    put("minus_half", np.full((P, TILES), -0.5, np.float32))

    def rows(a, hid):
        return a.reshape(-1, hid // P, P, P).transpose(2, 0, 1, 3).reshape(P, -1)

    big = {
        "xT": f["x"].transpose(0, 2, 1),
        "pack": pack,
        "ew_0": np.concatenate([f["L0_ffn_w1"].transpose(1, 0, 2), f["L0_ffn_w3"].transpose(1, 0, 2),
                                rows(f["L0_ffn_w2"], HID0).reshape(P, E0, -1)], 2).reshape(P, -1),
        "sw13": np.concatenate([f["L0_ffn_sw1"], f["L0_ffn_sw3"]], 1),
        "sw2": rows(f["L0_ffn_sw2"][None], HID0),
        "ew_1": np.concatenate([f["L1_ffn_e_w1"].transpose(1, 0, 2), rows(f["L1_ffn_e_w2"], HID1).reshape(P, E1, -1)],
                               2).reshape(P, -1),
        "bias": np.concatenate([f["L1_ffn_e_b1"].reshape(P, -1), np.concatenate([
            f["L0_attn_bias_y"], bqkv[2 * P:], f["L1_attn_b_out"], np.pad(f["L1_ffn_rc_b2"], (0, P - E1)),
            f["L1_ffn_sh_b2"]]).reshape(P, -1)], 1),
        "eb2": f["L1_ffn_e_b2"].reshape(1, -1),
        "conv1": f["L1_ffn_sh_w1"].transpose(1, 2, 0).reshape(P, -1),
        "conv2": rows(f["L1_ffn_sh_w2"][:, :, 0].T[None], HID1),
    }
    return {k: np.ascontiguousarray(v) for k, v in big.items()}


def build(nc, arrays):
    d = {k: nc.dram_tensor(f"in_{k}", a.shape, mybir.dt.from_np(a.dtype), kind="ExternalInput").ap() for k, a in arrays.items()}
    out = nc.dram_tensor("out_0", (B, L, P), F32, kind="ExternalOutput").ap()
    audio_tower(nc, d, out)


def kernel(**inputs):
    import concourse.bacc as bacc
    from concourse.bass_utils import run_bass_kernel_spmd

    arrays = _layout(inputs)
    nc = bacc.Bacc("TRN2", target_bir_lowering=False, num_devices=1)
    build(nc, arrays)
    r = run_bass_kernel_spmd(nc, [{f"in_{k}": a for k, a in arrays.items()}], core_ids=[0])
    return r.results[0]["out_0"]
```

```python
from contextlib import ExitStack

import numpy as np
import concourse.bass as bass
from concourse import mybir

F32 = mybir.dt.float32
U32 = mybir.dt.uint32
BF16 = mybir.dt.bfloat16
I32 = mybir.dt.int32
ALU = mybir.AluOpType
ACT = mybir.ActivationFunctionType
AX = mybir.AxisListType

P = 128
B, T = 8, 750
L = T - 2
HALF_T = T // 2
TOK_ROWS = T // 6
TILES = 6
WIDTH = [min(P, L - P * j) for j in range(TILES)]
SPAN = [(0, 384), (384, L)]
NTILE = B * TILES
PAIRS = 2 * B * L
EXPERT_TILES = 104
E0, HID0 = 8, 256
E1, HID1 = 10, 512
assert (PAIRS + (E1 - 1 + 1) * (P - 1)) // P <= EXPERT_TILES
PAD = 4
NCOL = L + 2 * PAD
HEADS, DH = 8, 16
LANES = 2
ITERS = B // LANES
OUT_LANES = 4
OUT_ITERS = B // OUT_LANES
B_SHARE = 0.7
STRIDE0 = 2 * HID0 + (HID0 // P) * P
STRIDE1 = HID1 + (HID1 // P) * P
SLOTS = 4
EITERS = EXPERT_TILES // SLOTS
KTAPS = 9
EPS = 1e-5

BIAS_ROWS = ["bias_y", "b_v", "b_out", "b_rc2", "b_sh2"]

PACK = {}
PACK_COLS = 0


def _place(name, rows, cols):
    global PACK_COLS
    PACK[name] = (PACK_COLS, rows, cols)
    PACK_COLS += cols


for _n, _r, _c in [
    ("compress", P, P), ("main01", P, 64), ("main2", 64, 64), ("expand", 65, P), ("ff1", P, 64), ("ff2", 65, P),
    ("b_compress", P, 1), ("b_main", 64, 1), ("b_ff1", 64, 1), ("g_conv", P, 1), ("b_conv", P, 1),
    ("g_ff", P, 1), ("b_ff", P, 1), ("A", P, 1), ("bias_h", P, 1),
    ("Wg", P, P), ("Bm", P, P), ("C", P, P), ("D", P, P), ("gate", P, E0), ("gate_bias", P, E0), 
    ("q0", P, P), ("q1", P, P), ("k0", P, P), ("k1", P, P), ("b_qk", P, 4), ("v", P, P),
    ("out", P, P),
    ("rc1", P, 3 * P), ("b_rc1", P, 1), ("rc2", P, 3 * E1), ("b_sh1", P, 4), ("head_of", P, 2),
    ("ln_g", P, P), ("ln_b", P, P),
    ("ident", P, P), ("ones", P, P), ("earlier", P, P), ("causal", P, 2 * P), ("cos_sin", P, L), ("block", P, 136),
    ("valid", P, NTILE), ("descend", P, E1), ("nought", P, 1), ("tile_rows", P, 47), ("tile_id", P, EXPERT_TILES), ("minus_half", P, TILES),
]:
    _place(_n, _r, _c)

AHEAD = {"xT": 3, "load": 2, "up": 2, "silu": 2, "exp": 2, "u": 2, "uT": 1, "down": 0, "y": 0}


def turns(eng, stages, begin=None, end=None):
    def run(i, u, first=False, last=False):
        for name, f in stages:
            t = u + AHEAD[name]
            if first and t < 0 or last and t >= SLOTS:
                continue
            f(t % SLOTS, i + t // SLOTS, t)

    for u in range(-3, 0):
        run(0, u, first=True)
    with eng.Fori(0, EITERS - 1) as i:
        if begin:
            begin()
        for u in range(SLOTS):
            run(i, u)
        if end:
            end()
    if begin:
        begin()
    for u in range(SLOTS):
        run(EITERS - 1, u, last=True)


class Steps:

    CREDIT = 32

    def __init__(self, phases):
        self.phases, self.base, self.next = phases, {}, {}
        at = {}
        for phase, (iters, count, names) in phases.items():
            assert len(names) <= self.CREDIT
            for lane in self.lanes(count):
                self.base[phase, lane] = at.get(lane, self.CREDIT)
                at[lane] = self.base[phase, lane] + iters * len(names)

    @staticmethod
    def lanes(count):
        return count if isinstance(count, tuple) else range(count)

    def step(self, phase, step, lane):
        names = self.phases[phase][2]
        n = self.next.get((phase, lane), 0)
        assert names[n] == step, (phase, lane, step, names[n])
        self.next[phase, lane] = (n + 1) % len(names)
        return 1

    def at(self, phase, step, lane, i):
        names = self.phases[phase][2]
        return i * len(names) + (self.base[phase, lane] + names.index(step) + 1)

    def end(self, phase):
        if phase not in self.phases:
            return []
        iters, count, names = self.phases[phase]
        return [(lane, self.base[phase, lane] + iters * len(names)) for lane in self.lanes(count)]


def audio_tower(nc, d, out):
    with ExitStack() as ctx:
        def sb(name, shape, dt=F32):
            return ctx.enter_context(nc.sbuf_tensor(name, shape, dt))

        def sem(name):
            return ctx.enter_context(nc.semaphore(name))

        rows_in = [nc.dram_tensor(f"rows_in{m}", (EXPERT_TILES * P, P), F32, kind="Internal").ap() for m in range(2)]
        rows_out = [nc.dram_tensor(f"rows_out{m}", (EXPERT_TILES * P, P), F32, kind="Internal").ap() for m in range(2)]

        pack = sb("pack", [P, PACK_COLS])
        H = sb("H", [P, NTILE, P])
        N = sb("N", [P, NTILE, P])
        NT = sb("NT", [P, B, NCOL])
        S = sb("S", [P, NTILE, E1])
        gates = sb("gates", [P, 2, NTILE])
        slot_u = sb("slot_u", [P, 2, NTILE], U32)
        tile_expert = sb("tile_expert", [P, EXPERT_TILES], I32)
        zeros = sb("zeros", [P, P])
        a_minus_1 = sb("a_minus_1", [P, 1])

        def w(name, cols=None):
            at, rows, n = PACK[name]
            lo, hi = cols or (0, n)
            return pack[0:rows, at + lo:at + hi]

        ident = w("ident")

        W_COLS = 7040
        wreg = sb("wreg", [P, W_COLS])
        ew_0 = wreg[:, 0:E0 * STRIDE0]
        sw13 = wreg[:, 6144:6144 + 512]
        sw2 = wreg[:, 6656:6656 + 256]
        conv1 = wreg[:, 0:KTAPS * 512]
        conv2 = wreg[:, 4608:4608 + 512]

        LANE_COLS = 7776
        work = sb("work", [P, LANES * LANE_COLS])
        ew_1 = work[:, 0:E1 * STRIDE1]
        eb = wreg[0:3, 0:E1 * STRIDE1 // 2].bitcast(BF16)
        eb_v = eb.rearrange("q (x c) -> q x c", x=E1)
        ones3 = sb("ones3", [3, P], BF16)
        EB1 = E1 * HID1 // P
        EB = EB1 + len(BIAS_ROWS)
        rows3 = sb("rows3", [3, len(BIAS_ROWS) * P], BF16)
        rows_dram = nc.dram_tensor("bias_rows", (3, len(BIAS_ROWS) * P), BF16, kind="Internal").ap()

        def add_bias(acc, name, n, cols=P):
            at = BIAS_ROWS.index(name) * P
            return nc.tensor.matmul(acc, ones3[:, 0:n], rows3[:, at:at + cols], start=False, stop=True)

        eb1_f = sb("eb1_f", [P, EB])
        eb1_part = sb("eb1_part", [P, 3, EB], BF16)
        eb1_dram = nc.dram_tensor("eb1_parts", (3, E1 * HID1), BF16, kind="Internal").ap()
        eb1_split = sem("eb1_split")
        eb1_stored = sem("eb1_stored")
        eb2_dram = nc.dram_tensor("eb2_parts", (3, E1 * P), BF16, kind="Internal").ap()
        rows_in_sb = sem("bias_rows_in")
        eb2_split = sem("eb2_split")
        eb2_stored = sem("eb2_stored")
        eb2_in = sem("eb2_in")
        eb2 = wreg[0:1, 5120:5120 + E1 * P]
        eb2_part = wreg[0:1, 6400:6400 + E1 * P // 2].bitcast(BF16)

        def view(lane, at, n, rows=P):
            return work[0:rows, lane * LANE_COLS + at:lane * LANE_COLS + at + n]

        class Lane:
            pass

        lanes = []
        for ln in range(LANES):
            v = Lane()
            v.norm = view(ln, 2304, 768).rearrange("p (j d) -> p j d", d=P)
            v.nT = view(ln, 4608, L)
            v.y2T = view(ln, 3840, T)
            v.Y = [view(ln, 768 * k, 768).rearrange("p (j d) -> p j d", d=P) for k in range(2)]
            v.QK = [view(ln, a, L) for a in (0, 768, 3072, 3840)]
            v.oT = view(ln, 4608, L)
            v.V = view(ln, 5376, 816).rearrange("p (j h e) -> p j h e", h=HEADS, e=DH + 1)
            v.ktok = view(ln, 7216, 256)
            v.state = view(ln, 7472, 136)
            v.rden = view(ln, 7608, 8)
            v.rcT = view(ln, 3072, L + 2)
            v.st = sb(f"stats{ln}", [P, TILES, 6])
            v.mv = sb(f"mean_var{ln}", [P, TILES, 2])
            v.ve = sb(f"var_eps{ln}", [P, TILES])
            v.rstd = sb(f"rstd{ln}", [P, TILES])
            v.upd = sb(f"upd{ln}", [P, 136])
            lanes.append(v)

        slots = []
        for u in range(SLOTS):
            v = Lane()
            at = 10240 + u * 1300
            v.x = work[:, at:at + P]
            v.xT = work[:, at + 128:at + 256]
            v.e = work[:, at + 256:at + 768]
            v.uT = work[:, at + 768:at + 1280]
            v.y = sb(f"expert_y{u}", [P, P])[:]
            slots.append(v)
        assert 10240 + SLOTS * 1300 <= LANES * LANE_COLS

        conv_h = sb("conv_h", [P, 4, SPAN[0][1]])
        conv_rows = [sb(f"conv_rows{q}", [P, 3 * P]) for q in range(2)]
        shared_rows = nc.dram_tensor("shared_rows", (B, 2, P, 3 * P), F32, kind="Internal").ap()

        def route_buf(n, ne):
            return work[:, 10240 + 480 * n:10240 + 480 * n + NTILE * ne].rearrange("p (t e) -> p t e", e=ne)

        def route_small(at, n):
            return work[:, 14560 + at:14560 + at + n]

        top_vals = route_small(48, 2 * NTILE)
        for v in lanes:
            v.gk = sb(f"gate_b{lanes.index(v)}", [P, 2, TILES])
            v.ix = sb(f"slot_b{lanes.index(v)}", [P, 2, TILES], U32)
        minus_one = sb("minus_one", [P, 1])

        psum = ctx.enter_context(nc.psum_tensor("psum", [P, 8, 512], F32))
        for ln, v in enumerate(lanes):
            v.P = psum[:, 4 * ln:4 * ln + 2, :]
            v.TK = psum[:, 4 * ln + 2:4 * ln + 4, :].rearrange("p b (j d) -> p (b j) d", d=P)
            v.TKf = psum[:, 4 * ln + 2:4 * ln + 4, :]
            v.AB = psum[:, 3 * ln:3 * ln + 2, :]
            v.ABt = v.AB.rearrange("p b (j d) -> p (b j) d", d=P)
            v.C = psum[:, 3 * ln + 2, :]
            v.QB = view(ln, 4608, 512).rearrange("p (g s i) -> p g s i", g=2, s=2)
            v.Q2 = view(ln, 0, 2 * 768).rearrange("p (g c) -> p g c", g=2)
            v.AT2 = view(ln, 6192, 1024).rearrange("p (x i) -> p x i", i=P)
        outs = []
        for ln in range(OUT_LANES):
            v = Lane()
            at = ln * (LANES * LANE_COLS // OUT_LANES)
            v.Y = [work[:, at + 768 * q:at + 768 * (q + 1)].rearrange("p (j d) -> p j d", d=P) for q in range(2)]
            v.norm = work[:, at + 1536:at + 2304].rearrange("p (j d) -> p j d", d=P)
            v.sh = work[:, at + 2304:at + 3072].rearrange("p (h c) -> p h c", h=2)
            v.st = sb(f"out_stats{ln}", [P, TILES, 6])
            v.mv = sb(f"out_mean_var{ln}", [P, TILES, 2])
            v.ve = sb(f"out_var_eps{ln}", [P, TILES])
            v.rstd = sb(f"out_rstd{ln}", [P, TILES])
            v.gk = sb(f"out_gate_b{ln}", [P, 2, TILES])
            v.ix = sb(f"out_slot_b{ln}", [P, 2, TILES], U32)
            outs.append(v)

        mix = []
        for ln in range(LANES):
            v = Lane()
            v.xT = view(ln, 0, T)
            v.h1 = view(ln, 768, T + 2)
            v.h2 = view(ln, 1536, T)
            v.norm = view(ln, 2304, 768).rearrange("p (j d) -> p j d", d=P)
            v.y2T = view(ln, 2304, T)
            v.y1T = view(ln, 3072, T)
            v.tmp = view(ln, 3072, T)
            v.h1tok = view(ln, 3840, 768).rearrange("p (j d) -> p j d", d=P)
            v.norm3 = view(ln, 4608, 768).rearrange("p (j d) -> p j d", d=P)
            v.st, v.mv, v.ve, v.rstd = lanes[ln].st, lanes[ln].mv, lanes[ln].ve, lanes[ln].rstd
            mix.append(v)
        for ln in range(LANES):
            v = Lane()
            v.h1tok = mix[ln].h1tok
            v.norm = mix[ln].norm3
            v.g = v.hs = view(ln, 4608, L)
            v.a = view(ln, 5376, L)
            v.bc = view(ln, 6144, L)
            v.nT = view(ln, 6912, L)
            o = outs[LANES + ln]
            v.st, v.mv, v.ve, v.rstd = o.st, o.mv, o.ve, o.rstd
            mix.append(v)
        for q, v in enumerate(mix):
            v.P = psum[:, 2 * q:2 * q + 2, :]
            v.TKf = v.P
            v.TK = v.P.rearrange("p b (j d) -> p (b j) d", d=P)

        A_STEPS = ["pe compress", "act h1", "pe main", "act h2", "pe r1", "dve var1", "pool rstd1", "dve norm1", "pe norm1T",
                   "act y1T", "pe ff1", "act ff", "pe r2", "dve var2", "pool rstd2", "dve norm2", "pe norm2T", "act y2T",
                   "dve pool", "pe h1tok", "dve var3", "pool rstd3", "dve norm3", "act h1tok"]
        B_STEPS = ["pe norm3T", "act n1T", "pe Wg", "act g", "dve gates", "pe xB", "dve b", "dve scan", "pe y", "dve h2",
                   "dve var4", "pool rstd4", "dve norm4", "pe norm4T", "act n4T", "pe scores", "dve scores"]

        def mixer(eng, engine, steps):
            order_a = [((n + 0.5) / len(A_STEPS), "mix_a", x) for n, x in enumerate(A_STEPS)]
            order_b = [((n + 0.5) / len(B_STEPS) * B_SHARE, "mix_b", x) for n, x in enumerate(B_STEPS)]

            def run(order, i):
                for _, phase, x in sorted(order):
                    if x.split()[0] == engine:
                        for k in range(LANES):
                            if phase == "mix_a":
                                steps[x.split()[1]](k, i)
                            else:
                                steps[x.split()[1]](LANES + k, i - 1)

            run(order_a, 0)
            with eng.Fori(1, ITERS) as i:
                run(order_a + order_b, i)
            run(order_b, ITERS)

        def lane(phase, k):
            return {"output": outs, "mix_a": mix, "mix_b": mix}.get(phase, lanes)[k]

        def batch(phase, k, i):
            return i * (OUT_LANES if phase == "output" else LANES) + (k % LANES if phase == "mix_b" else k)

        conv_bank = [psum[:, 6 + q, :] for q in range(2)]
        for u, v in enumerate(slots):
            v.ps1 = psum[:, 2 * u, :]
            v.psx = psum[:, 2 * u, 0:P]
            v.psy = psum[:, 2 * u + 1, 0:P]

        def chunk_steps(names):
            return [f"{n}{c}" for c in range(TILES) for n in names]

        pe_done = [sem(f"pe_done{k}") for k in range(4)]
        pe = Steps({
            "mix_a": (ITERS, (0, 1), ["compress", "main", "r1", "norm1T", "ff1", "r2", "norm2T", "h1tok"]),
            "mix_b": (ITERS, (2, 3), ["norm3T", "Wg", "xB", "y", "norm4T", "scores"]),
            "route0": (1, 1, ["counts"]),
            "shared0": (ITERS, LANES, ["up0_0", "up0_1", "up1_0", "up1_1", "down"]),
            "experts0": (EITERS, SLOTS, ["xT", "up", "uT", "down"]),
            "attention": (ITERS, LANES, ["norm5T", "q0", "q1", "k0", "k1", "v"]
                          + chunk_steps(["sc", "cx"]) + ["oT", "out", "norm6T", "rc1", "scores"]),
            "route1": (1, 1, ["counts"]),
            "colsum": (1, 1, ["colsum"]),
            "experts1": (EITERS, SLOTS, ["xT", "up", "uT", "down"]),
        })
        act_done = [sem(f"act_done{k}") for k in range(4)]
        act = Steps({
            "mix_a": (ITERS, (0, 1), ["h1", "h2", "y1T", "ff", "y2T", "h1tok"]),
            "mix_b": (ITERS, (2, 3), ["n1T", "g", "n4T"]),
            "route0": (1, 1, ["sigmoid"]),
            "shared0": (ITERS, LANES, ["s0_0", "s0_1", "s1_0", "s1_1"]),
            "experts0": (EITERS, SLOTS, ["silu", "uT"]),
            "attention": (ITERS, LANES, ["n5T", "q0", "q1", "k0", "k1", "v"] + chunk_steps(["kt"])
                          + ["oT", "n6T", "rc1"]),
            "route1": (1, 1, ["exp"]),
            "experts1": (EITERS, SLOTS, ["exp", "uT"]),
            "output": (OUT_ITERS, OUT_LANES, ["weighed"]),
        })
        dve_done = [sem(f"dve_done{k}") for k in range(4)]
        dve = Steps({
            "mix_a": (ITERS, (0, 1), ["var1", "norm1", "var2", "norm2", "pool", "var3", "norm3"]),
            "mix_b": (ITERS, (2, 3), ["gates", "b", "scan", "h2", "var4", "norm4", "scores"]),
            "route0": (1, 1, ["onehot", "values", "slots", "done"]),
            "shared0": (ITERS, LANES, ["u0_0", "u0_1", "u1_0", "u1_1", "h"]),
            "experts0": (EITERS, SLOTS, ["xT", "u", "y"]),
            "attention": (ITERS, LANES, ["h3", "var5", "norm5", "q0", "q1", "k0", "k1", "qb"]
                          + chunk_steps(["at", "st"]) + ["otok", "h4", "var6", "norm6", "scores"]),
            "route1": (1, 1, ["onehot", "values", "slots", "done"]),
            "colsum": (1, 1, ["bias"]),
            "experts1": (EITERS, SLOTS, ["xT", "u", "y"]),
            "output": (OUT_ITERS, OUT_LANES, ["gates", "z", "var7", "norm7", "h5"]),
        })
        pool_done = [sem(f"pool_done{k}") for k in range(4)]
        pool = Steps({
            "mix_a": (ITERS, (0, 1), ["rstd1", "rstd2", "rstd3"]),
            "mix_b": (ITERS, (2, 3), ["rstd4"]),
            "attention": (ITERS, LANES, ["rstd5", "rstd6"]),
            "output": (OUT_ITERS, OUT_LANES, ["rstd7"]),
        })

        UNITS = 2 * LANES
        pe_conv_done, act_conv_done = sem("pe_conv_done"), sem("act_conv_done")
        pe_conv = Steps({"conv": (ITERS, 1, [f"{x}{q}" for q in range(UNITS) for x in ("c0_", "c1_", "c2_", "c3_", "rows")])})
        act_conv = Steps({"conv": (ITERS, 1, [f"{x}{q}" for q in range(UNITS) for x in ("s0_", "s1_", "s2_", "s3_", "rows")])})
        conv_stored = [sem(f"conv_rows_stored{q}") for q in range(2)]
        shared_rows_in = [sem(f"shared_rows_in{k}") for k in range(OUT_LANES)]
        PARTS = [("taps", q, m, t) for q in range(UNITS) for m in range(4) for t in range(3)]
        for q in range(UNITS):
            PARTS.insert(min(13 * q + 13, len(PARTS)), ("rows", q, 0, 0))
        ATT_STEPS = 6 + 2 * TILES + 5

        WEIGHT = [0, 0, 0, 0, 1, 0] + [1, 1] * TILES + [1, 5, 1, 1, 8]

        def interleaved(conv):
            order, n, reached = [], 0, 0
            for x in range(ATT_STEPS * LANES):
                order.append(("attention", x // LANES, x % LANES))
                reached += WEIGHT[x // LANES]
                while conv and n * sum(WEIGHT) * LANES < reached * len(PARTS) and n < len(PARTS):
                    order.append(("conv", n, 0))
                    n += 1
            return order

        def barrier(eng, phase):
            for lane, value in pe.end(phase):
                eng.wait_ge(pe_done[lane], value)
            for lane, value in act.end(phase):
                eng.wait_ge(act_done[lane], value)
            for lane, value in dve.end(phase):
                eng.wait_ge(dve_done[lane], value)
            for lane, value in pool.end(phase):
                eng.wait_ge(pool_done[lane], value)

        inputs_in = sem("inputs_in")
        shared_in = sem("shared_weights_in")
        zero_set = sem("zeros_set")
        rows_zeroed = sem("rows_zeroed")
        x_in = [sem(f"x_in{k}") for k in range(LANES)]
        scattered = [sem(f"rows_scattered{m}") for m in range(2)]
        row_in = [sem(f"expert_row_in{u}") for u in range(SLOTS)]
        row_stored = [sem(f"expert_row_stored{u}") for u in range(SLOTS)]
        gathered = {"attention": [sem(f"rows_gathered{k}") for k in range(LANES)],
                    "output": [sem(f"out_rows_gathered{k}") for k in range(OUT_LANES)]}
        experts1_in = sem("experts1_in")
        conv_in = sem("conv_in")
        out_stored = [sem(f"out_stored{k}") for k in range(OUT_LANES)]
        SCATTERS = 2 * NTILE
        GATHERS = 2 * TILES

        block = ctx.enter_context(nc.Block())
        HP = [(0, 5, P), (5, 6, WIDTH[5])]

        def batch_tiles(b):
            return bass.ds(b * TILES, TILES)

        @block.sync
        def _(sp):
            sp.dma_start(pack[:], d["pack"]).then_inc(inputs_in, 16)
            sp.dma_start(eb1_f[:], d["bias"]).then_inc(inputs_in, 16)

            def load_x(k, i):
                sp.dma_start(mix[k].xT, d["xT"][bass.ds(i * LANES + k, 1)].rearrange("a p t -> p (a t)")
                             ).then_inc(x_in[k], 16)

            for k in range(LANES):
                load_x(k, 0)
            for name, dst in (("ew_0", ew_0), ("sw13", sw13), ("sw2", sw2)):
                sp.dma_start(dst, d[name]).then_inc(shared_in, 16)
            sp.wait_ge(eb1_split, 1)
            for q in range(3):
                sp.dma_start(eb1_dram[q].rearrange("(p c) -> p c", p=P), eb1_part[:, q, 0:EB1]).then_inc(eb1_stored, 16)
                sp.dma_start(rows_dram[q].rearrange("(p c) -> p c", p=P), eb1_part[:, q, EB1:EB]).then_inc(eb1_stored, 16)
            sp.wait_ge(eb1_stored, 96)
            sp.dma_start(rows3[:], rows_dram).then_inc(rows_in_sb, 16)
            sp.wait_ge(zero_set, 1)
            for m in range(2):
                sp.dma_start(rows_in[m].rearrange("(p r) d -> p r d", p=P),
                             zeros[:].unsqueeze(1).broadcast_to([P, EXPERT_TILES, P])).then_inc(rows_zeroed, 16)
            with sp.Fori(1, ITERS) as i:
                for k in range(LANES):
                    sp.wait_ge(pe_done[k], pe.at("mix_a", "r1", k, i - 1))
                    load_x(k, i)

            def expert_tiles(m, phase):
                sp.wait_ge(scattered[m], 16 * SCATTERS)
                sp.wait_ge(dve_done[0], dve.at(("route0", "route1")[m], "done", 0, 0))
                if m == 1:
                    sp.wait_ge(dve_done[0], dve.at("colsum", "bias", 0, 0))
                with sp.Fori(0, EITERS) as i:
                    for u in range(SLOTS):
                        sp.wait_ge(pe_done[u], pe.at(phase, "xT", u, i - 1))
                        sp.dma_start(slots[u].x, rows_in[m].rearrange("(t p) d -> t p d", p=P)[
                            bass.ds(i * SLOTS + u, 1)].rearrange("a p d -> p (a d)")).then_inc(row_in[u], 16)

            barrier(sp, "shared0")
            expert_tiles(0, "experts0")
            barrier(sp, "experts0")
            for name, dst in (("conv1", conv1), ("conv2", conv2)):
                sp.dma_start(dst, d[name]).then_inc(conv_in, 16)

            def store_conv_rows(i):
                for q in range(UNITS):
                    sp.wait_ge(act_conv_done, act_conv.at("conv", f"rows{q}", 0, i))
                    sp.dma_start(shared_rows[bass.ds(i * LANES + q // 2, 1), q % 2].rearrange("a p c -> (a p) c"),
                                 conv_rows[q % 2][:]).then_inc(conv_stored[q % 2], 16)

            with sp.Fori(0, ITERS - 1) as i:
                store_conv_rows(i)
            barrier(sp, "attention")
            for name, dst in (("ew_1", ew_1), ("eb2", eb2)):
                sp.dma_start(dst, d[name]).then_inc(experts1_in, 16)
            store_conv_rows(ITERS - 1)
            for q in range(3):
                sp.wait_ge(eb2_split, q + 1)
                sp.dma_start(eb2_dram[q:q + 1], eb2_part).then_inc(eb2_stored, 16)
            sp.dma_start(eb_v[:, :, 0:HID1], eb1_dram.rearrange("q (x c) -> q x c", x=E1)).then_inc(eb2_in, 16)
            sp.wait_ge(eb2_stored, 48)
            sp.dma_start(eb_v[:, :, HID1:HID1 + P], eb2_dram.rearrange("q (x c) -> q x c", x=E1)).then_inc(eb2_in, 16)
            expert_tiles(1, "experts1")
            for s_ in conv_stored:
                sp.wait_ge(s_, 16 * UNITS // 2 * ITERS)
            barrier(sp, "experts1")

            def load_shared(k, i):
                sp.dma_start(outs[k].sh, shared_rows[bass.ds(batch("output", k, i), 1)].rearrange("a h p c -> p (a h) c")
                             ).then_inc(shared_rows_in[k], 16)

            def store_out(k, i):
                sp.wait_ge(dve_done[k], dve.at("output", "h5", k, i))
                b = batch("output", k, i)
                ob = out[bass.ds(b, 1)].rearrange("a t d -> (a t) d")
                hb = H[:, batch_tiles(b), :]
                sp.dma_start(ob[0:5 * P].rearrange("(j p) d -> p j d", p=P), hb[:, 0:5, :]).then_inc(out_stored[k], 16)
                sp.dma_start(ob[5 * P:L], hb[0:WIDTH[5], 5, :]).then_inc(out_stored[k], 16)

            for k in range(OUT_LANES):
                load_shared(k, 0)
            with sp.Fori(0, OUT_ITERS - 1) as i:
                for k in range(OUT_LANES):
                    store_out(k, i)
                    load_shared(k, i + 1)
            for k in range(OUT_LANES):
                store_out(k, OUT_ITERS - 1)
            for k in range(OUT_LANES):
                sp.wait_ge(out_stored[k], 32 * OUT_ITERS)

        @block.tensor
        def _(e):
            mm = nc.tensor.matmul
            for done in pe_done:
                e.sem_inc(done, Steps.CREDIT)
            e.sem_inc(pe_conv_done, Steps.CREDIT)
            e.wait_ge(inputs_in, 32)

            def transposes(v, src, widths, acc=None):
                for j in range(TILES):
                    c0 = sum(widths[:j % 3]) if j < 3 else sum(widths[3:j])
                    r = nc.tensor.transpose((acc or v.P)[:, j // 3, c0:c0 + widths[j]], src(j), ident[0:widths[j], 0:widths[j]])
                return r

            TOKW = [TOK_ROWS] * TILES

            def mixer_compress(k, i):
                v = mix[k]
                e.wait_ge(x_in[k], i * 16 + 16)
                e.wait_ge(act_done[k], act.at("mix_a", "h1tok", k, i - 1))
                for h in range(2):
                    r = mm(v.P[:, h, 0:HALF_T], w("compress"), v.xT[:, h * HALF_T:(h + 1) * HALF_T], start=True, stop=True)
                r.then_inc(pe_done[k], pe.step("mix_a", "compress", k))

            def mixer_main(k, i):
                v = mix[k]
                e.wait_ge(act_done[k], act.at("mix_a", "h1", k, i))
                for h in range(2):
                    c = h * HALF_T
                    mm(v.P[0:64, h, 0:HALF_T], w("main01"), v.h1[:, c:c + HALF_T], start=True, stop=False)
                    r = mm(v.P[0:64, h, 0:HALF_T], w("main2"), v.h1[0:64, c + 2:c + 2 + HALF_T], start=False, stop=True)
                r.then_inc(pe_done[k], pe.step("mix_a", "main", k))

            def mixer_r1(k, i):
                v = mix[k]
                e.wait_ge(act_done[k], act.at("mix_a", "h2", k, i))
                for j in range(TILES):
                    c = slice(j * TOK_ROWS, (j + 1) * TOK_ROWS)
                    mm(v.TK[0:TOK_ROWS, j, :], v.h2[0:65, c], w("expand"), start=True, stop=False)
                    r = mm(v.TK[0:TOK_ROWS, j, :], v.xT[:, c], ident, start=False, stop=True)
                r.then_inc(pe_done[k], pe.step("mix_a", "r1", k))

            def norm_T(step, norm_step, widths, phase):
                def f(k, i):
                    v = lane(phase, k)
                    e.wait_ge(dve_done[k], dve.at(phase, norm_step, k, i))
                    r = transposes(v, lambda j: v.norm[0:widths[j], j, :], widths)
                    r.then_inc(pe_done[k], pe.step(phase, step, k))
                return f

            def norm3_T(k, i):
                v = mix[k]
                e.wait_ge(dve_done[k - LANES], dve.at("mix_a", "norm3", k - LANES, i))
                e.wait_ge(dve_done[k], dve.at("mix_b", "scores", k, i - 1))
                r = transposes(v, lambda j: v.norm[0:WIDTH[j], j, :], WIDTH)
                r.then_inc(pe_done[k], pe.step("mix_b", "norm3T", k))

            def mixer_ff1(k, i):
                v = mix[k]
                e.wait_ge(act_done[k], act.at("mix_a", "y1T", k, i))
                for h in range(2):
                    r = mm(v.P[0:64, h, 0:HALF_T], w("ff1"), v.y1T[:, h * HALF_T:(h + 1) * HALF_T], start=True, stop=True)
                r.then_inc(pe_done[k], pe.step("mix_a", "ff1", k))

            def mixer_r2(k, i):
                v = mix[k]
                e.wait_ge(act_done[k], act.at("mix_a", "ff", k, i))
                for j in range(TILES):
                    c = slice(j * TOK_ROWS, (j + 1) * TOK_ROWS)
                    mm(v.TK[0:TOK_ROWS, j, :], v.h2[0:65, c], w("ff2"), start=True, stop=False)
                    r = mm(v.TK[0:TOK_ROWS, j, :], v.y1T[:, c], ident, start=False, stop=True)
                r.then_inc(pe_done[k], pe.step("mix_a", "r2", k))

            def mixer_h1tok(k, i):
                v = mix[k]
                e.wait_ge(dve_done[k], dve.at("mix_a", "pool", k, i))
                for j in range(TILES):
                    r = nc.tensor.transpose(v.TK[0:WIDTH[j], j, :], v.y2T[:, j * P:j * P + WIDTH[j]], ident)
                r.then_inc(pe_done[k], pe.step("mix_a", "h1tok", k))

            def mixer_Wg(k, i):
                v = mix[k]
                e.wait_ge(act_done[k], act.at("mix_b", "n1T", k, i))
                for h, (c0, c1) in enumerate(SPAN):
                    r = mm(v.P[:, h, 0:c1 - c0], w("Wg"), v.nT[:, c0:c1], start=True, stop=True)
                r.then_inc(pe_done[k], pe.step("mix_b", "Wg", k))

            def mixer_xB(k, i):
                v = mix[k]
                e.wait_ge(act_done[k], act.at("mix_b", "g", k, i))
                for h, (c0, c1) in enumerate(SPAN):
                    r = mm(v.TKf[:, h, 0:c1 - c0], w("Bm"), v.nT[:, c0:c1], start=True, stop=True)
                r.then_inc(pe_done[k], pe.step("mix_b", "xB", k))

            def mixer_y(k, i):
                v = mix[k]
                e.wait_ge(rows_in_sb, 16)
                e.wait_ge(dve_done[k], dve.at("mix_b", "scan", k, i))
                for j in range(TILES):
                    n = WIDTH[j]
                    c = slice(j * P, j * P + n)
                    mm(v.TK[0:n, j, :], v.hs[:, c], w("C"), start=True, stop=False)
                    mm(v.TK[0:n, j, :], v.nT[:, c], w("D"), start=False, stop=False)
                    r = add_bias(v.TK[0:n, j, :], "bias_y", n)
                r.then_inc(pe_done[k], pe.step("mix_b", "y", k))

            def mixer_scores(k, i):
                v = mix[k]
                e.wait_ge(act_done[k], act.at("mix_b", "n4T", k, i))
                for j in range(TILES):
                    r = mm(v.TK[0:WIDTH[j], j, 0:E0], v.nT[:, j * P:j * P + WIDTH[j]], w("gate"), start=True, stop=True)
                r.then_inc(pe_done[k], pe.step("mix_b", "scores", k))

            mixer(e, "pe", {
                "compress": mixer_compress, "main": mixer_main, "r1": mixer_r1, "norm1T": norm_T("norm1T", "norm1", TOKW, "mix_a"),
                "ff1": mixer_ff1, "r2": mixer_r2, "norm2T": norm_T("norm2T", "norm2", TOKW, "mix_a"), "h1tok": mixer_h1tok,
                "norm3T": norm3_T, "Wg": mixer_Wg, "xB": mixer_xB, "y": mixer_y,
                "norm4T": norm_T("norm4T", "norm4", WIDTH, "mix_b"), "scores": mixer_scores})

            def route(phase, ne):
                e.wait_ge(dve_done[0], dve.at(phase, "onehot", 0, 0))
                both = route_buf(4, ne).rearrange("p t e -> p (t e)")
                mm(psum[:, 0, 0:NTILE * ne], w("earlier"), both, start=True, stop=True)
                r = mm(psum[:, 1, 0:NTILE * ne], w("ones"), both, start=True, stop=True)
                r.then_inc(pe_done[0], pe.step(phase, "counts", 0))

            def expert_tiles(m, phase):
                hid = (HID0, HID1)[m]
                nh = hid // P
                weights = (wreg, work)[m]

                stride = (STRIDE0, STRIDE1)[m]
                regs = [e.alloc_register(f"{phase}_expert{t}") for t in range(SLOTS + 2)]
                which = {}

                def load(u, i, t):
                    e.reg_load(regs[t], tile_expert[0:1, bass.ds(i * SLOTS + u, 1)])
                    which[t] = e.snap(regs[t], min_val=0, max_val=stride * ((E0, E1)[m] - 1))

                def begin():
                    for t in range(2):
                        which[t] = e.snap(regs[t], min_val=0, max_val=stride * ((E0, E1)[m] - 1))

                def end():
                    for t in range(2):
                        e.reg_mov(regs[t], regs[SLOTS + t])

                def xT(u, i, t):
                    v = slots[u]
                    e.wait_ge(row_in[u], i * 16 + (16 + m * 16 * EITERS))
                    nc.tensor.transpose(v.psx, v.x, ident).then_inc(pe_done[u], pe.step(phase, "xT", u))

                def up(u, i, t):
                    v = slots[u]
                    e.wait_ge(dve_done[u], dve.at(phase, "xT", u, i))
                    if m == 0:
                        r = mm(v.ps1, v.xT, wreg[:, bass.ds(which[t], 512)], start=True, stop=True)
                    else:
                        mm(v.ps1, v.xT, work[:, bass.ds(which[t], 512)], start=True, stop=False)
                        r = mm(v.ps1, ones3[:], eb[:, bass.ds(which[t], 512)], start=False, stop=True)
                    r.then_inc(pe_done[u], pe.step(phase, "up", u))

                def uT(u, i, t):
                    v = slots[u]
                    e.wait_ge(dve_done[u], dve.at(phase, "u", u, i))
                    for c in range(nh):
                        r = nc.tensor.transpose(v.ps1[:, c * P:(c + 1) * P], v.e[:, c * P:(c + 1) * P], ident)
                    r.then_inc(pe_done[u], pe.step(phase, "uT", u))

                def down(u, i, t):
                    v = slots[u]
                    e.wait_ge(act_done[u], act.at(phase, "uT", u, i))
                    for c in range(nh):
                        r = mm(v.psy, v.uT[:, c * P:(c + 1) * P],
                               weights[:, bass.ds(which[t] + (512 + c * P), P)], start=(c == 0), stop=(m == 0 and c == nh - 1))
                    if m == 1:
                        r = mm(v.psy, ones3[:], eb[:, bass.ds(which[t] + HID1, P)], start=False, stop=True)
                    r.then_inc(pe_done[u], pe.step(phase, "down", u))

                turns(e, [("xT", xT), ("load", load), ("up", up), ("uT", uT), ("down", down)], begin, end)

            route("route0", E0)
            e.wait_ge(dve_done[0], dve.at("route0", "done", 0, 0))

            e.wait_ge(shared_in, 48)

            def shared_up(m, h):
                def f(k, i):
                    v = lanes[k]
                    nt = NT[:, bass.ds(i * LANES + k % LANES, 1), :]
                    c0, c1 = SPAN[h]
                    n = c1 - c0
                    if (m, h) == (0, 0):
                        e.wait_ge(dve_done[k], dve.at("shared0", "u1_1", k, i - 1))
                    elif h == 0:
                        e.wait_ge(dve_done[k], dve.at("shared0", "u0_1", k, i))
                    else:
                        e.wait_ge(dve_done[k], dve.at("shared0", f"u{m}_0", k, i))
                    mm(v.P[:, 0, 0:n], sw13[:, m * P:(m + 1) * P], nt[:, 0, PAD + c0:PAD + c1], start=True, stop=True)
                    r = mm(v.P[:, 1, 0:n], sw13[:, 256 + m * P:256 + (m + 1) * P], nt[:, 0, PAD + c0:PAD + c1], start=True, stop=True)
                    r.then_inc(pe_done[k], pe.step("shared0", f"up{m}_{h}", k))
                return f

            def shared_down(k, i):
                v = lanes[k]
                e.wait_ge(dve_done[k], dve.at("shared0", "u1_1", k, i))
                e.wait_ge(dve_done[k], dve.at("shared0", "h", k, i - 1))
                for j in range(TILES):
                    n = WIDTH[j]
                    for m in range(2):
                        r = mm(v.TK[0:n, j, :], v.QK[m][:, j * P:j * P + n], sw2[:, m * P:(m + 1) * P],
                               start=(m == 0), stop=(m == 1))
                r.then_inc(pe_done[k], pe.step("shared0", "down", k))

            with e.Fori(0, ITERS) as i:
                for m in range(2):
                    for h in range(2):
                        for k in range(LANES):
                            shared_up(m, h)(k, i)
                for k in range(LANES):
                    shared_down(k, i)
            barrier(e, "shared0")
            expert_tiles(0, "experts0")

            def att_norm_T(step, norm_step):
                def f(k, i):
                    v = lanes[k]
                    e.wait_ge(dve_done[k], dve.at("attention", norm_step, k, i))
                    r = transposes(v, lambda j: v.norm[0:WIDTH[j], j, :], WIDTH, v.AB)
                    r.then_inc(pe_done[k], pe.step("attention", step, k))
                return f

            def qk(n):
                def f(k, i):
                    v = lanes[k]
                    name = ("q0", "q1", "k0", "k1")[n]
                    e.wait_ge(act_done[k], act.at("attention", ("n5T", "q0", "q1", "k0")[n], k, i))
                    for h, (c0, c1) in enumerate(SPAN):
                        r = mm(v.AB[:, h, 0:c1 - c0], w(name), v.nT[:, c0:c1], start=True, stop=True)
                    r.then_inc(pe_done[k], pe.step("attention", name, k))
                return f

            def vproj(k, i):
                v = lanes[k]
                e.wait_ge(act_done[k], act.at("attention", "k1", k, i))
                for j in range(TILES):
                    n = WIDTH[j]
                    mm(v.ABt[0:n, j, :], v.nT[:, j * P:j * P + n], w("v"), start=True, stop=False)
                    r = add_bias(v.ABt[0:n, j, :], "b_v", n)
                r.then_inc(pe_done[k], pe.step("attention", "v", k))

            def chunk_scores(c):
                def f(k, i):
                    v = lanes[k]
                    n = WIDTH[c]
                    col = slice(c * P, c * P + n)
                    if c == 0:
                        e.wait_ge(dve_done[k], dve.at("attention", "qb", k, i))
                        e.wait_ge(act_done[k], act.at("attention", "v", k, i))
                        e.wait_ge(dve_done[k], dve.at("attention", "scores", k, i - 1))
                    else:
                        e.wait_ge(dve_done[k], dve.at("attention", f"st{c - 1}", k, i))
                    for g in range(2):
                        for r2 in range(2):
                            rows = slice(64 * r2, 64 * r2 + 64)
                            acc = v.AB[0:n, r2, g * 256:g * 256 + 256].rearrange("p (s i) -> p s i", s=2)
                            mm(acc[:, :, 0:n], v.QK[2 + g][rows, col], v.QB[rows, g, :, 0:n], start=True, stop=True)
                    for g in range(2):
                        r = nc.tensor.transpose(v.C[0:n, g * P:(g + 1) * P], v.QK[2 + g][:, col], ident)
                    r.then_inc(pe_done[k], pe.step("attention", f"sc{c}", k))
                return f

            def chunk_context(c):
                def f(k, i):
                    v = lanes[k]
                    n = WIDTH[c]
                    col = slice(c * P, c * P + n)
                    e.wait_ge(dve_done[k], dve.at("attention", f"at{c}", k, i))
                    e.wait_ge(act_done[k], act.at("attention", f"kt{c}", k, i))
                    ctxp = v.C[0:n, 256:392]
                    for g in range(2):
                        mm(ctxp[:, g * 68:(g + 1) * 68], v.QK[g][:, col], v.state[:, g * 68:(g + 1) * 68],
                           start=(g == 0), stop=False, skip_group_check=True)
                    for h in range(HEADS):
                        g, r2, s2 = h // 4, h // 2 % 2, h % 2
                        r = mm(ctxp[:, h * 17:(h + 1) * 17], v.AT2[0:n, 4 * r2 + 2 * g + s2, 0:n], v.V[0:n, c, h, :],
                               start=False, stop=(h == HEADS - 1), skip_group_check=True)
                    if c < TILES - 1:
                        for g in range(2):
                            r = mm(v.AB[:, 0, g * 68:(g + 1) * 68], v.ktok[0:n, g * P:(g + 1) * P],
                                   v.V[0:n, c, 4 * g:4 * g + 4, :].rearrange("p h e -> p (h e)"), start=True, stop=True)
                    r.then_inc(pe_done[k], pe.step("attention", f"cx{c}", k))
                return f

            def attn_out(k, i):
                v = lanes[k]
                e.wait_ge(act_done[k], act.at("attention", "oT", k, i))
                for j in range(TILES):
                    n = WIDTH[j]
                    mm(v.ABt[0:n, j, :], v.oT[:, j * P:j * P + n], w("out"), start=True, stop=False)
                    r = add_bias(v.ABt[0:n, j, :], "b_out", n)
                r.then_inc(pe_done[k], pe.step("attention", "out", k))

            def rc1(k, i):
                v = lanes[k]
                e.wait_ge(act_done[k], act.at("attention", "n6T", k, i))
                nt = NT[:, bass.ds(i * LANES + k % LANES, 1), :]
                for h, (c0, c1) in enumerate(SPAN):
                    for t in range(3):
                        r = mm(v.AB[:, h, 0:c1 - c0], w("rc1", (t * P, t * P + P)),
                               nt[:, 0, PAD - 1 + t + c0:PAD - 1 + t + c1], start=(t == 0), stop=(t == 2))
                r.then_inc(pe_done[k], pe.step("attention", "rc1", k))

            def rc2(k, i):
                v = lanes[k]
                e.wait_ge(act_done[k], act.at("attention", "rc1", k, i))
                for j in range(TILES):
                    n = WIDTH[j]
                    acc = v.C[0:n, 16 * j:16 * j + E1]
                    for t in range(3):
                        mm(acc, v.rcT[:, j * P + t:j * P + t + n], w("rc2", (t * E1, t * E1 + E1)), start=(t == 0), stop=False)
                    r = add_bias(acc, "b_rc2", n, E1)
                r.then_inc(pe_done[k], pe.step("attention", "scores", k))

            def conv_part(n, i):
                what, q, m, t3 = PARTS[n]
                if what == "taps":
                    if t3 == 0:
                        before = (f"s2_{q - 1}", f"rows{q - 1}", f"s0_{q}", f"s1_{q}")[m]
                        before_i = i
                        if q == 0 and m < 2:
                            before, before_i = (f"s2_{UNITS - 1}", f"rows{UNITS - 1}")[m], i - 1
                        e.wait_ge(act_conv_done, act_conv.at("conv", before, 0, before_i))
                    nt = NT[:, bass.ds(i * LANES + q // 2, 1), :]
                    c0, c1 = SPAN[q % 2]
                    for t in range(3 * t3, 3 * t3 + 3):
                        r = mm(conv_bank[m % 2][:, 0:c1 - c0], conv1[:, t * 512 + m * P:t * 512 + (m + 1) * P],
                               nt[:, 0, t + c0:t + c1], start=(t == 0), stop=(t == KTAPS - 1))
                    if t3 == 2:
                        r.then_inc(pe_conv_done, pe_conv.step("conv", f"c{m}_{q}", 0))
                else:
                    e.wait_ge(act_conv_done, act_conv.at("conv", f"s3_{q}", 0, i))
                    for j in range(3):
                        n_ = WIDTH[3 * (q % 2) + j]
                        acc = conv_bank[1][0:n_, j * P:(j + 1) * P]
                        for m in range(4):
                            mm(acc, conv_h[:, m, j * P:j * P + n_], conv2[:, m * P:(m + 1) * P], start=(m == 0), stop=False)
                        r = add_bias(acc, "b_sh2", n_)
                    r.then_inc(pe_conv_done, pe_conv.step("conv", f"rows{q}", 0))

            att = [att_norm_T("norm5T", "norm5"), qk(0), qk(1), qk(2), qk(3), vproj]
            for c in range(TILES):
                att += [chunk_scores(c), chunk_context(c)]
            att += [att_norm_T("oT", "otok"), attn_out, att_norm_T("norm6T", "norm6"), rc1, rc2]
            assert len(att) == ATT_STEPS

            def attention(i, conv):
                for what, n, k in interleaved(conv):
                    if what == "attention":
                        att[n](k, i)
                    else:
                        conv_part(n, i - 1)

            barrier(e, "experts0")
            e.wait_ge(conv_in, 32)
            attention(0, False)
            with e.Fori(1, ITERS) as i:
                attention(i, True)

            for n in range(12):
                conv_part(n, ITERS - 1)
            route("route1", E1)
            for n in range(12, len(PARTS)):
                conv_part(n, ITERS - 1)
            e.wait_ge(experts1_in, 32)
            barrier(e, "route1")
            ew2_v = ew_1.rearrange("p (x c d) -> p x c d", x=E1, c=8)[:, :, 4:8, :]
            for q, (x0, x1) in enumerate(((0, 4), (4, 8), (8, E1))):
                for c in range(4):
                    r = mm(psum[0:1, 2 + q, 0:(x1 - x0) * P], w("ones")[:, 0:1], ew2_v[:, x0:x1, c, :],
                           start=(c == 0), stop=(c == 3))
            r.then_inc(pe_done[0], pe.step("colsum", "colsum", 0))
            barrier(e, "colsum")
            e.wait_ge(act_conv_done, act_conv.end("conv")[0][1])
            e.wait_ge(eb2_in, 32)
            expert_tiles(1, "experts1")

        @block.scalar
        def _(e):
            A = nc.scalar.activation
            for done in act_done:
                e.sem_inc(done, Steps.CREDIT)
            e.sem_inc(act_conv_done, Steps.CREDIT)
            e.wait_ge(inputs_in, 32)
            e.wait_ge(zero_set, 1)

            def spans(f):
                for h, (c0, c1) in enumerate(SPAN):
                    r = f(h, c0, c1)
                return r

            def evac(phase, step, src, dst):
                def f(k, i):
                    e.wait_ge(pe_done[k], pe.at(phase, src, k, i))
                    dst(lane(phase, k), i, k).then_inc(act_done[k], act.step(phase, step, k))
                return f

            def h1(v, i, k):
                A(v.h1[0:64, 1:T + 1].rearrange("p (h c) -> p h c", h=2), v.P[0:64, :, 0:HALF_T], ACT.Silu, bias=w("b_compress")[0:64])
                return A(v.h1[64:128, 0:T].rearrange("p (h c) -> p h c", h=2), v.P[64:128, :, 0:HALF_T], ACT.Silu, bias=w("b_compress")[64:128])

            def h2(v, i, k):
                return A(v.h2[0:64, :].rearrange("p (h c) -> p h c", h=2), v.P[0:64, :, 0:HALF_T], ACT.Silu, bias=w("b_main"))

            def y1T(v, i, k):
                return A(v.y1T.rearrange("p (h c) -> p h c", h=2), v.P[:, :, 0:HALF_T], ACT.Identity, bias=w("b_conv"), scale=w("g_conv"))

            def ff(v, i, k):
                return A(v.h2[0:64, :].rearrange("p (h c) -> p h c", h=2), v.P[0:64, :, 0:HALF_T], ACT.Gelu, bias=w("b_ff1"))

            def y2T(v, i, k):
                return A(v.y2T.rearrange("p (h c) -> p h c", h=2), v.P[:, :, 0:HALF_T], ACT.Identity, bias=w("b_ff"), scale=w("g_ff"))

            def h1tok(v, i, k):
                for a, b, n in HP:
                    r = nc.scalar.copy(v.h1tok[0:n, a:b, :], v.TK[0:n, a:b, :])
                return r

            def to_nT(v, i, k):
                return spans(lambda h, c0, c1: nc.scalar.copy(v.nT[:, c0:c1], v.P[:, h, 0:c1 - c0]))

            def g(v, i, k):
                return spans(lambda h, c0, c1: A(v.g[:, c0:c1], v.P[:, h, 0:c1 - c0], ACT.Sigmoid))

            def to_NT(v, i, k):
                nt = NT[:, bass.ds(i * LANES + k % LANES, 1), :]
                return spans(lambda h, c0, c1: nc.scalar.copy(nt[:, 0, PAD + c0:PAD + c1], v.P[:, h, 0:c1 - c0]))

            def n4T(v, i, k):
                nb = N[:, batch_tiles(i * LANES + k % LANES), :]
                for a, b, n in HP:
                    nc.scalar.copy(nb[0:n, a:b, :], v.norm[0:n, a:b, :])
                to_NT(v, i, k)
                return to_nT(v, i, k)

            def keep_h1(k, i):
                e.wait_ge(dve_done[k], dve.at("mix_a", "norm3", k, i))
                e.wait_ge(dve_done[LANES + k], dve.at("mix_b", "h2", LANES + k, i - 1))
                evac("mix_a", "h1tok", "h1tok", h1tok)(k, i)

            mixer(e, "act", {
                "h1": evac("mix_a", "h1", "compress", h1), "h2": evac("mix_a", "h2", "main", h2),
                "y1T": evac("mix_a", "y1T", "norm1T", y1T), "ff": evac("mix_a", "ff", "ff1", ff),
                "y2T": evac("mix_a", "y2T", "norm2T", y2T), "h1tok": keep_h1,
                "n1T": evac("mix_b", "n1T", "norm3T", to_nT), "g": evac("mix_b", "g", "Wg", g),
                "n4T": evac("mix_b", "n4T", "norm4T", n4T)})

            e.wait_ge(dve_done[0], dve.at("route0", "values", 0, 0))
            A(top_vals, top_vals, ACT.Sigmoid).then_inc(act_done[0], act.step("route0", "sigmoid", 0))

            with e.Fori(0, ITERS) as i:
                for m in range(2):
                    for h, (c0, c1) in enumerate(SPAN):
                        for k in range(LANES):
                            v = lanes[k]
                            e.wait_ge(pe_done[k], pe.at("shared0", f"up{m}_{h}", k, i))
                            A(v.y2T[:, 0:c1 - c0], v.P[:, 0, 0:c1 - c0], ACT.Silu).then_inc(act_done[k], act.step("shared0", f"s{m}_{h}", k))
            barrier(e, "shared0")

            def expert_tiles(m, phase):
                n = (HID0, HID1)[m]

                def silu(u, i, t):
                    v = slots[u]
                    e.wait_ge(pe_done[u], pe.at(phase, "up", u, i))
                    A(v.e[:, 0:HID0], v.ps1[:, 0:HID0], ACT.Silu).then_inc(act_done[u], act.step(phase, "silu", u))

                def exp(u, i, t):
                    v = slots[u]
                    e.wait_ge(pe_done[u], pe.at(phase, "up", u, i))
                    A(v.e, v.ps1, ACT.Exp, bias=minus_one[:]).then_inc(act_done[u], act.step(phase, "exp", u))

                def uT(u, i, t):
                    v = slots[u]
                    e.wait_ge(pe_done[u], pe.at(phase, "uT", u, i))
                    nc.scalar.copy(v.uT[:, 0:n], v.ps1[:, 0:n]).then_inc(act_done[u], act.step(phase, "uT", u))

                turns(e, [("silu", silu) if m == 0 else ("exp", exp), ("uT", uT)])

            expert_tiles(0, "experts0")
            barrier(e, "experts0")

            def attn(step, src, f):
                def g(k, i):
                    v = lanes[k]
                    if step in ("q0", "q1"):
                        e.wait_ge(dve_done[k], dve.at("attention", "h3", k, i))
                    if step == "rc1":
                        e.wait_ge(dve_done[k], dve.at("attention", "h4", k, i))
                    e.wait_ge(pe_done[k], pe.at("attention", src, k, i))
                    f(v, i, k).then_inc(act_done[k], act.step("attention", step, k))
                return g

            def from_AB(dst_of):
                return lambda v, i, k: spans(lambda h, c0, c1: nc.scalar.copy(dst_of(v, i, k)[:, c0:c1], v.AB[:, h, 0:c1 - c0]))

            def relu(n):
                return lambda v, i, k: spans(lambda h, c0, c1: A(v.QK[n][:, c0:c1], v.AB[:, h, 0:c1 - c0], ACT.Relu,
                                                                 bias=w("b_qk", (n, n + 1))))

            def v_rows(v, i, k):
                for a, b, n in HP:
                    for j in range(a, b):
                        r = nc.scalar.copy(v.V[0:n, j, :, 0:DH], v.ABt[0:n, j, :].rearrange("p (h e) -> p h e", e=DH))
                return r

            def keys(c):
                return lambda v, i, k: nc.scalar.copy(v.ktok[0:WIDTH[c], :], v.C[0:WIDTH[c], 0:256])

            def rc1(v, i, k):
                return spans(lambda h, c0, c1: A(v.rcT[:, 1 + c0:1 + c1], v.AB[:, h, 0:c1 - c0], ACT.Gelu, bias=w("b_rc1")))

            def norm_kept(v, i, k):
                nb = N[:, batch_tiles(i * LANES + k), :]
                for a, b, n in HP:
                    nc.scalar.copy(nb[0:n, a:b, :], v.norm[0:n, a:b, :])
                return from_AB(lambda v, i, k: NT[:, bass.ds(i * LANES + k, 1), PAD:PAD + L].rearrange("p a c -> p (a c)"))(v, i, k)

            att = {0: attn("n5T", "norm5T", from_AB(lambda v, i, k: v.nT)), 5: attn("v", "v", v_rows)}
            for n, x in enumerate(("q0", "q1", "k0", "k1")):
                att[1 + n] = attn(x, x, relu(n))
            for c in range(TILES):
                att[6 + 2 * c] = attn(f"kt{c}", f"sc{c}", keys(c))
            after = 6 + 2 * TILES
            att[after] = attn("oT", "oT", from_AB(lambda v, i, k: v.oT))
            att[after + 2] = attn("n6T", "norm6T", norm_kept)
            att[after + 3] = attn("rc1", "rc1", rc1)

            def conv_part(n, i):
                what, q, m, t3 = PARTS[n]
                if what == "taps":
                    if t3 == 2:
                        c0, c1 = SPAN[q % 2]
                        e.wait_ge(pe_conv_done, pe_conv.at("conv", f"c{m}_{q}", 0, i))
                        A(conv_h[:, m, 0:c1 - c0], conv_bank[m % 2][:, 0:c1 - c0], ACT.Silu, bias=w("b_sh1", (m, m + 1))
                          ).then_inc(act_conv_done, act_conv.step("conv", f"s{m}_{q}", 0))
                else:
                    e.wait_ge(pe_conv_done, pe_conv.at("conv", f"rows{q}", 0, i))
                    e.wait_ge(conv_stored[q % 2], i * (16 * UNITS // 2) + 16 * (q // 2))
                    n_ = WIDTH[3 * (q % 2) + 2]
                    nc.scalar.copy(conv_rows[q % 2][:, 0:2 * P], conv_bank[1][:, 0:2 * P])
                    nc.scalar.copy(conv_rows[q % 2][0:n_, 2 * P:3 * P], conv_bank[1][0:n_, 2 * P:3 * P]
                                   ).then_inc(act_conv_done, act_conv.step("conv", f"rows{q}", 0))

            def attention(i, conv):
                for what, n, k in interleaved(conv):
                    if what == "conv":
                        conv_part(n, i - 1)
                    elif n in att:
                        att[n](k, i)

            attention(0, False)
            with e.Fori(1, ITERS) as i:
                attention(i, True)
            for n in range(len(PARTS)):
                conv_part(n, ITERS - 1)

            e.wait_ge(dve_done[0], dve.at("route1", "values", 0, 0))
            A(top_vals[:, 0:NTILE], top_vals[:, 0:NTILE], ACT.Exp).then_inc(act_done[0], act.step("route1", "exp", 0))
            barrier(e, "route1")
            barrier(e, "colsum")
            expert_tiles(1, "experts1")
            barrier(e, "experts1")

            with e.Fori(0, OUT_ITERS) as i:
                for k in range(OUT_LANES):
                    v = outs[k]
                    e.wait_ge(dve_done[k], dve.at("output", "gates", k, i))
                    e.wait_ge(gathered["output"][k], 16 * GATHERS * i + 16 * GATHERS)
                    for j in range(TILES):
                        n = WIDTH[j]
                        r = A(v.Y[0][0:n, j, :], v.Y[0][0:n, j, :], ACT.Identity, bias=w("nought")[0:n], scale=v.gk[0:n, 0, j:j + 1])
                    r.then_inc(act_done[k], act.step("output", "weighed", k))

        @block.vector
        def _(e):
            V = nc.vector
            for done in dve_done:
                e.sem_inc(done, Steps.CREDIT)
            for t in (zeros, NT, S):
                V.memset(t[:], 0.0)
            for v in lanes:
                V.memset(v.mv[:], 1.0)
            for v in outs:
                V.memset(v.mv[:], 1.0)
            for v in mix[0:LANES]:
                V.memset(v.h1, 0.0)
                V.memset(v.h2[64:65, :], 1.0)
            for t in conv_rows:
                V.memset(t[:], 0.0)
            V.memset(minus_one[:], -1.0)
            e.drain().then_inc(zero_set, 1)
            e.wait_ge(inputs_in, 32)
            V.tensor_scalar(a_minus_1[:], w("A"), -1.0, None, ALU.add)
            V.tensor_scalar(eb1_f[:, 0:EB1], eb1_f[:, 0:EB1], 1.0, None, ALU.add)
            V.memset(ones3[:], 1.0)
            for q in range(3):
                e.drain()
                V.tensor_copy(eb1_part[:, q, :], eb1_f[:])
                if q < 2:
                    e.drain()
                    V.tensor_tensor(eb1_f[:], eb1_f[:], eb1_part[:, q, :], ALU.subtract)
            e.drain().then_inc(eb1_split, 1)

            def var(n, phase, src, widths, after=None):
                def f(k, i):
                    v = lane(phase, k)
                    if after:
                        e.wait_ge(pe_done[k], pe.at(phase, after, k, i))
                    s = src(v, i, k)
                    for j in range(TILES):
                        V.bn_stats(v.st[0:widths[j], j, :], s[0:widths[j], j, :])
                    e.drain()
                    for j in range(TILES):
                        V.bn_aggr(v.mv[0:widths[j], j, :], v.st[0:widths[j], j, :])
                    e.drain()
                    V.tensor_scalar(v.ve[:], v.mv[:, :, 1], EPS, None, ALU.add).then_inc(dve_done[k], dve.step(phase, f"var{n}", k))
                return f

            def norm(n, phase, src, widths):
                def f(k, i):
                    v = lane(phase, k)
                    e.wait_ge(pool_done[k], pool.at(phase, f"rstd{n}", k, i))
                    s = src(v, i, k)
                    for j in range(TILES):
                        m = widths[j]
                        r = V.tensor_scalar(v.norm[0:m, j, :], s[0:m, j, :], v.mv[0:m, j, 0:1], v.rstd[0:m, j:j + 1],
                                            ALU.subtract, ALU.mult)
                    r.then_inc(dve_done[k], dve.step(phase, f"norm{n}", k))
                return f

            TOKW = [TOK_ROWS] * TILES

            def TK(v, i, k):
                return v.TK

            def Hb(v, i, k):
                return H[:, batch_tiles(i * LANES + k % LANES), :]

            def pooled(k, i):
                v = mix[k]
                e.wait_ge(act_done[k], act.at("mix_a", "y2T", k, i))
                V.tensor_tensor(v.tmp[:, 0:T - 1], v.y2T[:, 0:T - 1], v.y2T[:, 1:T], ALU.max)
                e.drain()
                V.tensor_tensor(v.y2T[:, 0:L], v.tmp[:, 0:L], v.y2T[:, 2:T], ALU.max).then_inc(dve_done[k], dve.step("mix_a", "pool", k))

            def decay(k, i):
                v = mix[k]
                e.wait_ge(act_done[k], act.at("mix_b", "g", k, i))
                V.tensor_scalar(v.g, v.g, 0.05, 0.95, ALU.max, ALU.min)
                e.drain()
                V.tensor_scalar(v.a, v.g, a_minus_1[:], 1.0, ALU.mult, ALU.add).then_inc(dve_done[k], dve.step("mix_b", "gates", k))

            def drive(k, i):
                v = mix[k]
                e.wait_ge(pe_done[k], pe.at("mix_b", "xB", k, i))
                for h, (c0, c1) in enumerate(SPAN):
                    r = V.scalar_tensor_tensor(v.bc[:, c0:c1], v.TKf[:, h, 0:c1 - c0], w("bias_h"), v.g[:, c0:c1], ALU.add, ALU.mult)
                r.then_inc(dve_done[k], dve.step("mix_b", "b", k))

            def scan(k, i):
                v = mix[k]
                e.drain()
                V.tensor_tensor_scan(v.hs, v.a, v.bc, 0.0, ALU.mult, ALU.add).then_inc(dve_done[k], dve.step("mix_b", "scan", k))

            def add_recurrence(k, i):
                v = mix[k]
                e.wait_ge(pe_done[k], pe.at("mix_b", "y", k, i))
                e.wait_ge(act_done[k - LANES], act.at("mix_a", "h1tok", k - LANES, i))
                hb = Hb(v, i, k)
                for a, b, n in HP:
                    V.scalar_tensor_tensor(hb[0:n, a:b, :], v.TK[0:n, a:b, :], P ** -0.5, v.h1tok[0:n, a:b, :], ALU.mult, ALU.add)
                e.drain().then_inc(dve_done[k], dve.step("mix_b", "h2", k))

            def keep_scores(phase, ne):
                def f(k, i):
                    v = lane(phase, k)
                    e.wait_ge(pe_done[k], pe.at(phase, "scores", k, i))
                    sb_ = S[:, batch_tiles(batch(phase, k, i)), :]
                    for a, b, n in HP:
                        src = v.TK if phase == "mix_b" else v.C[:, 0:16 * TILES].rearrange("p (j x) -> p j x", x=16)
                        r = V.tensor_copy(sb_[0:n, a:b, 0:ne], src[0:n, a:b, 0:ne])
                    r.then_inc(dve_done[k], dve.step(phase, "scores", k))
                return f

            def norm3(k, i):
                v = mix[k]
                e.wait_ge(act_done[LANES + k], act.at("mix_b", "n4T", LANES + k, i - 1))
                e.wait_ge(pool_done[k], pool.at("mix_a", "rstd3", k, i))
                for j in range(TILES):
                    m = WIDTH[j]
                    r = V.tensor_scalar(v.norm3[0:m, j, :], v.TK[0:m, j, :], v.mv[0:m, j, 0:1], v.rstd[0:m, j:j + 1],
                                        ALU.subtract, ALU.mult)
                r.then_inc(dve_done[k], dve.step("mix_a", "norm3", k))

            mixer(e, "dve", {
                "var1": var(1, "mix_a", TK, TOKW, "r1"), "norm1": norm(1, "mix_a", TK, TOKW),
                "var2": var(2, "mix_a", TK, TOKW, "r2"), "norm2": norm(2, "mix_a", TK, TOKW), "pool": pooled,
                "var3": var(3, "mix_a", TK, WIDTH, "h1tok"), "norm3": norm3, "gates": decay, "b": drive, "scan": scan,
                "h2": add_recurrence, "var4": var(4, "mix_b", Hb, WIDTH), "norm4": norm(4, "mix_b", Hb, WIDTH),
                "scores": keep_scores("mix_b", E0)})

            def over_experts(x, ne):
                return x.unsqueeze(2).broadcast_to([P, NTILE, ne])

            def over_tiles(x, ne):
                return x.unsqueeze(1).broadcast_to([P, NTILE, ne])

            def top2(x, ne, first, second, vals, tag):
                best = route_small(0, NTILE)
                for n, hot in enumerate((first, second)):
                    V.tensor_reduce(vals[n], x, AX.X, ALU.max)
                    e.drain()
                    V.tensor_tensor(tag, x, over_experts(vals[n], ne), ALU.is_equal)
                    e.drain()
                    V.tensor_tensor(tag, tag, over_tiles(w("descend", (E1 - ne, E1)), ne), ALU.mult)
                    e.drain()
                    V.tensor_reduce(best, tag, AX.X, ALU.max)
                    e.drain()
                    V.tensor_tensor(hot, tag, over_experts(best, ne), ALU.is_equal)
                    e.drain()
                    if n == 0:
                        V.scalar_tensor_tensor(x, hot, -3e38, x, ALU.mult, ALU.add)
                        e.drain()

            def route(m, phase):
                ne = (E0, E1)[m]
                x, tag, first, second, both, total, upto, pos, spare = (route_buf(n, ne) for n in range(9))
                vals = [top_vals[:, 0:NTILE], top_vals[:, NTILE:2 * NTILE]]
                barrier(e, ("mix_a", "attention")[m])
                if m == 0:
                    barrier(e, "mix_b")
                scores = S[:, :, 0:ne]
                if m == 0:
                    V.tensor_tensor(x, scores, over_tiles(w("gate_bias"), ne), ALU.add)
                else:
                    V.tensor_copy(x, scores)
                e.drain()
                top2(x, ne, first, second, vals, tag)
                if m == 0:
                    V.tensor_copy(x, scores)
                    e.drain()
                    top2(x, ne, pos, spare, vals, tag)
                for hot in (first, second):
                    V.tensor_tensor(hot, hot, over_experts(w("valid"), ne), ALU.mult)
                e.drain()
                V.tensor_tensor(both, first, second, ALU.add).then_inc(dve_done[0], dve.step(phase, "onehot", 0))
                if m == 1:
                    V.tensor_tensor(vals[0], vals[1], vals[0], ALU.subtract)
                e.drain().then_inc(dve_done[0], dve.step(phase, "values", 0))

                e.wait_ge(pe_done[0], pe.at(phase, "counts", 0, 0))
                V.tensor_copy(total.rearrange("p t e -> p (t e)"), psum[:, 1, 0:NTILE * ne])
                e.drain()
                for x_ in range(ne):
                    V.tensor_tensor_scan(upto[:, :, x_], w("ones")[:, 0:NTILE], total[:, :, x_], 0.0, ALU.mult, ALU.add)
                e.drain()
                V.tensor_tensor(pos, upto, total, ALU.subtract)
                e.drain()
                V.tensor_tensor(pos.rearrange("p t e -> p (t e)"), psum[:, 0, 0:NTILE * ne],
                                pos.rearrange("p t e -> p (t e)"), ALU.add)
                n_rows = w("tile_rows")
                cmp = work[:, 10240:10240 + ne * 47].rearrange("p (e j) -> p e j", j=47)
                tiles_of, tiles_upto, first_slot = (route_small(144 + 16 * q, ne) for q in range(3))
                V.tensor_tensor(cmp, upto[:, NTILE - 1, :].unsqueeze(2).broadcast_to([P, ne, 47]),
                                n_rows.unsqueeze(1).broadcast_to([P, ne, 47]), ALU.is_gt)
                e.drain()
                V.tensor_reduce(tiles_of, cmp, AX.X, ALU.add)
                e.drain()
                V.tensor_tensor_scan(tiles_upto, w("ones")[:, 0:ne], tiles_of, 0.0, ALU.mult, ALU.add)
                e.drain()
                V.tensor_tensor(first_slot, tiles_upto, tiles_of, ALU.subtract)
                e.drain()
                V.scalar_tensor_tensor(pos, over_tiles(first_slot, ne), float(P), pos, ALU.mult, ALU.add)
                e.drain()
                slot_f = route_small(200, NTILE)
                for n, hot in enumerate((first, second)):
                    V.tensor_tensor(tag, hot, pos, ALU.mult)
                    e.drain()
                    V.tensor_reduce(slot_f, tag, AX.X, ALU.add)
                    e.drain()
                    V.tensor_copy(slot_u[:, n, :], slot_f)
                    e.drain()
                e.drain().then_inc(dve_done[0], dve.step(phase, "slots", 0))
                cmp = work[:, 10240:10240 + EXPERT_TILES * ne].rearrange("p (t e) -> p t e", e=ne)
                V.tensor_tensor(cmp, tiles_upto.unsqueeze(1).broadcast_to([P, EXPERT_TILES, ne]),
                                w("tile_id").unsqueeze(2).broadcast_to([P, EXPERT_TILES, ne]), ALU.is_le)
                e.drain()
                which = route_small(256, EXPERT_TILES)
                V.tensor_reduce(which, cmp, AX.X, ALU.add)
                e.drain()
                V.tensor_scalar(tile_expert[:], which, float(ne - 1), float((STRIDE0, STRIDE1)[m]), ALU.min, ALU.mult)
                e.wait_ge(act_done[0], act.at(phase, ("sigmoid", "exp")[m], 0, 0))
                rs = route_small(0, NTILE)
                if m == 0:
                    V.tensor_tensor(rs, vals[0], vals[1], ALU.add)
                    e.drain()
                    V.reciprocal(rs, rs)
                    e.drain()
                    for n in range(2):
                        V.tensor_tensor(gates[:, n, :], vals[n], rs, ALU.mult)
                else:
                    V.tensor_scalar(rs, vals[0], 1.0, None, ALU.add)
                    e.drain()
                    V.reciprocal(gates[:, 0, :], rs)
                    e.drain()
                    V.tensor_tensor(gates[:, 1, :], gates[:, 0, :], vals[0], ALU.mult)
                e.drain().then_inc(dve_done[0], dve.step(phase, "done", 0))

            route(0, "route0")

            with e.Fori(0, ITERS) as i:
                for m in range(2):
                    for h, (c0, c1) in enumerate(SPAN):
                        for k in range(LANES):
                            v = lanes[k]
                            e.wait_ge(act_done[k], act.at("shared0", f"s{m}_{h}", k, i))
                            V.tensor_tensor(v.QK[m][:, c0:c1], v.y2T[:, 0:c1 - c0], v.P[:, 1, 0:c1 - c0], ALU.mult
                            ).then_inc(dve_done[k], dve.step("shared0", f"u{m}_{h}", k))
                for k in range(LANES):
                    v = lanes[k]
                    e.wait_ge(pe_done[k], pe.at("shared0", "down", k, i))
                    hb = Hb(v, i, k)
                    for a, b, n in HP:
                        r = V.tensor_tensor(hb[0:n, a:b, :], v.TK[0:n, a:b, :], hb[0:n, a:b, :], ALU.add)
                    r.then_inc(dve_done[k], dve.step("shared0", "h", k))
            barrier(e, "shared0")

            def expert_tiles(m, phase):
                def xT(u, i, t):
                    v = slots[u]
                    e.wait_ge(pe_done[u], pe.at(phase, "xT", u, i))
                    V.tensor_copy(v.xT, v.psx).then_inc(dve_done[u], dve.step(phase, "xT", u))

                def gated(u, i, t):
                    v = slots[u]
                    e.wait_ge(act_done[u], act.at(phase, "silu", u, i))
                    V.tensor_tensor(v.e[:, 0:HID0], v.e[:, 0:HID0], v.ps1[:, HID0:2 * HID0], ALU.mult
                                    ).then_inc(dve_done[u], dve.step(phase, "u", u))

                def elu(u, i, t):
                    v = slots[u]
                    e.wait_ge(act_done[u], act.at(phase, "exp", u, i))
                    V.scalar_tensor_tensor(v.e, v.e, 1.0, v.ps1, ALU.min, ALU.max
                                           ).then_inc(dve_done[u], dve.step(phase, "u", u))

                def y(u, i, t):
                    v = slots[u]
                    e.wait_ge(pe_done[u], pe.at(phase, "down", u, i))
                    e.wait_ge(row_stored[u], 16 * i + 16 * EITERS * m)
                    V.tensor_copy(v.y, v.psy).then_inc(dve_done[u], dve.step(phase, "y", u))

                turns(e, [("xT", xT), ("u", gated if m == 0 else elu), ("y", y)])

            expert_tiles(0, "experts0")
            barrier(e, "experts0")

            for v in lanes:
                V.memset(v.V, 1.0)
            e.drain()

            def weigh_rows(v, i, k, phase):
                if phase == "attention":
                    e.wait_ge(gathered[phase][k], 16 * GATHERS * i + 16 * GATHERS)
                    V.tensor_copy(v.gk[:], gates[:, :, batch_tiles(batch(phase, k, i))])
                    e.drain()
                    for j in range(TILES):
                        n = WIDTH[j]
                        V.tensor_scalar(v.Y[0][0:n, j, :], v.Y[0][0:n, j, :], v.gk[0:n, 0, j:j + 1], None, ALU.mult)
                    e.drain()
                else:
                    e.wait_ge(act_done[k], act.at(phase, "weighed", k, i))
                for j in range(TILES):
                    n = WIDTH[j]
                    V.scalar_tensor_tensor(v.Y[0][0:n, j, :], v.Y[1][0:n, j, :], v.gk[0:n, 1, j:j + 1], v.Y[0][0:n, j, :],
                                           ALU.mult, ALU.add)
                e.drain()

            def add_experts(k, i):
                v = lanes[k]
                weigh_rows(v, i, k, "attention")
                hb = Hb(v, i, k)
                for a, b, n in HP:
                    V.tensor_tensor(hb[0:n, a:b, :], v.Y[0][0:n, a:b, :], hb[0:n, a:b, :], ALU.add)
                V.memset(v.state, 0.0)
                e.drain().then_inc(dve_done[k], dve.step("attention", "h3", k))

            def cos_sin(n):
                def f(k, i):
                    v = lanes[k]
                    name = ("q0", "q1", "k0", "k1")[n]
                    e.wait_ge(act_done[k], act.at("attention", name, k, i))
                    V.tensor_tensor(v.QK[n], v.QK[n], w("cos_sin"), ALU.mult).then_inc(dve_done[k], dve.step("attention", name, k))
                return f

            def spread_queries(v, c):
                n = WIDTH[c]
                return V.tensor_tensor(v.QB[:, :, :, 0:n], v.Q2[:, :, c * P:c * P + n].unsqueeze(2).broadcast_to([P, 2, 2, n]),
                                       w("head_of").unsqueeze(1).unsqueeze(3).broadcast_to([P, 2, 2, n]), ALU.mult)

            def first_queries(k, i):
                v = lanes[k]
                e.drain()
                e.wait_ge(pe_done[k], pe.at("attention", "v", k, i))
                spread_queries(v, 0).then_inc(dve_done[k], dve.step("attention", "qb", k))

            def mask(c):
                def f(k, i):
                    v = lanes[k]
                    n = WIDTH[c]
                    e.wait_ge(pe_done[k], pe.at("attention", f"sc{c}", k, i))
                    r = V.tensor_tensor(v.AT2[0:n, :, 0:n], v.AB.rearrange("p b (x i) -> p (b x) i", i=P)[0:n, :, 0:n],
                                        w("causal")[0:n, 0:n].unsqueeze(1).broadcast_to([n, 8, n]), ALU.mult)
                    r.then_inc(dve_done[k], dve.step("attention", f"at{c}", k))
                    if c < TILES - 1:
                        spread_queries(v, c + 1)
                return f

            def context(c):
                def f(k, i):
                    v = lanes[k]
                    n = WIDTH[c]
                    e.wait_ge(pe_done[k], pe.at("attention", f"cx{c}", k, i))
                    cx = v.C[:, 256:256 + 136].rearrange("p (h e) -> p h e", e=DH + 1)
                    V.tensor_scalar(v.rden[0:n], cx[0:n, :, DH], 1e-6, None, ALU.add)
                    if c < TILES - 1:
                        V.tensor_tensor(v.upd[:], v.AB[:, 0, 0:136], w("block"), ALU.mult)
                    e.drain()
                    V.reciprocal(v.rden[0:n], v.rden[0:n])
                    if c < TILES - 1:
                        V.tensor_tensor(v.state, v.state, v.upd[:], ALU.add)
                    e.drain()
                    V.tensor_tensor(v.norm[0:n, c, :].rearrange("p (h e) -> p h e", e=DH), cx[0:n, :, 0:DH], 
                                    v.rden[0:n].unsqueeze(2).broadcast_to([n, HEADS, DH]), ALU.mult).then_inc(dve_done[k], dve.step("attention", f"st{c}", k))
                return f

            def otok(k, i):
                e.drain().then_inc(dve_done[k], dve.step("attention", "otok", k))

            def add_attention(k, i):
                v = lanes[k]
                e.wait_ge(pe_done[k], pe.at("attention", "out", k, i))
                hb = Hb(v, i, k)
                for a, b, n in HP:
                    V.tensor_tensor(hb[0:n, a:b, :], v.ABt[0:n, a:b, :], hb[0:n, a:b, :], ALU.add)
                V.memset(v.rcT[:, 0:1], 0.0)
                V.memset(v.rcT[:, L + 1:L + 2], 0.0)
                e.drain().then_inc(dve_done[k], dve.step("attention", "h4", k))

            with e.Fori(0, ITERS) as i:
                steps = [add_experts, var(5, "attention", Hb, WIDTH), norm(5, "attention", Hb, WIDTH)]
                steps += [cos_sin(n) for n in range(4)] + [first_queries]
                for c in range(TILES):
                    steps += [mask(c), context(c)]
                steps += [otok, add_attention, var(6, "attention", Hb, WIDTH), norm(6, "attention", Hb, WIDTH),
                          keep_scores("attention", E1)]
                for f in steps:
                    for k in range(LANES):
                        f(k, i)

            route(1, "route1")
            barrier(e, "route1")
            e.wait_ge(pe_done[0], pe.at("colsum", "colsum", 0, 0))
            e.wait_ge(experts1_in, 32)
            for q, (x0, x1) in enumerate(((0, 4), (4, 8), (8, E1))):
                r = V.tensor_tensor(eb2[0:1, x0 * P:x1 * P], eb2[0:1, x0 * P:x1 * P], psum[0:1, 2 + q, 0:(x1 - x0) * P], ALU.subtract)
            r.then_inc(dve_done[0], dve.step("colsum", "bias", 0))
            for q in range(3):
                e.drain()
                if q:
                    e.wait_ge(eb2_stored, 16 * q)
                V.tensor_copy(eb2_part, eb2)
                e.drain().then_inc(eb2_split, 1)
                if q < 2:
                    V.tensor_tensor(eb2, eb2, eb2_part, ALU.subtract)
            expert_tiles(1, "experts1")
            barrier(e, "experts1")

            def z(k, i):
                v = outs[k]
                weigh_rows(v, i, k, "output")
                e.wait_ge(shared_rows_in[k], i * 16 + 16)
                nb = N[:, batch_tiles(batch("output", k, i)), :]
                sh = v.sh.rearrange("p h (j d) -> p (h j) d", d=P)
                for a, b, n in HP:
                    V.tensor_tensor(v.Y[0][0:n, a:b, :], v.Y[0][0:n, a:b, :], sh[0:n, a:b, :], ALU.add)
                e.drain()
                for a, b, n in HP:
                    V.tensor_tensor(v.Y[0][0:n, a:b, :], v.Y[0][0:n, a:b, :], nb[0:n, a:b, :], ALU.add)
                e.drain().then_inc(dve_done[k], dve.step("output", "z", k))

            def batch_gates(k, i):
                V.tensor_copy(outs[k].gk[:], gates[:, :, batch_tiles(batch("output", k, i))]
                              ).then_inc(dve_done[k], dve.step("output", "gates", k))

            def Yb(v, i, k):
                return v.Y[0]

            def final(k, i):
                v = outs[k]
                hb = H[:, batch_tiles(batch("output", k, i)), :]
                e.drain()
                for a, b, n in HP:
                    V.tensor_tensor(v.norm[0:n, a:b, :], v.norm[0:n, a:b, :],
                                    w("ln_g")[0:n].unsqueeze(1).broadcast_to([n, b - a, P]), ALU.mult)
                    V.tensor_tensor(hb[0:n, a:b, :], hb[0:n, a:b, :],
                                    w("ln_b")[0:n].unsqueeze(1).broadcast_to([n, b - a, P]), ALU.add)
                e.drain()
                for a, b, n in HP:
                    r = V.tensor_tensor(hb[0:n, a:b, :], hb[0:n, a:b, :], v.norm[0:n, a:b, :], ALU.add)
                r.then_inc(dve_done[k], dve.step("output", "h5", k))

            var7, norm7 = var(7, "output", Yb, WIDTH), norm(7, "output", Yb, WIDTH)
            with e.Fori(0, OUT_ITERS) as i:
                for k in range(OUT_LANES):
                    batch_gates(k, i)
                for k in range(OUT_LANES + 1):
                    if k < OUT_LANES:
                        z(k, i)
                        var7(k, i)
                    if k > 0:
                        norm7(k - 1, i)
                        final(k - 1, i)

        @block.gpsimd
        def _(e):
            G = nc.gpsimd
            for done in pool_done:
                e.sem_inc(done, Steps.CREDIT)
            e.wait_ge(inputs_in, 32)

            def rstd(phase, n, k, i):
                e.wait_ge(dve_done[k], dve.at(phase, f"var{n}", k, i))
                v = lane(phase, k)
                G.tensor_tensor(v.rstd[:], v.ve[:], w("minus_half"), ALU.pow).then_inc(pool_done[k], pool.step(phase, f"rstd{n}", k))

            def scatter(m):
                e.wait_ge(rows_zeroed, 32)
                e.wait_ge(dve_done[0], dve.at(("route0", "route1")[m], "slots", 0, 0))
                for t in range(NTILE):
                    n = WIDTH[t % TILES]
                    for q in range(2):
                        G.indirect_dma_start(rows_in[m], bass.IndirectOffsetOnAxis(ap=slot_u[0:n, q, t:t + 1], axis=0),
                                             N[0:n, t, :], None).then_inc(scattered[m], 16)

            def gather(m, phase, k, i):
                v = lane(phase, k)
                G.tensor_copy(v.ix[:], slot_u[:, :, batch_tiles(batch(phase, k, i))])
                e.drain()
                for j in range(TILES):
                    n = WIDTH[j]
                    for q in range(2):
                        G.indirect_dma_start(v.Y[q][0:n, j, :], None, rows_out[m],
                                             bass.IndirectOffsetOnAxis(ap=v.ix[0:n, q, j:j + 1], axis=0)).then_inc(gathered[phase][k], 16)

            def rstd_step(phase, n):
                return lambda k, i: rstd(phase, n, k, i)

            mixer(e, "pool", {"rstd1": rstd_step("mix_a", 1), "rstd2": rstd_step("mix_a", 2), "rstd3": rstd_step("mix_a", 3),
                              "rstd4": rstd_step("mix_b", 4)})

            def store_rows(m, phase):
                with e.Fori(0, EITERS) as i:
                    for u in range(SLOTS):
                        e.wait_ge(dve_done[u], dve.at(phase, "y", u, i))
                        e.dma_start(rows_out[m].rearrange("(t p) d -> t p d", p=P)[
                            bass.ds(i * SLOTS + u, 1)].rearrange("a p d -> p (a d)"), slots[u].y).then_inc(row_stored[u], 16)

            scatter(0)
            store_rows(0, "experts0")
            for s in row_stored:
                e.wait_ge(s, 16 * EITERS)
            barrier(e, "experts0")
            with e.Fori(0, ITERS) as i:
                for k in range(LANES):
                    e.wait_ge(pe_done[k], pe.at("attention", "cx5", k, i - 1))
                    gather(0, "attention", k, i)
                for n in (5, 6):
                    for k in range(LANES):
                        rstd("attention", n, k, i)
            scatter(1)
            store_rows(1, "experts1")
            for s in row_stored:
                e.wait_ge(s, 32 * EITERS)
            barrier(e, "experts1")
            for k in range(OUT_LANES - 1):
                gather(1, "output", k, 0)

            def norm_and_fetch(i, last):
                for k in range(OUT_LANES):
                    rstd("output", 7, k, i)
                    ahead = k + OUT_LANES - 1
                    if ahead < OUT_LANES or not last:
                        lane_, i_ = ahead % OUT_LANES, i + ahead // OUT_LANES
                        e.wait_ge(dve_done[lane_], dve.at("output", "norm7", lane_, i_ - 1))
                        gather(1, "output", lane_, i_)

            with e.Fori(0, OUT_ITERS - 1) as i:
                norm_and_fetch(i, False)
            norm_and_fetch(OUT_ITERS - 1, True)


def _layout(x):
    f = {k: np.asarray(v) for k, v in x.items()}
    pack = np.zeros((P, PACK_COLS), np.float32)

    def put(name, a, col=0):
        at, rows, n = PACK[name]
        a = np.asarray(a)
        pack[0:a.shape[0], at + col:at + col + a.shape[1]] = a

    wc = f["L0_tok_w_compress"][:, :, 0].T
    put("compress", wc)
    put("compress", wc, 64)
    wm = f["L0_tok_w_main"]
    put("main01", np.concatenate([wm[:, :, 0].T, wm[:, :, 1].T]))
    put("main2", wm[:, :, 2].T)
    put("expand", np.concatenate([f["L0_tok_w_expand"][:, :, 0].T, f["L0_tok_b_expand"][None]]))
    put("ff1", f["L0_tok_w_ff1"].T)
    put("ff2", np.concatenate([f["L0_tok_w_ff2"].T, f["L0_tok_b_ff2"][None]]))
    put("b_compress", np.concatenate([f["L0_tok_b_compress"]] * 2)[:, None])
    for name, src in (("b_main", "L0_tok_b_main"), ("b_ff1", "L0_tok_b_ff1"), ("g_conv", "L0_tok_g_conv_norm"),
                      ("b_conv", "L0_tok_b_conv_norm"), ("g_ff", "L0_tok_g_ff_norm"), ("b_ff", "L0_tok_b_ff_norm"),
                      ("A", "L0_attn_A"), ("bias_h", "L0_attn_bias_h"), ("b_rc1", "L1_ffn_rc_b1")):
        put(name, f[src][:, None])
    for name, src in (("Wg", "L0_attn_Wg"), ("Bm", "L0_attn_B"), ("C", "L0_attn_C"), ("D", "L0_attn_D"), ("gate", "L0_ffn_gate_w")):
        put(name, f[src].T)
    put("gate_bias", np.broadcast_to(f["L0_ffn_biases"], (P, E0)))
    wqkv, bqkv = f["L1_attn_W_qkv"], f["L1_attn_b_qkv"]
    twice = np.concatenate([np.concatenate([np.arange(DH * h, DH * h + DH)] * 2) for h in range(HEADS)])
    for s in range(2):
        for g in range(2):
            cols = s * P + twice[g * P:(g + 1) * P]
            put("qk"[s] + str(g), wqkv[:, cols])
            put("b_qk", bqkv[cols][:, None], 2 * s + g)
    put("v", wqkv[:, 2 * P:])
    put("out", f["L1_attn_W_out"])
    put("rc1", f["L1_ffn_rc_w1"].transpose(1, 2, 0).reshape(P, 3 * P))
    put("rc2", f["L1_ffn_rc_w2"].transpose(1, 2, 0).reshape(P, 3 * E1))
    put("b_sh1", f["L1_ffn_sh_b1"].reshape(4, P).T)
    put("ln_g", np.broadcast_to(f["L1_ffn_ln_g"], (P, P)))
    put("ln_b", np.broadcast_to(f["L1_ffn_ln_b"], (P, P)))
    r = np.arange(P)
    put("ident", np.eye(P, dtype=np.float32))
    put("ones", np.ones((P, P), np.float32))
    put("earlier", (r[:, None] < r[None]).astype(np.float32))
    put("causal", np.tile((r[:, None] <= r[None]).astype(np.float32), (1, 2)))
    angle = (np.float32(np.pi / 2) * np.arange(L, dtype=np.float32) / np.float32(L))[None]
    put("cos_sin", np.where((r // DH % 2 == 0)[:, None], np.cos(angle), np.sin(angle)).astype(np.float32))
    put("head_of", (r[:, None] // 32 % 2 == np.arange(2)[None]).astype(np.float32))
    put("block", np.tile((r[:, None] // 32 == np.arange(68)[None] // 17), (1, 2)).astype(np.float32))
    put("valid", (r[:, None] < np.array(WIDTH * B)[None]).astype(np.float32))
    put("descend", np.broadcast_to(np.arange(E1, 0, -1, dtype=np.float32), (P, E1)))
    put("tile_rows", np.broadcast_to(P * np.arange(47, dtype=np.float32), (P, 47)))
    put("tile_id", np.broadcast_to(np.arange(EXPERT_TILES, dtype=np.float32), (P, EXPERT_TILES)))
    put("minus_half", np.full((P, TILES), -0.5, np.float32))

    def rows(a, hid):
        return a.reshape(-1, hid // P, P, P).transpose(2, 0, 1, 3).reshape(P, -1)

    big = {
        "xT": f["x"].transpose(0, 2, 1),
        "pack": pack,
        "ew_0": np.concatenate([f["L0_ffn_w1"].transpose(1, 0, 2), f["L0_ffn_w3"].transpose(1, 0, 2),
                                rows(f["L0_ffn_w2"], HID0).reshape(P, E0, -1)], 2).reshape(P, -1),
        "sw13": np.concatenate([f["L0_ffn_sw1"], f["L0_ffn_sw3"]], 1),
        "sw2": rows(f["L0_ffn_sw2"][None], HID0),
        "ew_1": np.concatenate([f["L1_ffn_e_w1"].transpose(1, 0, 2), rows(f["L1_ffn_e_w2"], HID1).reshape(P, E1, -1)],
                               2).reshape(P, -1),
        "bias": np.concatenate([f["L1_ffn_e_b1"].reshape(P, -1), np.concatenate([
            f["L0_attn_bias_y"], bqkv[2 * P:], f["L1_attn_b_out"], np.pad(f["L1_ffn_rc_b2"], (0, P - E1)),
            f["L1_ffn_sh_b2"]]).reshape(P, -1)], 1),
        "eb2": f["L1_ffn_e_b2"].reshape(1, -1),
        "conv1": f["L1_ffn_sh_w1"].transpose(1, 2, 0).reshape(P, -1),
        "conv2": rows(f["L1_ffn_sh_w2"][:, :, 0].T[None], HID1),
    }
    return {k: np.ascontiguousarray(v) for k, v in big.items()}


def build(nc, arrays):
    d = {k: nc.dram_tensor(f"in_{k}", a.shape, mybir.dt.from_np(a.dtype), kind="ExternalInput").ap() for k, a in arrays.items()}
    out = nc.dram_tensor("out_0", (B, L, P), F32, kind="ExternalOutput").ap()
    audio_tower(nc, d, out)


def kernel(**inputs):
    import concourse.bacc as bacc
    from concourse.bass_utils import run_bass_kernel_spmd

    arrays = _layout(inputs)
    nc = bacc.Bacc("TRN2", target_bir_lowering=False, num_devices=1)
    build(nc, arrays)
    r = run_bass_kernel_spmd(nc, [{f"in_{k}": a for k, a in arrays.items()}], core_ids=[0])
    return r.results[0]["out_0"]
```
